# Optimizing a Trainium2 kernel written in Bass

```python
import numpy as np
import jax
import jax.numpy as jnp

def _softmax(x, axis=-1):
    return jax.nn.softmax(x, axis=axis)

def _gelu(x):
    return jax.nn.gelu(x, approximate=True)

def _silu(x):
    return jax.nn.silu(x)

def _sigmoid(x):
    return jax.nn.sigmoid(x)

def _layernorm(x, axis=-1, eps=1e-05):
    m = jnp.mean(x, axis=axis, keepdims=True)
    v = jnp.var(x, axis=axis, keepdims=True)
    return (x - m) / jnp.sqrt(v + eps)

def _scatter_add(tgt, idx, src, axis=0):
    return tgt.at[idx].add(src)

def _segment_sum(src, seg, n):
    return jax.ops.segment_sum(src, seg, n)
kernel_name = 'mk_macaron_d1_jaxref_r8_d94de5'

def setup_inputs(seed: int=0):
    np.random.seed(seed)
    _w = jnp.asarray

    def _L0_attn_setup():
        import jax, jax.numpy as jnp
        import numpy as np
        import math
        B, T, C = (2, 256, 128)
        NH = 16
        HD = C // NH

        def _rope_factor(T, d, dtype):
            theta = 1.0 / 10000.0 ** (2.0 * jnp.arange(0, d // 2, dtype=jnp.float32) / d)
            seq = jnp.arange(1, T + 1, dtype=jnp.float32)
            ang = jnp.einsum('n,d->nd', seq, theta)
            ang = jnp.concatenate([ang, ang], axis=-1)
            return (jnp.cos(ang) + jnp.sin(ang)).astype(dtype)
        key = jax.random.key(seed)
        ks = jax.random.split(key, 5)
        s = 0.02
        return {'x': jax.random.normal(ks[0], (B, T, C), dtype=jnp.float32), 'W_attn': jax.random.normal(ks[1], (3 * C, C), dtype=jnp.float32) * s, 'b_attn': jax.random.normal(ks[2], (3 * C,), dtype=jnp.float32) * s, 'W_proj': jax.random.normal(ks[3], (C, C), dtype=jnp.float32) * s, 'b_proj': jax.random.normal(ks[4], (C,), dtype=jnp.float32) * s}
    _L0_attn_in = _L0_attn_setup()

    def _L0_ffn_setup():
        import jax, jax.numpy as jnp
        import numpy as np
        DIM = 128
        DEPTH = 2
        HEADS = 8
        DIM_HEAD = 64
        WINDOW = 64
        INNER = HEADS * DIM_HEAD
        HID = int(DIM * 4 * 2 / 3)
        B, N = (2, 1024)
        QK_SCALE = 8.0

        def shift_token(t):
            t1, t2 = jnp.split(t, 2, axis=-1)
            t2 = jnp.pad(t2, ((0, 0), (1, 0), (0, 0)))[:, :-1]
            return jnp.concatenate([t1, t2], axis=-1)

        def l2norm(t):
            return t / jnp.clip(jnp.linalg.norm(t, axis=-1, keepdims=True), 1e-12)

        def rotate_half(x):
            x1, x2 = jnp.split(x, 2, axis=-1)
            return jnp.concatenate([-x2, x1], axis=-1)

        def rotary_xpos(q, k):
            n = q.shape[-2]
            half_idx = jnp.arange(0, DIM_HEAD, 2, dtype=jnp.float32)
            inv_freq = 1.0 / 10000.0 ** (half_idx / DIM_HEAD)
            t = jnp.arange(n, dtype=jnp.float32)
            freqs = t[:, None] * inv_freq[None, :]
            freqs = jnp.concatenate([freqs, freqs], axis=-1)
            base = (half_idx + 0.4 * DIM_HEAD) / (1.4 * DIM_HEAD)
            power = (t - n // 2) / float(WINDOW // 2)
            scale = base[None, :] ** power[:, None]
            scale = jnp.concatenate([scale, scale], axis=-1)
            cos, sin = (jnp.cos(freqs), jnp.sin(freqs))
            q = q * cos * scale + rotate_half(q) * sin * scale
            k = k * cos / scale + rotate_half(k) * sin / scale
            return (q, k)

        def local_attention(q, k, v):
            b, h, n, d = q.shape
            w = n // WINDOW
            bq = q.reshape(b, h, w, WINDOW, d) * QK_SCALE
            bk = k.reshape(b, h, w, WINDOW, d)
            bv = v.reshape(b, h, w, WINDOW, d)

            def look_around(t):
                p = jnp.pad(t, ((0, 0), (0, 0), (1, 0), (0, 0), (0, 0)))
                return jnp.concatenate([p[:, :, :w], p[:, :, 1:]], axis=3)
            bk, bv = (look_around(bk), look_around(bv))
            bt = jnp.arange(n).reshape(w, WINDOW)
            btp = jnp.pad(bt, ((1, 0), (0, 0)), constant_values=-1)
            btk = jnp.concatenate([btp[:w], btp[1:]], axis=1)
            sim = jnp.einsum('bhwid,bhwjd->bhwij', bq, bk)
            i = bt[:, :, None]
            j = btk[:, None, :]
            mask = (i < j) | (i > j + WINDOW) | (j == -1)
            sim = jnp.where(mask, -jnp.finfo(sim.dtype).max, sim)
            attn = jax.nn.softmax(sim, axis=-1)
            out = jnp.einsum('bhwij,bhwjd->bhwid', attn, bv)
            return out.reshape(b, h, n, d)

        def _layer(x, wqkv, qs, ksc, wo, lg, lb, w1, b1, w2, b2):
            b, n, _ = x.shape
            h = shift_token(x)
            qkv = h @ wqkv
            q, k, v = jnp.split(qkv, 3, axis=-1)
            to_heads = lambda t: t.reshape(b, n, HEADS, DIM_HEAD).transpose(0, 2, 1, 3)
            q, k, v = (to_heads(q), to_heads(k), to_heads(v))
            q = l2norm(q) * qs
            k = l2norm(k) * ksc
            q, k = rotary_xpos(q, k)
            o = local_attention(q, k, v)
            o = o.transpose(0, 2, 1, 3).reshape(b, n, INNER)
            x = x + o @ wo
            h = shift_token(x)
            mu = h.mean(-1, keepdims=True)
            var = h.var(-1, keepdims=True)
            h = (h - mu) / jnp.sqrt(var + 1e-05) * lg + lb
            h = h @ w1 + b1
            a, g = jnp.split(h, 2, axis=-1)
            h = a * jax.nn.gelu(g, approximate=False)
            x = x + h @ w2 + b2
            return x
        key = jax.random.key(seed)
        ks = jax.random.split(key, 6)
        return {'x': jax.random.normal(ks[0], (B, N, DIM), jnp.float32), 'wqkv': jax.random.normal(ks[1], (DEPTH, DIM, 3 * INNER), jnp.float32) * 0.02, 'q_scale': jnp.ones((DEPTH, DIM_HEAD), jnp.float32), 'k_scale': jnp.ones((DEPTH, DIM_HEAD), jnp.float32), 'wo': jax.random.normal(ks[2], (DEPTH, INNER, DIM), jnp.float32) * 0.02, 'ln_g': jnp.ones((DEPTH, DIM), jnp.float32), 'ln_b': jnp.zeros((DEPTH, DIM), jnp.float32), 'w1': jax.random.normal(ks[3], (DEPTH, DIM, 2 * HID), jnp.float32) * 0.02, 'b1': jnp.zeros((DEPTH, 2 * HID), jnp.float32), 'w2': jax.random.normal(ks[4], (DEPTH, HID, DIM), jnp.float32) * 0.02, 'b2': jnp.zeros((DEPTH, DIM), jnp.float32)}
    _L0_ffn_in = _L0_ffn_setup()
    _d = {'L0_attn_x': _L0_attn_in['x'], 'L0_attn_W_attn': _L0_attn_in['W_attn'], 'L0_attn_b_attn': _L0_attn_in['b_attn'], 'L0_attn_W_proj': _L0_attn_in['W_proj'], 'L0_attn_b_proj': _L0_attn_in['b_proj'], 'L0_ffn_wqkv': _L0_ffn_in['wqkv'], 'L0_ffn_q_scale': _L0_ffn_in['q_scale'], 'L0_ffn_k_scale': _L0_ffn_in['k_scale'], 'L0_ffn_wo': _L0_ffn_in['wo'], 'L0_ffn_ln_g': _L0_ffn_in['ln_g'], 'L0_ffn_ln_b': _L0_ffn_in['ln_b'], 'L0_ffn_w1': _L0_ffn_in['w1'], 'L0_ffn_b1': _L0_ffn_in['b1'], 'L0_ffn_w2': _L0_ffn_in['w2'], 'L0_ffn_b2': _L0_ffn_in['b2']}
    _x0 = _d['L0_attn_x']
    _d['L0_attn_x'] = jax.random.normal(jax.random.fold_in(jax.random.key(seed), 1), (4, 512, 128), dtype=_x0.dtype)
    del _x0
    return _d

def reference(L0_attn_x, L0_attn_W_attn, L0_attn_b_attn, L0_attn_W_proj, L0_attn_b_proj, L0_ffn_wqkv, L0_ffn_q_scale, L0_ffn_k_scale, L0_ffn_wo, L0_ffn_ln_g, L0_ffn_ln_b, L0_ffn_w1, L0_ffn_b1, L0_ffn_w2, L0_ffn_b2):

    def _L0_attn_ref(x, W_attn, b_attn, W_proj, b_proj):
        import jax, jax.numpy as jnp
        import numpy as np
        import math
        B, T, C = (2, 256, 128)
        NH = 16
        HD = C // NH

        def _rope_factor(T, d, dtype):
            theta = 1.0 / 10000.0 ** (2.0 * jnp.arange(0, d // 2, dtype=jnp.float32) / d)
            seq = jnp.arange(1, T + 1, dtype=jnp.float32)
            ang = jnp.einsum('n,d->nd', seq, theta)
            ang = jnp.concatenate([ang, ang], axis=-1)
            return (jnp.cos(ang) + jnp.sin(ang)).astype(dtype)
        Bs, Ts, Cs = x.shape
        qkv = x @ W_attn.T + b_attn
        q, k, v = jnp.split(qkv, 3, axis=-1)

        def to_heads(t):
            return t.reshape(Bs, Ts, NH, HD).transpose(0, 2, 1, 3)
        q, k, v = (to_heads(q), to_heads(k), to_heads(v))
        f = _rope_factor(Ts, HD, x.dtype)
        q = q * f
        k = k * f
        att = jnp.einsum('bhqd,bhkd->bhqk', q, k) * (1.0 / math.sqrt(HD))
        causal = jnp.tril(jnp.ones((Ts, Ts), dtype=bool))
        att = jnp.where(causal, att, jnp.finfo(att.dtype).min)
        att = jax.nn.softmax(att, axis=-1)
        y = jnp.einsum('bhqk,bhkd->bhqd', att, v)
        y = y.transpose(0, 2, 1, 3).reshape(Bs, Ts, Cs)
        y = y @ W_proj.T + b_proj
        return y

    def _L0_ffn_ref(x, wqkv, q_scale, k_scale, wo, ln_g, ln_b, w1, b1, w2, b2):
        import jax, jax.numpy as jnp
        import numpy as np
        DIM = 128
        DEPTH = 2
        HEADS = 8
        DIM_HEAD = 64
        WINDOW = 64
        INNER = HEADS * DIM_HEAD
        HID = int(DIM * 4 * 2 / 3)
        B, N = (2, 1024)
        QK_SCALE = 8.0

        def shift_token(t):
            t1, t2 = jnp.split(t, 2, axis=-1)
            t2 = jnp.pad(t2, ((0, 0), (1, 0), (0, 0)))[:, :-1]
            return jnp.concatenate([t1, t2], axis=-1)

        def l2norm(t):
            return t / jnp.clip(jnp.linalg.norm(t, axis=-1, keepdims=True), 1e-12)

        def rotate_half(x):
            x1, x2 = jnp.split(x, 2, axis=-1)
            return jnp.concatenate([-x2, x1], axis=-1)

        def rotary_xpos(q, k):
            n = q.shape[-2]
            half_idx = jnp.arange(0, DIM_HEAD, 2, dtype=jnp.float32)
            inv_freq = 1.0 / 10000.0 ** (half_idx / DIM_HEAD)
            t = jnp.arange(n, dtype=jnp.float32)
            freqs = t[:, None] * inv_freq[None, :]
            freqs = jnp.concatenate([freqs, freqs], axis=-1)
            base = (half_idx + 0.4 * DIM_HEAD) / (1.4 * DIM_HEAD)
            power = (t - n // 2) / float(WINDOW // 2)
            scale = base[None, :] ** power[:, None]
            scale = jnp.concatenate([scale, scale], axis=-1)
            cos, sin = (jnp.cos(freqs), jnp.sin(freqs))
            q = q * cos * scale + rotate_half(q) * sin * scale
            k = k * cos / scale + rotate_half(k) * sin / scale
            return (q, k)

        def local_attention(q, k, v):
            b, h, n, d = q.shape
            w = n // WINDOW
            bq = q.reshape(b, h, w, WINDOW, d) * QK_SCALE
            bk = k.reshape(b, h, w, WINDOW, d)
            bv = v.reshape(b, h, w, WINDOW, d)

            def look_around(t):
                p = jnp.pad(t, ((0, 0), (0, 0), (1, 0), (0, 0), (0, 0)))
                return jnp.concatenate([p[:, :, :w], p[:, :, 1:]], axis=3)
            bk, bv = (look_around(bk), look_around(bv))
            bt = jnp.arange(n).reshape(w, WINDOW)
            btp = jnp.pad(bt, ((1, 0), (0, 0)), constant_values=-1)
            btk = jnp.concatenate([btp[:w], btp[1:]], axis=1)
            sim = jnp.einsum('bhwid,bhwjd->bhwij', bq, bk)
            i = bt[:, :, None]
            j = btk[:, None, :]
            mask = (i < j) | (i > j + WINDOW) | (j == -1)
            sim = jnp.where(mask, -jnp.finfo(sim.dtype).max, sim)
            attn = jax.nn.softmax(sim, axis=-1)
            out = jnp.einsum('bhwij,bhwjd->bhwid', attn, bv)
            return out.reshape(b, h, n, d)

        def _layer(x, wqkv, qs, ksc, wo, lg, lb, w1, b1, w2, b2):
            b, n, _ = x.shape
            h = shift_token(x)
            qkv = h @ wqkv
            q, k, v = jnp.split(qkv, 3, axis=-1)
            to_heads = lambda t: t.reshape(b, n, HEADS, DIM_HEAD).transpose(0, 2, 1, 3)
            q, k, v = (to_heads(q), to_heads(k), to_heads(v))
            q = l2norm(q) * qs
            k = l2norm(k) * ksc
            q, k = rotary_xpos(q, k)
            o = local_attention(q, k, v)
            o = o.transpose(0, 2, 1, 3).reshape(b, n, INNER)
            x = x + o @ wo
            h = shift_token(x)
            mu = h.mean(-1, keepdims=True)
            var = h.var(-1, keepdims=True)
            h = (h - mu) / jnp.sqrt(var + 1e-05) * lg + lb
            h = h @ w1 + b1
            a, g = jnp.split(h, 2, axis=-1)
            h = a * jax.nn.gelu(g, approximate=False)
            x = x + h @ w2 + b2
            return x
        for l in range(DEPTH):
            x = _layer(x, wqkv[l], q_scale[l], k_scale[l], wo[l], ln_g[l], ln_b[l], w1[l], b1[l], w2[l], b2[l])
        return x
    x = L0_attn_x
    x = x + 0.5 * _L0_ffn_ref(_layernorm(x, axis=-1), L0_ffn_wqkv, L0_ffn_q_scale, L0_ffn_k_scale, L0_ffn_wo, L0_ffn_ln_g, L0_ffn_ln_b, L0_ffn_w1, L0_ffn_b1, L0_ffn_w2, L0_ffn_b2)
    x = x + _L0_attn_ref(_layernorm(x, axis=-1), L0_attn_W_attn, L0_attn_b_attn, L0_attn_W_proj, L0_attn_b_proj)
    x = x + 0.5 * _L0_ffn_ref(_layernorm(x, axis=-1), L0_ffn_wqkv, L0_ffn_q_scale, L0_ffn_k_scale, L0_ffn_wo, L0_ffn_ln_g, L0_ffn_ln_b, L0_ffn_w1, L0_ffn_b1, L0_ffn_w2, L0_ffn_b2)
    return x

_drawn_inputs = setup_inputs


def setup_inputs(seed=0):
    import zlib

    import numpy as np

    out = dict(_drawn_inputs(seed))
    spreads = {'L0_ffn_q_scale': (1.0, 0.6),
     'L0_ffn_k_scale': (1.0, 0.6),
     'L0_ffn_ln_g': (1.0, 0.6),
     'L0_ffn_ln_b': (0.0, 0.8),
     'L0_ffn_b1': (0.0, 0.8),
     'L0_ffn_b2': (0.0, 0.1)}
    factors = {'L0_attn_W_attn': 8.0,
     'L0_attn_b_attn': 8.0,
     'L0_attn_W_proj': 8.0,
     'L0_attn_b_proj': 12.327,
     'L0_ffn_wqkv': 3.174,
     'L0_ffn_wo': 3.167,
     'L0_ffn_w1': 5.295,
     'L0_ffn_w2': 5.209}
    for name, (base, spread) in spreads.items():
        noise = np.random.default_rng([zlib.crc32(name.encode()), seed]).standard_normal(out[name].shape)
        drawn = base * np.exp(spread * noise) if base else spread * noise
        out[name] = jnp.asarray(drawn.astype(out[name].dtype))
    for name, factor in factors.items():
        out[name] = (out[name] * factor).astype(out[name].dtype)
    return out
```

```python
import math
import concourse.bass as bass
from concourse import mybir
from contextlib import ExitStack

import numpy as np

BATCH, SEQ, DIM = 4, 512, 128
HEADS, DH, WIN = 8, 64, 64
INNER = HEADS * DH
LAYERS = 2
HID = int(DIM * 4 * 2 / 3)
TILES = SEQ // 128
HB = [114, 114, HID - 228]
HO = [0, 114, 228]
NH, HD = 16, DIM // 16
BIG = -1e30

C_ID, C_CEN, C_ONE, C_MF, C_MS, C_CS, C_CT, C_COS, C_SIN, C_F = (
    0, 128, 256, 384, 512, 640, 768, 896, 1408, 1920)
C_ALL = C_F + 2 * SEQ


def constants():
    c = np.zeros((128, C_ALL), np.float32)
    i = np.arange(128)
    c[:, C_ID:C_ID + 128] = np.eye(128)
    c[:, C_CEN:C_CEN + 128] = np.eye(128) - 1.0 / 128
    c[:, C_ONE:C_ONE + 128] = 1.0 / 128
    q, col = i[:64, None], i[None, :]
    first = np.where(col < 64, col <= q, col >= q + 64)
    second = (col >= q) & (col <= q + 64)
    start = first & (col < 64)
    c[:, C_MS:C_MS + 128] = np.where(np.concatenate([first, second]), 0, BIG)
    c[:, C_MF:C_MF + 128] = np.where(np.concatenate([start, second]), 0, BIG)
    c[:, C_CS:C_CS + 128] = np.where(i[None, :] <= i[:, None], 0, BIG)
    c[:, C_CT:C_CT + 128] = np.where(i[None, :] >= i[:, None], 0, BIG)
    half = np.arange(0, DH, 2, dtype=np.float32)
    inv = (np.float32(1.0) / np.float32(10000.0) ** (half / np.float32(DH))).astype(np.float32)
    t = np.arange(SEQ, dtype=np.float32)
    fr = (t[:, None] * inv[None, :]).astype(np.float32)
    fr = np.concatenate([fr, fr], -1).astype(np.float64)
    base = ((half + 0.4 * DH) / (1.4 * DH)).astype(np.float32).astype(np.float64)
    sc = base[None, :] ** ((t.astype(np.float64) - SEQ // 2) / float(WIN // 2))[:, None]
    sc = np.concatenate([sc, sc], -1)
    sign = np.where(np.arange(DH) < DH // 2, -1.0, 1.0)
    for h, (s, g) in enumerate(((sc, 8.0), (1 / sc, 1.0))):
        cos = np.cos(fr) * s * g * 256.0
        sin = np.sin(fr) * s * g * 256.0 * sign
        for j in range(TILES):
            o = j * 128 + h * DH
            c[:, C_COS + o:C_COS + o + DH] = cos[j * 128:(j + 1) * 128]
            c[:, C_SIN + o:C_SIN + o + DH] = sin[j * 128:(j + 1) * 128]
    th = (1.0 / 10000.0 ** (2.0 * np.arange(0, HD // 2, dtype=np.float32) / HD)).astype(np.float32)
    ang = (np.arange(1, SEQ + 1, dtype=np.float32)[:, None] * th[None, :]).astype(np.float32)
    ang = np.concatenate([ang, ang], -1).astype(np.float64)
    f = np.repeat((np.cos(ang) + np.sin(ang)).T, NH, axis=0)
    c[:, C_F:C_F + SEQ] = f / math.sqrt(HD)
    c[:, C_F + SEQ:] = f
    return c


def macaron(nc, x, W_attn, b_attn, W_proj, b_proj, wqkv, q_scale, k_scale, wo, ln_g, ln_b,
            w1, b1, w2, b2, cst, out):
    F, BF = mybir.dt.float32, mybir.dt.bfloat16
    ALU, ACT, AX = mybir.AluOpType, mybir.ActivationFunctionType, mybir.AxisListType.X

    ctx = ExitStack()
    with ctx:
        def sb(name, shape, dt=F):
            return ctx.enter_context(nc.sbuf_tensor(name, shape, dt))

        def sem(name):
            return ctx.enter_context(nc.semaphore(name))

        PS = ctx.enter_context(nc.psum_tensor("PS", [128, 8, 512], F))
        qk_ps = PS[:, 0:2, :].rearrange("p a n -> p (a n)")
        v_ps = PS[:, 2, :]
        sc_ps = PS[:, 3:5, :].rearrange("p a n -> p (a n)")
        tr_ps = PS[:, 5:7, :].rearrange("p a n -> p (a n)")
        o_ps = PS[:, 7, :]

        C = sb("C", [128, C_ALL])
        ident, centre, mean = C[:, 0:128], C[:, 128:256], C[:, 256:384]
        cb = sb("cb", [128, 5, 128], BF)
        identb, mask_start, mask_inner, mask_qk, mask_kq = (cb[:, i, :] for i in range(5))
        cc = sb("cc", [128, 2])
        xT = sb("xT", [128, BATCH, SEQ])
        yT = sb("yT", [128, BATCH, SEQ + 2])
        zT = sb("zT", [128, BATCH, SEQ + 2])
        wqkv_s = sb("wqkv_s", [128, LAYERS, 3 * INNER])
        wo_s = sb("wo_s", [128, LAYERS, 4, DIM])
        w1_s = sb("w1_s", [128, LAYERS, 2 * HID])
        w2_s = sb("w2_s", [128, LAYERS, 3, DIM])
        g_s = sb("g_s", [128, LAYERS, 2])
        b1_s = sb("b1_s", [128, LAYERS, 2, 3])
        b2_s = sb("b2_s", [128, LAYERS])
        qks = sb("qks", [128, LAYERS, 2, DH])
        cosT = sb("cosT", [128, LAYERS, TILES, 2, DH])
        sinT = sb("sinT", [128, LAYERS, TILES, 2, DH])
        wqkT = sb("wqkT", [128, 3, DIM])
        wpT = sb("wpT", [128, DIM])
        bqk = sb("bqk", [128, 2])
        bvp = sb("bvp", [128, 3])
        hn = sb("hn", [128, SEQ])
        sq5 = sb("sq5", [128, SEQ])
        lnv = sb("lnv", [128, SEQ])
        rstd = sb("rstd", [128, SEQ])

        arena = sb("arena", [128, 28160])
        at = [0]

        def carve(*shape):
            n = int(np.prod(shape))
            v = arena[:, at[0]:at[0] + n]
            at[0] += n
            if len(shape) == 2:
                v = v.rearrange("p (a b) -> p a b", a=shape[0])
            if len(shape) == 3:
                v = v.rearrange("p (a b c) -> p a b c", a=shape[0], b=shape[1])
            if len(shape) == 4:
                v = v.rearrange("p (a b c d) -> p a b c d", a=shape[0], b=shape[1], c=shape[2])
            return v

        h_in = carve(2, 128)
        sq = carve(1024)
        nrm = carve(3, 16)
        rn = carve(16)
        qn = carve(2, 1024)
        rs = carve(2, 1024)
        rc = carve(1024)
        qr = carve(2, 1024)
        qz = carve(HEADS, 128)
        kT = carve(2, 4, 128)
        v_s = carve(4, INNER)
        vm = carve(4, INNER)
        p_s = carve(2, HEADS, 128)
        nmax = carve(2, HEADS)
        den = carve(2, HEADS)
        rden = carve(2, HEADS)
        pT = carve(HEADS, 128)
        oT = carve(4, 128)
        u_s = carve(3, SEQ)
        layer_words = at[0]

        at[0] = 0
        qst = carve(2, NH * SEQ // 2)
        kst = carve(2, NH * SEQ // 2)
        vp = carve(TILES, NH, 32)
        qkf = carve(2, SEQ)
        part = carve(3, SEQ)
        mx = carve(4, 16)
        mres = carve(128)
        mpart = carve(3 * 64)
        osb = carve(SEQ)
        rec = carve(TILES, 4)
        ytok = carve(TILES, DIM)
        yaT = carve(SEQ)
        pe_s = carve(4, 1280)
        mid_words = at[0]
        assert max(layer_words, mid_words) <= 28160, (layer_words, mid_words)
        qstb = qst.bitcast(BF).rearrange("p s (h t) -> p s h t", h=NH)
        kstb = kst.bitcast(BF).rearrange("p s (h t) -> p s h t", h=NH)
        partb = part.bitcast(BF).rearrange("p i (c t) -> p i c t", c=2)
        mpartb = mpart.bitcast(BF).rearrange("p (i t) -> p i t", i=3)

        xin = arena[:, 0:2048].rearrange("p (n f) -> p n f", f=DIM)
        wa = arena[:, 2048:2048 + 512].rearrange("p (n f) -> p n f", f=DIM)

        scr = nc.dram_tensor("scr", (3, 128, 2, SEQ), BF, kind="Internal").ap()
        scrm = nc.dram_tensor("scrm", (3, NH, TILES, 128), BF, kind="Internal").ap()

        loaded = sem("loaded")
        xt_ps = sem("xt_ps")
        xt_done = sem("xt_done")
        scaled = sem("scaled")
        w_ps = sem("w_ps")
        w_done = sem("w_done")
        bias_ps = sem("bias_ps")
        zeroed = sem("zeroed")
        h_ready = sem("h_ready")
        qkv_done = sem("qkv_done")
        sq_done = sem("sq_done")
        v_ready = sem("v_ready")
        ss_done = sem("ss_done")
        ssc_done = sem("ssc_done")
        lnq_done = sem("lnq_done")
        r_done = sem("r_done")
        qn_done = sem("qn_done")
        rots_done = sem("rots_done")
        rotc_done = sem("rotc_done")
        qr_done = sem("qr_done")
        qktr_done = sem("qktr_done")
        qzhi_done = sem("qzhi_done")
        qzlo_done = sem("qzlo_done")
        kt_done = sem("kt_done")
        sc_done = sem("sc_done")
        max_done = sem("max_done")
        exp_done = sem("exp_done")
        rden_done = sem("rden_done")
        pn_done = sem("pn_done")
        pttr_done = sem("pttr_done")
        pta_done = sem("pta_done")
        ptd_done = sem("ptd_done")
        pv_done = sem("pv_done")
        oev_done = sem("oev_done")
        wo_done = sem("wo_done")
        z_done = sem("z_done")
        vm_done = sem("vm_done")
        cen_done = sem("cen_done")
        csq_done = sem("csq_done")
        var_done = sem("var_done")
        lnr_done = sem("lnr_done")
        rstd_done = sem("rstd_done")
        hn_done = sem("hn_done")
        g_done = sem("g_done")
        gl_done = sem("gl_done")
        a_done = sem("a_done")
        u_done = sem("u_done")
        w2_done = sem("w2_done")
        y_ready = sem("y_ready")
        x_ready = sem("x_ready")
        out_ps = sem("out_ps")
        out_sb = sem("out_sb")
        stored = sem("stored")
        m_qk = sem("m_qk")
        m_v = sem("m_v")
        m_vp = sem("m_vp")
        m_f = sem("m_f")
        m_p1 = sem("m_p1")
        m_r1 = sem("m_r1")
        m_p2 = sem("m_p2")
        m_p3 = sem("m_p3")
        m_sav = sem("m_sav")
        m_stk = sem("m_stk")
        m_s = sem("m_s")
        m_max = sem("m_max")
        m_t = sem("m_t")
        m_m1 = sem("m_m1")
        m_m2 = sem("m_m2")
        m_m3 = sem("m_m3")
        m_m4 = sem("m_m4")
        m_msav = sem("m_msav")
        m_st = sem("m_st")
        m_exp = sem("m_exp")
        m_pv = sem("m_pv")
        m_osb = sem("m_osb")
        m_ot = sem("m_ot")
        m_rec = sem("m_rec")
        m_yt = sem("m_yt")
        m_ytt = sem("m_ytt")
        m_ya = sem("m_ya")
        m_pr = sem("m_pr")
        m_free = sem("m_free")
        max_stacked = [sem(f"max_stacked{g}") for g in range(4)]

        def y_count(L, b):
            return (L + L // 2) * 4 + b + 1

        def tile(L, b, j, back):
            if j >= back:
                return L, b, j - back
            if isinstance(b, int) and b == 0:
                return (L - 1, BATCH - 1, j - back + 4) if L % 2 else None
            return L, b - 1, j - back + 4

        def num(t):
            L, b, j = t
            return 16 * L + 4 * b + j

        def ln_centre(pe, src, dst):
            return nc.tensor.matmul(dst, centre, src, start=True, stop=True)

        def norm_index(L, b):
            return (4 + 4 * L + b) if L < 2 else (SECOND_NORM + 4 + 4 * (L - 2) + b)

        MID_NORM, SECOND_NORM = 12, 16

        ORDER = [("t", 0), ("t", 1), ("o", 0), ("t", 2), ("o", 1), ("t", 3), ("o", 2), ("o", 3), ("y", 0)]

        def bank7_before_max(b, g):
            return len(ORDER) * b + ORDER.index(("t", g))

        def bank7_before_pv(b, g):
            return len(ORDER) * b + ORDER.index(("o", g))

        block = ctx.enter_context(nc.Block())

        LOADS = []

        def load(dst, src):
            LOADS.append((dst, src))

        for i in range(BATCH * TILES):
            load(xin[:, i, :], x[i // TILES, 128 * (i % TILES):128 * (i % TILES) + 128, :])
        load(C[:, :], cst)
        load(g_s[:, :, 0:1], ln_g.rearrange("l (p o) -> p l o", o=1))
        load(g_s[:, :, 1:2], ln_b.rearrange("l (p o) -> p l o", o=1))
        load(qks[:, :, 0, :], q_scale.rearrange("(o l) d -> o l d", o=1).broadcast_to((128, LAYERS, DH)))
        load(qks[:, :, 1, :], k_scale.rearrange("(o l) d -> o l d", o=1).broadcast_to((128, LAYERS, DH)))
        load(wqkv_s[:, :, :], wqkv.rearrange("l p n -> p l n"))
        load(wo_s[:, :, :, :], wo.rearrange("l (k p) n -> p l k n", p=128))
        load(w1_s[:, :, :], w1.rearrange("l p n -> p l n"))
        for l in range(LAYERS):
            for m in range(3):
                load(w2_s[0:HB[m], l, m, :], w2[l, HO[m]:HO[m] + HB[m], :])
                for a in range(2):
                    o = a * HID + HO[m]
                    load(b1_s[0:HB[m], l, a, m:m + 1],
                         b1[l, o:o + HB[m]].rearrange("(p o) -> p o", o=1))
        load(b2_s[:, :], b2.rearrange("l p -> p l"))
        load(wa[:, 0:3, :], W_attn.rearrange("(c p) n -> p c n", p=128))
        load(wa[:, 3, :], W_proj)
        for c in range(2):
            for d in range(HD):
                load(bqk[16 * d:16 * d + 16, c:c + 1],
                     b_attn[c * DIM:(c + 1) * DIM].rearrange("(h d o) -> d h o", d=HD, o=1)[d])
        load(bvp[:, 0:1], b_attn[2 * DIM:3 * DIM].rearrange("(p o) -> p o", o=1))
        load(bvp[:, 1:2], b_proj.rearrange("(p o) -> p o", o=1))

        @block.sync
        def _(sp):
            with nc.allow_non_contiguous_dma("small vectors, one element per partition"):
                for dst, src in LOADS:
                    sp.dma_start(dst, src).then_inc(loaded, 16)

            def stack(b, k):
                sp.wait_ge(m_p3, b + 1)
                if b == 0:
                    sp.wait_ge(zeroed, 2)
                for i in range(3):
                    sp.dma_start(scr[i], partb[:, i, :, :]).then_inc(m_sav, 16)
                sp.wait_ge(m_sav, 48 * (b + 1))
                v = scr.rearrange("i (d h) c t -> (i d) c h t", h=NH)
                for i in range(3):
                    sp.dma_start(kstb[24 * i:24 * i + 24, k, :, :], v[:, 1, :, :]).then_inc(m_stk, 16)
                    for j in range(3):
                        r = 24 * i + 8 * j
                        sp.dma_start(qstb[r:r + 8, k, :, :], v[8 * i:8 * i + 8, 0, :, :]).then_inc(m_stk, 16)
                sp.dma_start(qstb[72:75, k, :, :], qstb[76:79, k, :, :]).then_inc(m_stk, 16)

            def stack_max(b, g, k):
                n = 4 * b + g
                sp.wait_ge(m_m4, n + 1)
                sp.dma_start(scrm[:, 4 * g:4 * g + 4, :, :].rearrange("i h q t -> (h q) i t"),
                             mpartb[0:16, :, :]).then_inc(m_msav, 16)
                sp.wait_ge(m_msav, 16 * (n + 1))
                sp.dma_start(qstb[72:75, k, 4 * g:4 * g + 4, :],
                             scrm[:, 4 * g:4 * g + 4, :, :].rearrange("i h q t -> i h (q t)")
                             ).then_inc(max_stacked[g], 16)

            for b in range(BATCH):
                stack(b, b % 2)
                for g in range(4):
                    stack_max(b, g, b % 2)
            for b in range(BATCH):
                sp.wait_ge(out_sb, 4 * b + 4)
                sp.dma_start(out[b].rearrange("(n p) f -> p n f", p=128),
                             arena[:, b * 512:(b + 1) * 512].rearrange("p (n f) -> p n f", f=DIM)
                             ).then_inc(stored, 16)
            sp.wait_ge(stored, 16 * BATCH)

        N_LOADS = 16 * len(LOADS)

        @block.tensor
        def _(pe):
            mm, tr = nc.tensor.matmul, nc.tensor.transpose

            def qkv(t):
                (L, b, j), n = t, num(t)
                pe.wait_ge(h_ready, n + 1)
                if not (isinstance(b, int) and n == 0):
                    pe.wait_ge(qn_done, n)
                    pe.wait_ge(v_ready, n)
                h = h_in[:, j % 2, :]
                mm(qk_ps[:, 0:512], h, wqkv_s[:, L % 2, 0:512], start=True, stop=True)
                mm(qk_ps[:, 512:1024], h, wqkv_s[:, L % 2, 512:1024], start=True, stop=True)
                mm(v_ps, h, wqkv_s[:, L % 2, 1024:1536], start=True, stop=True).then_inc(qkv_done, 1)

            def qk_transposes(t):
                (L, b, j), n = t, num(t)
                pe.wait_ge(qr_done, n + 1)
                if not (isinstance(b, int) and n < 2):
                    pe.wait_ge(pta_done, n - 1)
                    pe.wait_ge(ptd_done, n - 1)
                for i in range(8):
                    last = tr(tr_ps[:, i * 128:(i + 1) * 128], qr[:, j % 2, i * 128:(i + 1) * 128], ident)
                last.then_inc(qktr_done, 1)

            def scores(t):
                (L, b, j), n = t, num(t)
                k = j % 2
                if not (isinstance(b, int) and n == 0):
                    pe.wait_ge(exp_done, n)
                for c in range(2):
                    m = (mask_inner if j else mask_start).rearrange("p (o n) -> p o n", o=1)
                    mm(sc_ps[:, c * 512:(c + 1) * 512].rearrange("p (h n) -> p h n", h=4), identb,
                       m.broadcast_to((128, 4, 128)), start=True, stop=False)
                    if c == 0:
                        pe.wait_ge(qzhi_done, n + 1)
                        pe.wait_ge(qzlo_done, n + 1)
                        pe.wait_ge(kt_done, n + 1)
                    for h in range(4 * c, 4 * c + 4):
                        o = sc_ps[:, h * 128:(h + 1) * 128]
                        keys = kT[:, k, h // 2, :]
                        base = keys.offset
                        step = (1 - 2 * k) * 512 + 64
                        split = bass.AP(keys.tensor, base, [list(keys.ap[0]), [step, 2], [1, 64]])
                        mm(o[0:64].rearrange("p (a c) -> p a c", a=2), qz[:, h, 0:64], split,
                           start=False, stop=h % 4 == 3)
                        last = mm(o[64:128], qz[:, h, 64:128], keys, start=False, stop=h % 4 == 3)
                last.then_inc(sc_done, 1)

            def p_transposes(t, newer):
                n = num(t)
                pe.wait_ge(pn_done, n + 1)
                if newer is not None:
                    m = num(newer)
                    pe.wait_ge(qzhi_done, m + 1)
                    pe.wait_ge(qzlo_done, m + 1)
                    pe.wait_ge(kt_done, m + 1)
                for h in range(HEADS):
                    last = tr(tr_ps[:, h * 128:(h + 1) * 128], p_s[:, t[2] % 2, h, :], ident)
                last.then_inc(pttr_done, 1)

            def pv(t):
                (L, b, j), n = t, num(t)
                pe.wait_ge(pta_done, n + 1)
                pe.wait_ge(ptd_done, n + 1)
                pe.wait_ge(v_ready, n + 1)
                pe.wait_ge(vm_done, n + 1)
                if not (isinstance(b, int) and n == 0):
                    pe.wait_ge(z_done, n)
                for w in range(2):
                    for h in range(HEADS):
                        r, c = 64 * (h % 2), (h // 2) * 128 + 64 * w
                        val = v_s if w else vm
                        last = mm(o_ps[r:r + 64, c:c + 64], val[:, j, h * 64:(h + 1) * 64],
                                  pT[:, h, 64 * w:64 * w + 64], start=True, stop=True)
                last.then_inc(pv_done, 1)

            def project(t):
                L, n = t[0], num(t)
                pe.wait_ge(oev_done, n + 1)
                for k in range(4):
                    last = mm(o_ps[:, 0:128], wo_s[:, L % 2, k, :], oT[:, k, :], start=k == 0, stop=k == 3)
                last.then_inc(wo_done, 1)

            def norm(q, src):
                mm(PS[:, 0, :], centre, src, start=True, stop=True).then_inc(cen_done, 1)
                pe.wait_ge(csq_done, q + 1)
                mm(PS[:, 1, :], mean, sq5[:, :], start=True, stop=True).then_inc(var_done, 1)

            def mlp(L, b, newest):
                q, nq = norm_index(L, b), 4 * L + b
                pe.wait_ge(z_done, num((L, b, 3)) + 1)
                pe.wait_ge(qn_done, num(newest) + 1)
                pe.wait_ge(v_ready, num(newest) + 1)
                norm(q, zT[:, b, 0:SEQ])
                pe.wait_ge(hn_done, q + 1)
                l = L % 2
                for m in range(3):
                    o = HID + HO[m]
                    mm(PS[0:HB[m], m, :], w1_s[:, l, o:o + HB[m]], hn[:, :], start=True,
                       stop=True).then_inc(g_done, 1)
                for m in range(3):
                    pe.wait_ge(gl_done, 3 * nq + m + 1)
                    mm(PS[0:HB[m], m, :], w1_s[:, l, HO[m]:HO[m] + HB[m]], hn[:, :], start=True,
                       stop=True).then_inc(a_done, 1)
                for m in range(3):
                    pe.wait_ge(u_done, 3 * nq + m + 1)
                    last = mm(o_ps, w2_s[0:HB[m], l, m, :], u_s[0:HB[m], m, :], start=m == 0, stop=m == 2)
                last.then_inc(w2_done, 1)
                pe.wait_ge(y_ready, y_count(L + 1, b) if L % 2 == 0 else y_count(L, b) + 4)

            def step(L, b, j, live=True):
                if (t := tile(L, b, j, 2)) is not None:
                    if live or j < 2:
                        scores(t)
                if (t := tile(L, b, j, 3)) is not None:
                    p_transposes(t, tile(L, b, j, 2) if live or j < 2 else None)
                if live:
                    qkv((L, b, j))
                if (t := tile(L, b, j, 3)) is not None:
                    pv(t)
                if (t := tile(L, b, j, 1)) is not None and (live or j < 1):
                    qk_transposes(t)
                if (t := tile(L, b, j, 3)) is not None:
                    project(t)
                    if t[2] == 3:
                        mlp(t[0], t[1], (L, b, j) if live else t)

            def layers(block_no):
                for L in (2 * block_no, 2 * block_no + 1):
                    for j in range(4):
                        step(L, 0, j)
                    with pe.Fori(1, BATCH) as b:
                        for j in range(4):
                            step(L, b, j)
                for j in range(3):
                    step(L, BATCH, j, live=False)

            def norms(base, wait_x):
                for b in range(BATCH):
                    pe.wait_ge(x_ready, wait_x + b)
                    if b or base:
                        pe.wait_ge(hn_done, base + b)
                    norm(base + b, xT[:, b, :])

            pe.wait_ge(loaded, N_LOADS)
            for i in range(16):
                if i >= 8:
                    pe.wait_ge(xt_done, i // 4 - 1)
                last = tr(PS[:, (i // 4) % 2, (i % 4) * 128:(i % 4) * 128 + 128], xin[:, i, :], ident)
                if i % 4 == 3:
                    last.then_inc(xt_ps, 1)
            for i in range(4):
                last = tr(PS[:, 2, i * 128:(i + 1) * 128], wa[:, i, :], ident)
            last.then_inc(w_ps, 1)
            for l in range(LAYERS):
                for a in range(2):
                    for m in range(3):
                        i = (l * 2 + a) * 3 + m
                        o = a * HID + HO[m]
                        mm(PS[0:HB[m], 3, i:i + 1], w1_s[:, l, o:o + HB[m]], g_s[:, l, 1:2],
                           start=True, stop=True)
            pe.wait_ge(w_done, 1)
            mm(PS[:, 3, 12:13], wpT[:, :], bvp[:, 0:1], start=True, stop=True).then_inc(bias_ps, 1)
            pe.wait_ge(scaled, 1)
            norms(0, 1)
            pe.wait_ge(hn_done, 4)
            layers(0)

            def prepare(b, k):
                pe.wait_ge(x_ready, 4 + b + 1)
                q = MID_NORM + b
                if b:
                    pe.wait_ge(m_exp, 24 * b)
                norm(q, xT[:, b, :])
                pe.wait_ge(hn_done, q + 1)
                for c in range(2):
                    mm(PS[:, 2 + c, :], wqkT[:, c, :], hn[:, :], start=True, stop=True).then_inc(m_qk, 1)
                for i in range(TILES):
                    last = mm(PS[:, 4, i * 128:(i + 1) * 128], hn[:, i * 128:(i + 1) * 128], wqkT[:, 2, :],
                              start=True, stop=True)
                last.then_inc(m_v, 1)

            def s_block(bank, col, k, h, qt):
                n = 128 * (qt + 1)
                mm(PS[:, bank, col:col + n], qstb[0:96, k, h, 128 * qt:128 * qt + 128],
                   kstb[0:96, k, h, 0:n], start=True, stop=False)
                return mm(PS[:, bank, col + n - 128:col + n], identb, mask_qk, start=False, stop=True)

            def s_pass(b, g, k):
                for p in range(2):
                    h = 4 * g + 2 * p
                    units = [[(0, h, 3)], [(0, h, 2), (384, h, 0)], [(0, h + 1, 3)],
                             [(0, h + 1, 2), (384, h + 1, 0)], [(0, h, 1), (256, h + 1, 1)]]
                    for i, unit in enumerate(units):
                        n = ((b * 4 + g) * 2 + p) * 5 + i
                        if n >= 2:
                            pe.wait_ge(m_max, n - 1)
                        for col, hh, qt in unit:
                            last = s_block(5 + n % 2, col, k, hh, qt)
                        last.then_inc(m_s, 1)
                n = 4 * b + g
                pe.wait_ge(m_max, 10 * (n + 1))
                if n:
                    pe.wait_ge(m_free, bank7_before_max(b, g))
                tr(PS[0:16, 7, 0:128], mx[:, g, :], ident).then_inc(m_t, 1)

            def st_block(bank, col, k, h, kt):
                n = SEQ - 128 * kt
                mm(PS[:, bank, col:col + n], kstb[0:96, k, h, 128 * kt:128 * kt + 128],
                   qstb[0:96, k, h, 128 * kt:SEQ], start=True, stop=False)
                return mm(PS[:, bank, col:col + 128], identb, mask_kq, start=False, stop=True)

            def st_pass(b, g, k):
                pe.wait_ge(max_stacked[g], 16 * (b + 1))
                if g == 0:
                    pe.wait_ge(m_f, 2 * b + 2)
                    pe.wait_ge(m_vp, b + 1)
                for p in range(2):
                    h = 4 * g + 2 * p
                    pair = (b * 4 + g) * 2 + p
                    units = [[(0, 0, h, 0), (1, 0, h, 1), (1, 384, h, 3)],
                             [(2, 0, h + 1, 0), (3, 0, h + 1, 1), (3, 384, h + 1, 3)],
                             [(4, 0, h, 2), (4, 256, h + 1, 2)]]
                    for i, unit in enumerate(units):
                        if pair:
                            pe.wait_ge(m_exp, 3 * (pair - 1) + i + 1)
                        for bank, col, hh, kt in unit:
                            last = st_block(bank, col, k, hh, kt)
                        last.then_inc(m_st, 1)

            PT_COL = {0: 0, 1: 512, 3: 896, 2: 1024}

            def mid_pv(b, g):
                n = 4 * b + g
                pe.wait_ge(m_exp, 6 * (n + 1))
                pe.wait_ge(m_vp, b + 1)
                pe.wait_ge(m_free, bank7_before_pv(b, g))
                for kt in range(TILES):
                    for j in range(4):
                        h = 4 * g + j
                        last = mm(PS[32 * j:32 * j + 32, 7, 128 * kt:SEQ], vp[:, kt, h, :],
                                  pe_s[:, j, PT_COL[kt]:PT_COL[kt] + SEQ - 128 * kt],
                                  start=kt == 0, stop=kt == TILES - 1, tile_position=(0, 32 * j))
                last.then_inc(m_pv, 1)
                pe.wait_ge(m_osb, n + 1)
                for i in range(TILES):
                    last = tr(PS[:, 7, i * 128:(i + 1) * 128], osb[:, i * 128:(i + 1) * 128], ident)
                last.then_inc(m_ot, 1)

            def mid_project(b):
                pe.wait_ge(m_yt, 4 * (b + 1))
                for i in range(TILES):
                    last = tr(PS[:, 7, i * 128:(i + 1) * 128], ytok[:, i, :], ident)
                last.then_inc(m_ytt, 1)
                pe.wait_ge(m_ya, b + 1)
                mm(PS[:, 7, :], wpT[:, :], yaT[:, :], start=True, stop=True).then_inc(m_pr, 1)

            for b in range(BATCH):
                k = b % 2
                prepare(b, k)
                pe.wait_ge(m_stk, 16 * 13 * (b + 1))
                for g in range(4):
                    s_pass(b, g, k)
                    if g:
                        st_pass(b, g - 1, k)
                        mid_pv(b, g - 1)
                st_pass(b, 3, k)
                mid_pv(b, 3)
                mid_project(b)

            norms(SECOND_NORM, 9)
            pe.wait_ge(hn_done, SECOND_NORM + 4)
            layers(1)
            for i in range(16):
                pe.wait_ge(x_ready, 12 + i // 4 + 1)
                if i >= 2:
                    pe.wait_ge(out_sb, i - 1)
                tr(PS[:, i % 2, 0:128], xT[:, i // 4, (i % 4) * 128:(i % 4) * 128 + 128], ident).then_inc(
                    out_ps, 1)

        @block.scalar
        def _(act):
            A = nc.scalar.activation
            nc.scalar.preload_act_table_set("natural_log_exp_and_others")

            def squares(t):
                n = num(t)
                act.wait_ge(qkv_done, n + 1)
                if not isinstance(t[1], int) or n:
                    act.wait_ge(ss_done, n)
                A(sq, qk_ps, ACT.Square).then_inc(sq_done, 1)

            def v_evict(t):
                n = num(t)
                if not isinstance(t[1], int) or n >= 4:
                    act.wait_ge(pv_done, n - 3)
                    act.wait_ge(vm_done, n - 2)
                A(v_s[:, t[2], :], v_ps, ACT.Copy).then_inc(v_ready, 1)

            def norms_of_heads(t):
                n = num(t)
                act.wait_ge(ssc_done, n + 1)
                A(nrm[:, 2, :], nrm[:, 1, :], ACT.Ln, scale=65536.0).then_inc(lnq_done, 1)
                act.wait_ge(lnq_done, n + 1)
                if not isinstance(t[1], int) or n:
                    act.wait_ge(qn_done, n)
                A(rn, nrm[:, 2, :], ACT.Exp, scale=-0.5).then_inc(r_done, 1)

            def q_upper(t):
                n = num(t)
                act.wait_ge(qktr_done, n + 1)
                if not isinstance(t[1], int) or n:
                    act.wait_ge(sc_done, n)
                A(qz[64:128, 1::2, :], tr_ps[64:128, 0:512].rearrange("p (h n) -> p h n", h=4),
                  ACT.Copy).then_inc(qzhi_done, 1)

            def softmax(t):
                (L, b, j), n = t, num(t)
                k = j % 2
                act.wait_ge(max_done, n + 1)
                if not isinstance(b, int) or n >= 2:
                    act.wait_ge(pttr_done, n - 1)
                    act.wait_ge(rden_done, n - 1)
                for h in range(HEADS):
                    last = A(p_s[:, k, h, :], sc_ps[:, h * 128:(h + 1) * 128], ACT.Exp,
                             bias=nmax[:, k, h:h + 1], accum_out=den[:, k, h:h + 1])
                last.then_inc(exp_done, 1)

            def pt_evict(t):
                n = num(t)
                act.wait_ge(pttr_done, n + 1)
                if not isinstance(t[1], int) or n:
                    act.wait_ge(pv_done, n)
                A(pT[:, 0:4, :], tr_ps[:, 0:512].rearrange("p (h n) -> p h n", h=4),
                  ACT.Copy).then_inc(pta_done, 1)

            def o_evict(t):
                n = num(t)
                act.wait_ge(pv_done, n + 1)
                if not isinstance(t[1], int) or n:
                    act.wait_ge(wo_done, n)
                A(oT, o_ps.rearrange("p (k n) -> p k n", k=4), ACT.Copy).then_inc(oev_done, 1)

            def norm(q):
                act.wait_ge(cen_done, q + 1)
                A(sq5[:, :], PS[:, 0, :], ACT.Square).then_inc(csq_done, 1)
                act.wait_ge(var_done, q + 1)
                A(lnv[:, :], PS[:, 1, :], ACT.Ln, bias=cc[:, 0:1]).then_inc(lnr_done, 1)
                act.wait_ge(lnr_done, q + 1)
                if not isinstance(q, int) or q:
                    act.wait_ge(hn_done, q)
                A(rstd[:, :], lnv[:, :], ACT.Exp, scale=-0.5).then_inc(rstd_done, 1)

            def mlp(L, b):
                q, nq = norm_index(L, b), 4 * L + b
                norm(q)
                for m in range(3):
                    act.wait_ge(g_done, 3 * nq + m + 1)
                    if not (isinstance(nq, int) and nq == 0):
                        act.wait_ge(w2_done, nq)
                    A(u_s[0:HB[m], m, :], PS[0:HB[m], m, :], ACT.Gelu,
                      bias=b1_s[0:HB[m], L % 2, 1, m:m + 1]).then_inc(gl_done, 1)
                nc.scalar.preload_act_table_set("natural_log_exp_and_others")

            def step(L, b, j, live=True):
                t2, t3, t1 = tile(L, b, j, 2), tile(L, b, j, 3), tile(L, b, j, 1)
                if t2 is not None and (live or j < 2):
                    softmax(t2)
                if t3 is not None:
                    pt_evict(t3)
                if live:
                    squares((L, b, j))
                    v_evict((L, b, j))
                    norms_of_heads((L, b, j))
                if t3 is not None:
                    o_evict(t3)
                if t1 is not None and (live or j < 1):
                    q_upper(t1)
                if t3 is not None and t3[2] == 3:
                    mlp(t3[0], t3[1])

            def layers(block_no):
                for L in (2 * block_no, 2 * block_no + 1):
                    for j in range(4):
                        step(L, 0, j)
                    with act.Fori(1, BATCH) as b:
                        for j in range(4):
                            step(L, b, j)
                for j in range(3):
                    step(L, BATCH, j, live=False)

            act.wait_ge(zeroed, 1)
            for q in range(4):
                norm(q)
            layers(0)

            def mid_softmax(b, g):
                for p in range(2):
                    pair = (b * 4 + g) * 2 + p
                    j = 2 * p
                    if pair >= 2:
                        act.wait_ge(m_pv, (pair - 2) // 2 + 1)
                    act.wait_ge(m_st, 3 * pair + 1)
                    A(pe_s[:, j, 0:1024], PS[:, 0:2, :].rearrange("p a n -> p (a n)"),
                      ACT.Exp).then_inc(m_exp, 1)
                    act.wait_ge(m_st, 3 * pair + 2)
                    A(pe_s[:, j + 1, 0:1024], PS[:, 2:4, :].rearrange("p a n -> p (a n)"),
                      ACT.Exp).then_inc(m_exp, 1)
                    act.wait_ge(m_st, 3 * pair + 3)
                    A(pe_s[:, j:j + 2, 1024:1280], PS[:, 4, :].rearrange("p (a n) -> p a n", a=2),
                      ACT.Exp).then_inc(m_exp, 1)

            def o_evict_mid(b, g):
                n = 4 * b + g
                act.wait_ge(m_pv, n + 1)
                A(osb, PS[:, 7, :], ACT.Copy).then_inc(m_osb, 1)

            for b in range(BATCH):
                norm(MID_NORM + b)
                act.wait_ge(m_v, b + 1)
                if b == 0:
                    act.wait_ge(zeroed, 2)
                A(vp[:, :, :, 0:HD], PS[:, 4, :].rearrange("p (t h d) -> p t h d", t=TILES, h=NH),
                  ACT.Copy).then_inc(m_vp, 1)
                for g in range(4):
                    mid_softmax(b, g)
                    o_evict_mid(b, g)
                act.wait_ge(m_ytt, b + 1)
                A(yaT, PS[:, 7, :], ACT.Copy).then_inc(m_ya, 1)
            for q in range(4):
                norm(SECOND_NORM + q)
            layers(1)

        @block.vector
        def _(dve):
            V = nc.vector

            def sum_squares(t):
                n = num(t)
                dve.wait_ge(sq_done, n + 1)
                V.reduce_sum(nrm[:, 0, :], sq.rearrange("p (g d) -> p g d", d=DH), AX).then_inc(ss_done, 1)
                dve.wait_ge(ss_done, n + 1)
                if not isinstance(t[1], int) or n:
                    dve.wait_ge(lnq_done, n)
                V.tensor_scalar(nrm[:, 1, :], nrm[:, 0, :], 1e-24, None, ALU.max).then_inc(ssc_done, 1)

            def copy_v(t):
                (L, b, j), n = t, num(t)
                dve.wait_ge(v_ready, n + 1)
                if not isinstance(b, int) or n >= 4:
                    dve.wait_ge(pv_done, n - 3)
                V.tensor_copy(vm[0:64, j, :], v_s[0:64, j, :])
                V.tensor_copy(vm[64:128, j, :], v_s[64:128, (j + 3) % 4, :]).then_inc(vm_done, 1)

            def normalise(t):
                n, k = num(t), t[2] % 2
                dve.wait_ge(r_done, n + 1)
                if not isinstance(t[1], int) or n >= 2:
                    dve.wait_ge(rots_done, n - 1)
                    dve.wait_ge(rotc_done, n - 1)
                V.tensor_tensor(qn[:, k, :].rearrange("p (g d) -> p g d", d=DH),
                                qk_ps.rearrange("p (g d) -> p g d", d=DH),
                                rn.rearrange("p (g o) -> p g o", o=1).broadcast_to((128, 16, DH)),
                                ALU.mult).then_inc(qn_done, 1)

            def rotate(t):
                (L, b, j), n = t, num(t)
                k = j % 2
                dve.wait_ge(qn_done, n + 1)
                if not isinstance(b, int) or n:
                    dve.wait_ge(qr_done, n)
                V.tensor_tensor(rc.rearrange("p (c h d) -> p c h d", c=2, h=HEADS),
                                qn[:, k, :].rearrange("p (c h d) -> p c h d", c=2, h=HEADS),
                                cosT[:, L % 2, j, :, :].rearrange("p c (o d) -> p c o d", o=1)
                                .broadcast_to((128, 2, HEADS, DH)), ALU.mult).then_inc(rotc_done, 1)
                dve.wait_ge(rotc_done, n + 1)
                dve.wait_ge(rots_done, n + 1)
                if not isinstance(b, int) or n >= 2:
                    dve.wait_ge(qktr_done, n - 1)
                V.tensor_tensor(qr[:, k, :], rc, rs[:, k, :], ALU.add).then_inc(qr_done, 1)

            def q_lower_and_k(t):
                n, k = num(t), t[2] % 2
                dve.wait_ge(qktr_done, n + 1)
                if not isinstance(t[1], int) or n:
                    dve.wait_ge(sc_done, n)
                V.tensor_copy(qz[0:64, 0::2, :],
                              tr_ps[0:64, 0:512].rearrange("p (h n) -> p h n", h=4)).then_inc(qzlo_done, 1)
                V.tensor_copy(kT[:, k, :, :],
                              tr_ps[:, 512:1024].rearrange("p (h n) -> p h n", h=4)).then_inc(kt_done, 1)

            def row_max(t):
                n, k = num(t), t[2] % 2
                dve.wait_ge(sc_done, n + 1)
                if not isinstance(t[1], int) or n >= 2:
                    dve.wait_ge(exp_done, n - 1)
                V.reduce_max(nmax[:, k, :], sc_ps.rearrange("p (h n) -> p h n", h=HEADS), AX,
                             negate=True).then_inc(max_done, 1)

            def reciprocal(t):
                n, k = num(t), t[2] % 2
                dve.wait_ge(exp_done, n + 1)
                if not isinstance(t[1], int) or n >= 2:
                    dve.wait_ge(pn_done, n - 1)
                V.reciprocal(rden[:, k, :], den[:, k, :]).then_inc(rden_done, 1)

            def pt_evict(t):
                n = num(t)
                dve.wait_ge(pttr_done, n + 1)
                if not isinstance(t[1], int) or n:
                    dve.wait_ge(pv_done, n)
                V.tensor_copy(pT[:, 4:8, :],
                              tr_ps[:, 512:1024].rearrange("p (h n) -> p h n", h=4)).then_inc(ptd_done, 1)

            def residual(t):
                (L, b, j), n = t, num(t)
                dve.wait_ge(wo_done, n + 1)
                lo, up = slice(128 * j, 128 * j + 128), slice(128 * j + 1, 128 * j + 129)
                V.tensor_tensor(zT[0:64, b, lo], o_ps[0:64, 0:128], yT[0:64, b, lo], ALU.add)
                V.tensor_tensor(zT[64:128, b, up], o_ps[64:128, 0:128], yT[64:128, b, up],
                                ALU.add).then_inc(z_done, 1)

            def norm(q, outs):
                dve.wait_ge(rstd_done, q + 1)
                for i, (dst, r) in enumerate(outs):
                    last = V.tensor_tensor(dst, PS[r, 0, :], rstd[r, :], ALU.mult)
                last.then_inc(hn_done, 1)

            LO, UP, ALLP = slice(0, 64), slice(64, 128), slice(0, 128)

            def mlp(L, b):
                q, nq, l = norm_index(L, b), 4 * L + b, L % 2
                norm(q, [(hn[:, :], ALLP)])
                for m in range(3):
                    dve.wait_ge(a_done, 3 * nq + m + 1)
                    V.scalar_tensor_tensor(u_s[0:HB[m], m, :], PS[0:HB[m], m, :],
                                           b1_s[0:HB[m], l, 0, m:m + 1], u_s[0:HB[m], m, :],
                                           ALU.add, ALU.mult).then_inc(u_done, 1)
                dve.wait_ge(w2_done, nq + 1)
                V.scalar_tensor_tensor(yT[0:64, b, 0:SEQ], o_ps[0:64, :], b2_s[0:64, l:l + 1],
                                       zT[0:64, b, 0:SEQ], ALU.add, ALU.add)
                V.scalar_tensor_tensor(yT[64:128, b, 1:SEQ + 1], o_ps[64:128, :], b2_s[64:128, l:l + 1],
                                       zT[64:128, b, 1:SEQ + 1], ALU.add, ALU.add).then_inc(y_ready, 1)

            def step(L, b, j, live=True):
                t1, t2, t3 = tile(L, b, j, 1), tile(L, b, j, 2), tile(L, b, j, 3)
                if t3 is not None:
                    reciprocal(t3)
                if t2 is not None and (live or j < 2):
                    row_max(t2)
                if t3 is not None:
                    pt_evict(t3)
                if live:
                    sum_squares((L, b, j))
                    copy_v((L, b, j))
                    normalise((L, b, j))
                if t1 is not None and (live or j < 1):
                    q_lower_and_k(t1)
                if live:
                    rotate((L, b, j))
                if t3 is not None:
                    residual(t3)
                    if t3[2] == 3:
                        mlp(t3[0], t3[1])

            def layers(block_no):
                for L in (2 * block_no, 2 * block_no + 1):
                    for j in range(4):
                        step(L, 0, j)
                    with dve.Fori(1, BATCH) as b:
                        for j in range(4):
                            step(L, b, j)
                for j in range(3):
                    step(L, BATCH, j, live=False)

            def block_norm(q, b):
                norm(q, [(yT[0:64, b, 0:SEQ], LO), (yT[64:128, b, 1:SEQ + 1], UP)])
                dve.wait_ge(hn_done, q + 1)
                V.engine_nop().then_inc(y_ready, 1)

            def add_half(b, k):
                dve.wait_ge(y_ready, 12 * (k + 1))
                V.scalar_tensor_tensor(xT[0:64, b, :], yT[0:64, b, 0:SEQ], 0.5, xT[0:64, b, :],
                                       ALU.mult, ALU.add)
                V.scalar_tensor_tensor(xT[64:128, b, :], yT[64:128, b, 1:SEQ + 1], 0.5, xT[64:128, b, :],
                                       ALU.mult, ALU.add).then_inc(x_ready, 1)

            V.memset(cc[:, 0:1], 1e-5)
            for b in range(BATCH):
                V.memset(yT[64:128, b, 0:1], 0.0)
                V.memset(zT[64:128, b, 0:1], 0.0)
            dve.wait_ge(loaded, N_LOADS)
            for i, o in enumerate((C_ID, C_MF, C_MS, C_CS, C_CT)):
                V.tensor_copy(cb[:, i, :], C[:, o:o + 128])
            for b in range(BATCH):
                dve.wait_ge(xt_ps, b + 1)
                V.tensor_copy(xT[:, b, :], PS[:, b % 2, :]).then_inc(xt_done, 1)
            dve.wait_ge(w_ps, 1)
            for c in range(2):
                V.tensor_copy(wqkT[:, c, :].rearrange("p (d h) -> p h d", d=HD),
                              PS[:, 2, c * 128:(c + 1) * 128].rearrange("p (h d) -> p h d", d=HD))
            V.tensor_copy(wqkT[:, 2, :], PS[:, 2, 256:384])
            V.tensor_copy(wpT[:, :], PS[:, 2, 384:512]).then_inc(w_done, 1)
            dve.wait_ge(bias_ps, 1)
            dve.wait_ge(xt_done, 4)
            for l in range(LAYERS):
                for a in range(2):
                    for m in range(3):
                        i = (l * 2 + a) * 3 + m
                        r = slice(0, HB[m])
                        V.tensor_tensor(b1_s[r, l, a, m:m + 1], b1_s[r, l, a, m:m + 1],
                                        PS[r, 3, i:i + 1], ALU.add)
            V.tensor_tensor(bvp[:, 2:3], bvp[:, 1:2], PS[:, 3, 12:13], ALU.add)
            for l in range(LAYERS):
                V.tensor_scalar(w1_s[:, l, :], w1_s[:, l, :], g_s[:, l, 0:1], None, ALU.mult)
                for j in range(TILES):
                    V.tensor_tensor(cosT[:, l, j, :, :],
                                    C[:, C_COS + 128 * j:C_COS + 128 * j + 128].rearrange("p (c d) -> p c d", c=2),
                                    qks[:, l, :, :], ALU.mult)
                    for half in range(2):
                        d, e = slice(32 * half, 32 * half + 32), slice(32 - 32 * half, 64 - 32 * half)
                        V.tensor_tensor(sinT[:, l, j, :, d],
                                        C[:, C_SIN + 128 * j:C_SIN + 128 * j + 128].rearrange(
                                            "p (c d) -> p c d", c=2)[:, :, d],
                                        qks[:, l, :, e], ALU.mult)
            for i in range(4):
                V.engine_nop().then_inc(x_ready, 1)
            V.memset(qz, 0.0)
            V.memset(kT, 0.0)
            V.memset(v_s[:, 3, :], 0.0).then_inc(scaled, 1)
            V.engine_nop().then_inc(zeroed, 1)
            for b in range(BATCH):
                block_norm(b, b)
            layers(0)
            for b in range(BATCH):
                add_half(b, 0)

            def zero_mid():
                for k in range(2):
                    V.memset(qst[64:96, k, :], 0.0)
                    V.memset(kstb[64:96, k, :, :], 1.0)
                V.memset(vp[:, :, :, HD + 1:32], 0.0)
                V.memset(vp[:, :, :, HD:HD + 1], 1.0).then_inc(zeroed, 1)

            def split_qk(b):
                for c in range(2):
                    dve.wait_ge(m_qk, 2 * b + c + 1)
                    if b:
                        dve.wait_ge(m_sav, 48 * b)
                    V.scalar_tensor_tensor(qkf[:, c, :], PS[:, 2 + c, :], bqk[:, c:c + 1],
                                           C[:, C_F + c * SEQ:C_F + (c + 1) * SEQ], ALU.add,
                                           ALU.mult).then_inc(m_f, 1)
                dve.wait_ge(m_f, 2 * b + 2)
                V.tensor_copy(partb[:, 0, :, :], qkf).then_inc(m_p1, 1)
                dve.wait_ge(m_p1, b + 1)
                V.tensor_tensor(qkf, qkf, partb[:, 0, :, :], ALU.subtract).then_inc(m_r1, 1)
                dve.wait_ge(m_r1, b + 1)
                V.tensor_copy(partb[:, 1, :, :], qkf).then_inc(m_p2, 1)
                dve.wait_ge(m_p2, b + 1)
                V.tensor_tensor(partb[:, 2, :, :], qkf, partb[:, 1, :, :], ALU.subtract).then_inc(m_p3, 1)

            def maxima(b, g):
                for p in range(2):
                    c = 8 * p
                    for i in range(5):
                        n = ((b * 4 + g) * 2 + p) * 5 + i
                        bank = PS[:, 5 + n % 2, :]
                        dve.wait_ge(m_s, n + 1)
                        if i == 0 and (4 * b + g) >= 1:
                            dve.wait_ge(m_t, 4 * b + g)
                        m = mx[:, g, :]
                        if i in (0, 2):
                            o = c + 4 * (i // 2) + 3
                            last = V.reduce_max(m[:, o:o + 1], bank, AX)
                        elif i in (1, 3):
                            o = c + 4 * (i // 2)
                            V.reduce_max(m[:, o + 2:o + 3], bank[:, 0:384], AX)
                            last = V.reduce_max(m[:, o:o + 1], bank[:, 384:512], AX)
                        else:
                            last = V.reduce_max(m[:, c + 1:c + 6:4],
                                                bank.rearrange("p (a n) -> p a n", a=2), AX)
                        last.then_inc(m_max, 1)
                n = 4 * b + g
                t = PS[0:16, 7, 0:128]
                dve.wait_ge(m_t, n + 1)
                if n:
                    dve.wait_ge(m_msav, 16 * n)
                V.tensor_scalar(mpartb[0:16, 0, :], t, -1.0, None, ALU.mult).then_inc(m_m1, 1)
                dve.wait_ge(m_m1, n + 1)
                V.scalar_tensor_tensor(mres[0:16, :], t, -1.0, mpartb[0:16, 0, :], ALU.mult,
                                       ALU.subtract).then_inc(m_m2, 1)
                dve.wait_ge(m_m2, n + 1)
                V.engine_nop().then_inc(m_free, 1)
                V.tensor_copy(mpartb[0:16, 1, :], mres[0:16, :]).then_inc(m_m3, 1)
                dve.wait_ge(m_m3, n + 1)
                V.tensor_tensor(mpartb[0:16, 2, :], mres[0:16, :], mpartb[0:16, 1, :],
                                ALU.subtract).then_inc(m_m4, 1)

            def mid_normalise(b, g):
                n = 4 * b + g
                dve.wait_ge(m_ot, n + 1)
                if n:
                    dve.wait_ge(m_yt, n)
                o = PS[:, 7, :].rearrange("p (q j e) -> p q j e", q=TILES, j=4)
                V.reciprocal(rec.rearrange("p q (j o) -> p q j o", o=1), o[:, :, :, HD:HD + 1]).then_inc(m_rec, 1)
                dve.wait_ge(m_rec, n + 1)
                if g == 0 and b:
                    dve.wait_ge(m_ytt, b)
                V.tensor_tensor(ytok[:, :, 32 * g:32 * g + 32].rearrange("p q (j e) -> p q j e", j=4),
                                o[:, :, :, 0:HD],
                                rec.rearrange("p q (j o) -> p q j o", o=1).broadcast_to((128, TILES, 4, HD)),
                                ALU.mult).then_inc(m_yt, 1)
                dve.wait_ge(m_yt, n + 1)
                V.engine_nop().then_inc(m_free, 1)

            zero_mid()
            for b in range(BATCH):
                norm(MID_NORM + b, [(hn[:, :], ALLP)])
                split_qk(b)
                for g in range(4):
                    maxima(b, g)
                    if g:
                        mid_normalise(b, g - 1)
                mid_normalise(b, 3)
                dve.wait_ge(m_pr, b + 1)
                V.scalar_tensor_tensor(xT[:, b, :], PS[:, 7, :], bvp[:, 2:3], xT[:, b, :],
                                       ALU.add, ALU.add).then_inc(x_ready, 1)
                dve.wait_ge(x_ready, 8 + b + 1)
                V.engine_nop().then_inc(m_free, 1)

            dve.wait_ge(m_pr, BATCH)
            V.memset(qz, 0.0)
            V.memset(kT, 0.0)
            V.memset(v_s[:, 3, :], 0.0).then_inc(zeroed, 1)
            for b in range(BATCH):
                block_norm(SECOND_NORM + b, b)
            layers(1)
            for b in range(BATCH):
                add_half(b, 1)
            for i in range(16):
                dve.wait_ge(out_ps, i + 1)
                V.tensor_copy(arena[:, i * 128:(i + 1) * 128], PS[:, i % 2, 0:128]).then_inc(out_sb, 1)

        @block.gpsimd
        def _(pool):
            P = nc.gpsimd

            def shifted_input(t):
                (L, b, j), n = t, num(t)
                pool.wait_ge(y_ready, y_count(L, b))
                if not isinstance(b, int) or n >= 2:
                    pool.wait_ge(qkv_done, n - 1)
                P.tensor_copy(h_in[:, j % 2, :], yT[:, b, 128 * j:128 * j + 128]).then_inc(h_ready, 1)

            def sine_part(t):
                (L, b, j), n = t, num(t)
                k = j % 2
                pool.wait_ge(qn_done, n + 1)
                if not isinstance(b, int) or n >= 2:
                    pool.wait_ge(qr_done, n - 1)
                for c in range(2):
                    src = qn[:, k, 512 * c:512 * c + 512]
                    base = src.offset
                    swapped = bass.AP(src.tensor, base + 32, [list(src.ap[0]), [64, HEADS], [-32, 2], [1, 32]])
                    last = P.tensor_tensor(
                        rs[:, k, 512 * c:512 * c + 512].rearrange("p (h a d) -> p h a d", h=HEADS, a=2),
                        swapped,
                        sinT[:, L % 2, j, c, :].rearrange("p (o a d) -> p o a d", o=1, a=2)
                        .broadcast_to((128, HEADS, 2, 32)), ALU.mult)
                last.then_inc(rots_done, 1)

            def normalise(t):
                n, k = num(t), t[2] % 2
                pool.wait_ge(rden_done, n + 1)
                P.tensor_tensor(p_s[:, k, :, :], p_s[:, k, :, :],
                                rden[:, k, :].rearrange("p (h o) -> p h o", o=1).broadcast_to((128, HEADS, 128)),
                                ALU.mult).then_inc(pn_done, 1)

            def step(L, b, j, live=True):
                t3 = tile(L, b, j, 3)
                if live:
                    shifted_input((L, b, j))
                if t3 is not None:
                    normalise(t3)
                if live:
                    sine_part((L, b, j))

            def layers(block_no):
                for L in (2 * block_no, 2 * block_no + 1):
                    for j in range(4):
                        step(L, 0, j)
                    with pool.Fori(1, BATCH) as b:
                        for j in range(4):
                            step(L, b, j)
                for j in range(3):
                    step(L, BATCH, j, live=False)

            pool.wait_ge(zeroed, 1)
            layers(0)
            pool.wait_ge(zeroed, 3)
            layers(1)


_INS = ['L0_attn_x', 'L0_attn_W_attn', 'L0_attn_b_attn', 'L0_attn_W_proj', 'L0_attn_b_proj',
        'L0_ffn_wqkv', 'L0_ffn_q_scale', 'L0_ffn_k_scale', 'L0_ffn_wo', 'L0_ffn_ln_g', 'L0_ffn_ln_b',
        'L0_ffn_w1', 'L0_ffn_b1', 'L0_ffn_w2', 'L0_ffn_b2']


def kernel(**inputs):
    import numpy as _np
    import concourse.bacc as _bacc
    from concourse import mybir as _mybir
    from concourse.bass_utils import run_bass_kernel_spmd as _run

    nc = _bacc.Bacc("TRN2", target_bir_lowering=False, num_devices=1)
    arrays, args = {}, []
    for name in _INS:
        a = _np.ascontiguousarray(inputs[name])
        arrays[f"in_{name}_dram"] = a
        args.append(nc.dram_tensor(f"in_{name}_dram", a.shape, _mybir.dt.from_np(a.dtype), kind="ExternalInput").ap())
    c = constants()
    arrays["constants_dram"] = c
    args.append(nc.dram_tensor("constants_dram", c.shape, _mybir.dt.float32, kind="ExternalInput").ap())
    args.append(nc.dram_tensor("out_0_dram", (BATCH, SEQ, DIM), _mybir.dt.float32, kind="ExternalOutput").ap())
    macaron(nc, *args)
    r = _run(nc, [arrays], core_ids=[0])
    return r.results[0]["out_0_dram"]
```

```python
import math
import concourse.bass as bass
from concourse import mybir
from contextlib import ExitStack

import numpy as np

BATCH, SEQ, DIM = 4, 512, 128
HEADS, DH, WIN = 8, 64, 64
INNER = HEADS * DH
LAYERS = 2
HID = int(DIM * 4 * 2 / 3)
TILES = SEQ // 128
HB = [114, 114, HID - 228]
HO = [0, 114, 228]
NH, HD = 16, DIM // 16
BIG = -1e30

C_ID, C_CEN, C_ONE, C_F = 0, 128, 256, 384
C_KEPT = C_F + 2 * SEQ
C_MF, C_MS, C_CS, C_CT = (C_KEPT + 128 * i for i in range(4))
C_COS = C_KEPT + 512
C_SIN = C_COS + 2 * SEQ // 2
C_ALL = C_SIN + 2 * SEQ // 2


def constants():
    c = np.zeros((128, C_ALL), np.float32)
    i = np.arange(128)
    c[:, C_ID:C_ID + 128] = np.eye(128)
    c[:, C_CEN:C_CEN + 128] = np.eye(128) - 1.0 / 128
    c[:, C_ONE:C_ONE + 128] = 1.0 / 128
    q, col = i[:64, None], i[None, :]
    first = np.where(col < 64, col <= q, col >= q + 64)
    second = (col >= q) & (col <= q + 64)
    start = first & (col < 64)
    c[:, C_MS:C_MS + 128] = np.where(np.concatenate([first, second]), 0, BIG)
    c[:, C_MF:C_MF + 128] = np.where(np.concatenate([start, second]), 0, BIG)
    c[:, C_CS:C_CS + 128] = np.where(i[None, :] <= i[:, None], 0, BIG)
    c[:, C_CT:C_CT + 128] = np.where(i[None, :] >= i[:, None], 0, BIG)
    half = np.arange(0, DH, 2, dtype=np.float32)
    inv = (np.float32(1.0) / np.float32(10000.0) ** (half / np.float32(DH))).astype(np.float32)
    t = np.arange(SEQ, dtype=np.float32)
    fr = (t[:, None] * inv[None, :]).astype(np.float32)
    fr = np.concatenate([fr, fr], -1).astype(np.float64)
    base = ((half + 0.4 * DH) / (1.4 * DH)).astype(np.float32).astype(np.float64)
    sc = base[None, :] ** ((t.astype(np.float64) - SEQ // 2) / float(WIN // 2))[:, None]
    sc = np.concatenate([sc, sc], -1)
    sign = np.where(np.arange(DH) < DH // 2, -1.0, 1.0)
    for h, (s, g) in enumerate(((sc, 8.0), (1 / sc, 1.0))):
        cos = np.cos(fr) * s * g * 256.0
        sin = np.sin(fr) * s * g * 256.0 * sign
        for j in range(TILES):
            o = j * 128 + h * DH
            c[:, C_COS + o:C_COS + o + DH] = cos[j * 128:(j + 1) * 128]
            c[:, C_SIN + o:C_SIN + o + DH] = sin[j * 128:(j + 1) * 128]
    th = (1.0 / 10000.0 ** (2.0 * np.arange(0, HD // 2, dtype=np.float32) / HD)).astype(np.float32)
    ang = (np.arange(1, SEQ + 1, dtype=np.float32)[:, None] * th[None, :]).astype(np.float32)
    ang = np.concatenate([ang, ang], -1).astype(np.float64)
    f = np.repeat((np.cos(ang) + np.sin(ang)).T, NH, axis=0)
    c[:, C_F:C_F + SEQ] = f / math.sqrt(HD)
    c[:, C_F + SEQ:C_KEPT] = f
    return c


def macaron(nc, x, W_attn, b_attn, W_proj, b_proj, wqkv, q_scale, k_scale, wo, ln_g, ln_b,
            w1, b1, w2, b2, cst, out):
    F, BF = mybir.dt.float32, mybir.dt.bfloat16
    ALU, ACT, AX = mybir.AluOpType, mybir.ActivationFunctionType, mybir.AxisListType.X

    ctx = ExitStack()
    with ctx:
        def sb(name, shape, dt=F):
            return ctx.enter_context(nc.sbuf_tensor(name, shape, dt))

        def sem(name):
            return ctx.enter_context(nc.semaphore(name))

        PS = ctx.enter_context(nc.psum_tensor("PS", [128, 8, 512], F))
        qk_ps = PS[:, 0:2, :].rearrange("p a n -> p (a n)")
        v_ps = PS[:, 2, :]
        sc_ps = PS[:, 3:5, :].rearrange("p a n -> p (a n)")
        tr_ps = PS[:, 5:7, :].rearrange("p a n -> p (a n)")
        o_ps = PS[:, 7, :]

        C = sb("C", [128, C_KEPT])
        ident, centre, mean = C[:, 0:128], C[:, 128:256], C[:, 256:384]
        cb = sb("cb", [128, 5, 128], BF)
        identb, mask_start, mask_inner, mask_qk, mask_kq = (cb[:, i, :] for i in range(5))
        cc = sb("cc", [128, 2])
        xT = sb("xT", [128, BATCH, SEQ])
        yT = sb("yT", [128, BATCH, SEQ + 2])
        zT = sb("zT", [128, BATCH, SEQ + 2])
        wqkv_s = sb("wqkv_s", [128, LAYERS, 3 * INNER])
        wo_s = sb("wo_s", [128, LAYERS, 4, DIM])
        w1_s = sb("w1_s", [128, LAYERS, 2 * HID])
        w2_s = sb("w2_s", [128, LAYERS, 3, DIM])
        g_s = sb("g_s", [128, LAYERS, 2])
        b1_s = sb("b1_s", [128, LAYERS, 2, 3])
        b2_s = sb("b2_s", [128, LAYERS])
        qks = sb("qks", [128, LAYERS, 2, DH])
        cosT = sb("cosT", [128, LAYERS, TILES, 2, DH])
        sinT = sb("sinT", [128, LAYERS, TILES, 2, DH])
        wqkT = sb("wqkT", [128, 3, DIM])
        wpT = sb("wpT", [128, DIM])
        bqk = sb("bqk", [128, 2])
        bvp = sb("bvp", [128, 3])
        hn = sb("hn", [128, SEQ])
        hc = sb("hc", [128, SEQ])
        nsq = sb("nsq", [128, BATCH, SEQ])
        rstd = sb("rstd", [128, BATCH, SEQ])

        arena = sb("arena", [128, 30208])
        at = [0]

        def carve(*shape):
            n = int(np.prod(shape))
            v = arena[:, at[0]:at[0] + n]
            at[0] += n
            if len(shape) == 2:
                v = v.rearrange("p (a b) -> p a b", a=shape[0])
            if len(shape) == 3:
                v = v.rearrange("p (a b c) -> p a b c", a=shape[0], b=shape[1])
            if len(shape) == 4:
                v = v.rearrange("p (a b c d) -> p a b c d", a=shape[0], b=shape[1], c=shape[2])
            return v

        h_in = carve(2, 128)
        sq = carve(1024)
        nrm = carve(3, 16)
        rn = carve(16)
        qn = carve(2, 1024)
        rs = carve(2, 1024)
        rc = carve(2, 1024)
        qr = carve(2, 1024)
        qz = carve(HEADS, 128)
        kT = carve(2, 4, 128)
        v_s = carve(4, INNER)
        vm = carve(4, INNER)
        p_s = carve(2, HEADS, 128)
        nmax = carve(2, HEADS)
        den = carve(2, HEADS)
        rden = carve(2, HEADS)
        pT = carve(HEADS, 128)
        oT = carve(4, 128)
        u_s = carve(3, SEQ)
        layer_words = at[0]

        at[0] = 0
        qst = carve(2, NH * SEQ // 2)
        kst = carve(2, NH * SEQ // 2)
        vp = carve(2, TILES, NH, 32)
        mx = carve(4, 16)
        mres = carve(128)
        mpart = carve(3 * 64)
        osb = carve(SEQ)
        rec = carve(TILES, 4)
        ytok = carve(TILES, DIM)
        yaT = carve(SEQ)
        pe_s = carve(6, 1280)
        mid_words = at[0]
        assert max(layer_words, mid_words) <= 30208, (layer_words, mid_words)
        qstb = qst.bitcast(BF).rearrange("p s (h t) -> p s h t", h=NH)
        kstb = kst.bitcast(BF).rearrange("p s (h t) -> p s h t", h=NH)
        qkf = rstd[:, 1:3, :]
        partb = nsq[:, 1:4, :].bitcast(BF).rearrange("p i (c t) -> p i c t", c=2)
        mpartb = mpart.bitcast(BF).rearrange("p (i t) -> p i t", i=3)

        xin = arena[:, 0:2048].rearrange("p (n f) -> p n f", f=DIM)
        wa = arena[:, 2048:2560].rearrange("p (n f) -> p n f", f=DIM)
        CS = arena[:, 28000 - (C_ALL - C_KEPT):28000]

        scr = nc.dram_tensor("scr", (3, 128, 2, SEQ), BF, kind="Internal").ap()
        scrm = nc.dram_tensor("scrm", (3, NH, TILES, 128), BF, kind="Internal").ap()

        loaded = sem("loaded")
        xt_ps = sem("xt_ps")
        xt_done = sem("xt_done")
        scaled = sem("scaled")
        w_ps = sem("w_ps")
        w_done = sem("w_done")
        bias_ps = sem("bias_ps")
        zeroed = sem("zeroed")
        h_ready = sem("h_ready")
        qkv_done = sem("qkv_done")
        sq_done = sem("sq_done")
        v_ready = sem("v_ready")
        ss_done = sem("ss_done")
        ssc_done = sem("ssc_done")
        lnq_done = sem("lnq_done")
        r_done = sem("r_done")
        qn_done = sem("qn_done")
        rots_done = sem("rots_done")
        rotc_done = sem("rotc_done")
        qr_done = sem("qr_done")
        qktr_done = sem("qktr_done")
        qzhi_done = sem("qzhi_done")
        qzlo_done = sem("qzlo_done")
        kt_done = sem("kt_done")
        sc_done = sem("sc_done")
        max_done = sem("max_done")
        exp_done = sem("exp_done")
        rden_done = sem("rden_done")
        pn_done = sem("pn_done")
        pttr_done = sem("pttr_done")
        pta_done = sem("pta_done")
        ptd_done = sem("ptd_done")
        pv_done = sem("pv_done")
        oev_done = sem("oev_done")
        wo_done = sem("wo_done")
        z_done = sem("z_done")
        vm_done = sem("vm_done")
        cen_done = sem("cen_done")
        hc_done = sem("hc_done")
        csq_done = sem("csq_done")
        var_done = sem("var_done")
        lnr_done = sem("lnr_done")
        rstd_done = sem("rstd_done")
        hn_done = sem("hn_done")
        g_done = sem("g_done")
        gl_done = sem("gl_done")
        a_done = sem("a_done")
        u_done = sem("u_done")
        w2_done = sem("w2_done")
        y_ready = sem("y_ready")
        x_ready = sem("x_ready")
        out_ps = sem("out_ps")
        out_sb = sem("out_sb")
        stored = sem("stored")
        m_qk = sem("m_qk")
        m_v = sem("m_v")
        m_vp = sem("m_vp")
        m_f = sem("m_f")
        m_p1 = sem("m_p1")
        m_r1 = sem("m_r1")
        m_p2 = sem("m_p2")
        m_p3 = sem("m_p3")
        m_sav = sem("m_sav")
        m_stk = sem("m_stk")
        m_s = sem("m_s")
        m_max = sem("m_max")
        m_t = sem("m_t")
        m_m1 = sem("m_m1")
        m_m2 = sem("m_m2")
        m_m3 = sem("m_m3")
        m_m4 = sem("m_m4")
        m_msav = sem("m_msav")
        m_st = sem("m_st")
        m_exp = sem("m_exp")
        m_pv = sem("m_pv")
        m_osb = sem("m_osb")
        m_ot = sem("m_ot")
        m_rec = sem("m_rec")
        m_yt = sem("m_yt")
        m_ytt = sem("m_ytt")
        m_ya = sem("m_ya")
        m_pr = sem("m_pr")
        m_hc = sem("m_hc")
        max_stacked = [sem(f"max_stacked{g}") for g in range(4)]

        def y_count(L, b):
            return (L + L // 2) * 4 + b + 1

        def y_after(L, b):
            return (L + 1 + L // 2) * 4 + b + 1

        def tile(L, b, j, back):
            while j < back:
                if isinstance(b, int) and b == 0:
                    if L % 2 == 0:
                        return None
                    L, b = L - 1, BATCH
                b, back = b - 1, back - 4
            return L, b, j - back

        def stages(L, b, j, live):
            return [(L, b, j) if live else None] + [tile(L, b, j, k) if live or j < k else None
                                                   for k in range(1, 5)]

        def late(t, n):
            return not isinstance(t[1], int) or num(t) >= n

        def num(t):
            L, b, j = t
            return 16 * L + 4 * b + j

        def norm_index(L, b):
            return (4 + 4 * L + b) if L < 2 else (SECOND_NORM + 4 + 4 * (L - 2) + b)

        MID_NORM, SECOND_NORM = 12, 16

        PAIRS, LAG = 8 * BATCH, 4

        def slots(r):
            work = [None, None, None]
            if r % 2 == 0:
                if 1 <= r // 2 <= 4 * BATCH:
                    work[0] = ("max", r // 2 - 1)
                if r >= LAG + 2:
                    work[1:] = [("pv", (r - LAG - 2) // 2), ("o", (r - LAG - 2) // 2)]
            else:
                b = r // 8
                if r % 8 == 1 and b + 1 < BATCH:
                    work = [("centre", b + 1), ("variance", b + 1), ("q", b + 1)]
                if r % 8 == 3 and b + 1 < BATCH:
                    work = [("k", b + 1), None, None]
                if r % 8 == 5 and b >= 1:
                    work = [("y", b - 1), ("project", b - 1), None]
                if r % 8 == 7 and b + 1 < BATCH:
                    work = [("v", b + 1), None, None]
            return work

        PREPARE = [("centre", 0), ("variance", 0), ("q", 0), ("k", 0), ("v", 0)]
        ROUNDS = PAIRS + LAG + 2
        USES = PREPARE + [w for r in range(ROUNDS) for w in slots(r) if w is not None]

        def freed(what, n):
            return {"centre": (m_hc, n + 1), "variance": (lnr_done, MID_NORM + n + 1),
                    "q": (m_f, 2 * n + 1), "k": (m_f, 2 * n + 2), "v": (m_vp, n + 1),
                    "max": (m_m2, n + 1), "pv": (m_osb, n + 1), "o": (m_yt, n + 1),
                    "y": (m_ya, n + 1), "project": (x_ready, 4 + n + 1)}[what]

        def s_units(n):
            h = 2 * (n % 8)
            return [[(0, h, 3)], [(0, h, 2), (384, h, 0)], [(0, h + 1, 3)],
                    [(0, h + 1, 2), (384, h + 1, 0)], [(0, h, 1), (256, h + 1, 1)]]

        def st_units(n):
            h = 2 * (n % 8)
            return [[(0, 0, h, 0), (1, 0, h, 1), (1, 384, h, 3)],
                    [(2, 0, h + 1, 0), (3, 0, h + 1, 1), (3, 384, h + 1, 3)],
                    [(4, 0, h, 2), (4, 256, h + 1, 2)]]

        block = ctx.enter_context(nc.Block())

        LOADS = []

        def load(dst, src):
            LOADS.append((dst, src))

        for i in range(BATCH * TILES):
            load(xin[:, i, :], x[i // TILES, 128 * (i % TILES):128 * (i % TILES) + 128, :])
        load(C[:, :], cst[:, 0:C_KEPT])
        load(CS, cst[:, C_KEPT:])
        load(g_s[:, :, 0:1], ln_g.rearrange("l (p o) -> p l o", o=1))
        load(g_s[:, :, 1:2], ln_b.rearrange("l (p o) -> p l o", o=1))
        load(qks[:, :, 0, :], q_scale.rearrange("(o l) d -> o l d", o=1).broadcast_to((128, LAYERS, DH)))
        load(qks[:, :, 1, :], k_scale.rearrange("(o l) d -> o l d", o=1).broadcast_to((128, LAYERS, DH)))
        load(wqkv_s[:, :, :], wqkv.rearrange("l p n -> p l n"))
        load(wo_s[:, :, :, :], wo.rearrange("l (k p) n -> p l k n", p=128))
        load(w1_s[:, :, :], w1.rearrange("l p n -> p l n"))
        for l in range(LAYERS):
            for m in range(3):
                load(w2_s[0:HB[m], l, m, :], w2[l, HO[m]:HO[m] + HB[m], :])
                for a in range(2):
                    o = a * HID + HO[m]
                    load(b1_s[0:HB[m], l, a, m:m + 1],
                         b1[l, o:o + HB[m]].rearrange("(p o) -> p o", o=1))
        load(b2_s[:, :], b2.rearrange("l p -> p l"))
        load(wa[:, 0:3, :], W_attn.rearrange("(c p) n -> p c n", p=128))
        load(wa[:, 3, :], W_proj)
        for c in range(2):
            for d in range(HD):
                load(bqk[16 * d:16 * d + 16, c:c + 1],
                     b_attn[c * DIM:(c + 1) * DIM].rearrange("(h d o) -> d h o", d=HD, o=1)[d])
        load(bvp[:, 0:1], b_attn[2 * DIM:3 * DIM].rearrange("(p o) -> p o", o=1))
        load(bvp[:, 1:2], b_proj.rearrange("(p o) -> p o", o=1))

        @block.sync
        def _(sp):
            with nc.allow_non_contiguous_dma("small vectors, one element per partition"):
                for dst, src in LOADS:
                    sp.dma_start(dst, src).then_inc(loaded, 16)

            def stack_max(n):
                b, g = n // 4, n % 4
                sp.wait_ge(m_m4, n + 1)
                sp.dma_start(scrm[:, 4 * g:4 * g + 4, :, :].rearrange("i h q t -> (h q) i t"),
                             mpartb[0:16, :, :]).then_inc(m_msav, 16)
                sp.wait_ge(m_msav, 16 * (n + 1))
                sp.dma_start(qstb[72:75, b % 2, 4 * g:4 * g + 4, :],
                             scrm[:, 4 * g:4 * g + 4, :, :].rearrange("i h q t -> i h (q t)")
                             ).then_inc(max_stacked[g], 16)

            for n in range(4 * BATCH):
                stack_max(n)
            for b in range(BATCH):
                sp.wait_ge(out_sb, 4 * b + 4)
                sp.dma_start(out[b].rearrange("(n p) f -> p n f", p=128),
                             arena[:, b * 512:(b + 1) * 512].rearrange("p (n f) -> p n f", f=DIM)
                             ).then_inc(stored, 16)
            sp.wait_ge(stored, 16 * BATCH)

        N_LOADS = 16 * len(LOADS)

        @block.tensor
        def _(pe):
            mm, tr = nc.tensor.matmul, nc.tensor.transpose

            def qkv(t):
                (L, b, j), n = t, num(t)
                pe.wait_ge(h_ready, n + 1)
                if not (isinstance(b, int) and n == 0):
                    pe.wait_ge(qn_done, n)
                    pe.wait_ge(v_ready, n)
                h = h_in[:, j % 2, :]
                mm(qk_ps[:, 0:512], h, wqkv_s[:, L % 2, 0:512], start=True, stop=True)
                mm(qk_ps[:, 512:1024], h, wqkv_s[:, L % 2, 512:1024], start=True, stop=True)
                mm(v_ps, h, wqkv_s[:, L % 2, 1024:1536], start=True, stop=True).then_inc(qkv_done, 1)

            def qk_transposes(t):
                (L, b, j), n = t, num(t)
                pe.wait_ge(qr_done, n + 1)
                if not (isinstance(b, int) and n < 2):
                    pe.wait_ge(pta_done, n - 1)
                    pe.wait_ge(ptd_done, n - 1)
                for i in range(8):
                    last = tr(tr_ps[:, i * 128:(i + 1) * 128], qr[:, j % 2, i * 128:(i + 1) * 128], ident)
                last.then_inc(qktr_done, 1)

            def scores(t):
                (L, b, j), n = t, num(t)
                k = j % 2
                if not (isinstance(b, int) and n == 0):
                    pe.wait_ge(exp_done, n)
                for c in range(2):
                    m = (mask_inner if j else mask_start).rearrange("p (o n) -> p o n", o=1)
                    mm(sc_ps[:, c * 512:(c + 1) * 512].rearrange("p (h n) -> p h n", h=4), identb,
                       m.broadcast_to((128, 4, 128)), start=True, stop=False)
                    if c == 0:
                        pe.wait_ge(qzhi_done, n + 1)
                        pe.wait_ge(qzlo_done, n + 1)
                        pe.wait_ge(kt_done, n + 1)
                    for h in range(4 * c, 4 * c + 4):
                        o = sc_ps[:, h * 128:(h + 1) * 128]
                        keys = kT[:, k, h // 2, :]
                        base = keys.offset
                        step = (1 - 2 * k) * 512 + 64
                        split = bass.AP(keys.tensor, base, [list(keys.ap[0]), [step, 2], [1, 64]])
                        mm(o[0:64].rearrange("p (a c) -> p a c", a=2), qz[:, h, 0:64], split,
                           start=False, stop=h % 4 == 3)
                        last = mm(o[64:128], qz[:, h, 64:128], keys, start=False, stop=h % 4 == 3)
                last.then_inc(sc_done, 1)

            def p_transposes(t, newer, behind):
                n = num(t)
                pe.wait_ge(pn_done, n + 1)
                if newer is not None:
                    m = num(newer)
                    pe.wait_ge(qzhi_done, m + 1)
                    pe.wait_ge(qzlo_done, m + 1)
                    pe.wait_ge(kt_done, m + 1)
                if t[2] == 1 and behind is not None:
                    pe.wait_ge(y_ready, y_after(behind[0], behind[1]))
                for h in range(HEADS):
                    last = tr(tr_ps[:, h * 128:(h + 1) * 128], p_s[:, t[2] % 2, h, :], ident)
                last.then_inc(pttr_done, 1)

            def pv(t):
                (L, b, j), n = t, num(t)
                pe.wait_ge(pta_done, n + 1)
                pe.wait_ge(ptd_done, n + 1)
                pe.wait_ge(v_ready, n + 1)
                pe.wait_ge(vm_done, n + 1)
                if not (isinstance(b, int) and n == 0):
                    pe.wait_ge(z_done, n)
                for w in range(2):
                    for h in range(HEADS):
                        r, c = 64 * (h % 2), (h // 2) * 128 + 64 * w
                        val = v_s if w else vm
                        last = mm(o_ps[r:r + 64, c:c + 64], val[:, j, h * 64:(h + 1) * 64],
                                  pT[:, h, 64 * w:64 * w + 64], start=True, stop=True)
                last.then_inc(pv_done, 1)

            def project(t):
                L, n = t[0], num(t)
                pe.wait_ge(oev_done, n + 1)
                for k in range(4):
                    last = mm(o_ps[:, 0:128], wo_s[:, L % 2, k, :], oT[:, k, :], start=k == 0, stop=k == 3)
                last.then_inc(wo_done, 1)

            def mlp_centre(t):
                L, b, _ = t
                pe.wait_ge(z_done, num(t) + 1)
                mm(o_ps, centre, zT[:, b, 0:SEQ], start=True, stop=True).then_inc(cen_done, 1)

            def mlp_variance(t):
                q = norm_index(t[0], t[1])
                pe.wait_ge(csq_done, q + 1)
                mm(o_ps, mean, nsq[:, 0, :], start=True, stop=True).then_inc(var_done, 1)
                pe.wait_ge(lnr_done, q + 1)

            def mlp(t, newest, live):
                L, b, _ = t
                q, nq, l = norm_index(L, b), 4 * L + b, L % 2
                g_ps, a_ps = (PS[:, 3, :], PS[:, 4, :], PS[:, 7, :]), (PS[:, 0, :], PS[:, 1, :], PS[:, 2, :])
                pe.wait_ge(hn_done, q + 1)
                for m in range(3):
                    if m == 0:
                        pe.wait_ge(exp_done, newest - 1 if live else newest + 1)
                    if m == 2:
                        pe.wait_ge(z_done, newest - 2 if live else newest + 1)
                    o = HID + HO[m]
                    mm(g_ps[m][0:HB[m]], w1_s[:, l, o:o + HB[m]], hn[:, :], start=True,
                       stop=True).then_inc(g_done, 1)
                for m in range(3):
                    if m == 0:
                        pe.wait_ge(qn_done, newest + 1)
                        pe.wait_ge(v_ready, newest + 1)
                    mm(a_ps[m][0:HB[m]], w1_s[:, l, HO[m]:HO[m] + HB[m]], hn[:, :], start=True,
                       stop=True).then_inc(a_done, 1)
                for evicted in (qzhi_done, qzlo_done, kt_done):
                    pe.wait_ge(evicted, newest if live else newest + 1)
                for m in range(3):
                    pe.wait_ge(u_done, 3 * nq + m + 1)
                    last = mm(PS[:, 5, :], w2_s[0:HB[m], l, m, :], u_s[0:HB[m], m, :],
                              start=m == 0, stop=m == 2)
                last.then_inc(w2_done, 1)

            def step(L, b, j, live=True):
                t0, t1, t2, t3, t4 = stages(L, b, j, live)
                mlp_due = t4 is not None and j == 3
                if t2 is not None:
                    scores(t2)
                if mlp_due:
                    mlp_centre(t4)
                if t3 is not None:
                    p_transposes(t3, t2, tile(L, b, j, 5) if j == 0 else None)
                if t0 is not None:
                    qkv(t0)
                if mlp_due:
                    mlp_variance(t4)
                if t3 is not None:
                    pv(t3)
                if t1 is not None:
                    qk_transposes(t1)
                if t3 is not None:
                    project(t3)
                if mlp_due:
                    mlp(t4, num(t0 if live else t4), live)

            def layers(block_no):
                for L in (2 * block_no, 2 * block_no + 1):
                    for j in range(4):
                        step(L, 0, j)
                    with pe.Fori(1, BATCH) as b:
                        for j in range(4):
                            step(L, b, j)
                for j in range(4):
                    step(L, BATCH, j, live=False)

            def norms(base, wait_x):
                for b in range(BATCH):
                    pe.wait_ge(x_ready, wait_x + b)
                    mm(PS[:, b, :], centre, xT[:, b, :], start=True, stop=True).then_inc(cen_done, 1)
                for b in range(BATCH):
                    pe.wait_ge(csq_done, base + b + 1)
                    mm(PS[:, 4 + b, :], mean, nsq[:, b, :], start=True, stop=True).then_inc(var_done, 1)

            pe.wait_ge(loaded, N_LOADS)
            for i in range(16):
                if i >= 8:
                    pe.wait_ge(xt_done, i // 4 - 1)
                last = tr(PS[:, (i // 4) % 2, (i % 4) * 128:(i % 4) * 128 + 128], xin[:, i, :], ident)
                if i % 4 == 3:
                    last.then_inc(xt_ps, 1)
            for i in range(4):
                last = tr(PS[:, 2, i * 128:(i + 1) * 128], wa[:, i, :], ident)
            last.then_inc(w_ps, 1)
            for l in range(LAYERS):
                for a in range(2):
                    for m in range(3):
                        i = (l * 2 + a) * 3 + m
                        o = a * HID + HO[m]
                        mm(PS[0:HB[m], 3, i:i + 1], w1_s[:, l, o:o + HB[m]], g_s[:, l, 1:2],
                           start=True, stop=True)
            pe.wait_ge(w_done, 1)
            mm(PS[:, 3, 12:13], wpT[:, :], bvp[:, 0:1], start=True, stop=True).then_inc(bias_ps, 1)
            pe.wait_ge(scaled, 1)
            norms(0, 1)
            pe.wait_ge(hn_done, 4)
            layers(0)

            def bank7(what, n):
                i = USES.index((what, n))
                if i:
                    pe.wait_ge(*freed(*USES[i - 1]))

            def slot(what, n):
                bank, b, g, k = PS[:, 7, :], n // 4, n % 4, n % 2
                bank7(what, n)
                if what == "centre":
                    pe.wait_ge(x_ready, 5 + n)
                    mm(bank, centre, xT[:, n, :], start=True, stop=True).then_inc(cen_done, 1)
                if what == "variance":
                    pe.wait_ge(csq_done, MID_NORM + n + 1)
                    mm(bank, mean, nsq[:, 0, :], start=True, stop=True).then_inc(var_done, 1)
                if what == "q":
                    pe.wait_ge(hn_done, MID_NORM + n + 1)
                    mm(bank, wqkT[:, 0, :], hn[:, :], start=True, stop=True).then_inc(m_qk, 1)
                if what == "k":
                    mm(bank, wqkT[:, 1, :], hn[:, :], start=True, stop=True).then_inc(m_qk, 1)
                if what == "v":
                    for i in range(TILES):
                        last = mm(bank[:, i * 128:(i + 1) * 128], hn[:, i * 128:(i + 1) * 128],
                                  wqkT[:, 2, :], start=True, stop=True)
                    last.then_inc(m_v, 1)
                if what == "max":
                    pe.wait_ge(m_max, 10 * (n + 1))
                    tr(bank[0:16, 0:128], mx[:, g, :], ident).then_inc(m_t, 1)
                if what == "pv":
                    pe.wait_ge(m_exp, 6 * (n + 1))
                    pe.wait_ge(m_vp, b + 1)
                    for kt in range(TILES):
                        for j in range(4):
                            col = {0: 0, 1: 512, 3: 896, 2: 1024}[kt]
                            row = 2 * ((2 * n + j // 2) % 3) + j % 2
                            last = mm(bank[32 * j:32 * j + 32, 128 * kt:SEQ], vp[:, b % 2, kt, 4 * g + j, :],
                                      pe_s[:, row, col:col + SEQ - 128 * kt],
                                      start=kt == 0, stop=kt == TILES - 1, tile_position=(0, 32 * j))
                    last.then_inc(m_pv, 1)
                if what == "o":
                    for i in range(TILES):
                        last = tr(bank[:, i * 128:(i + 1) * 128], osb[:, i * 128:(i + 1) * 128], ident)
                    last.then_inc(m_ot, 1)
                if what == "y":
                    pe.wait_ge(m_yt, 4 * (n + 1))
                    for i in range(TILES):
                        last = tr(bank[:, i * 128:(i + 1) * 128], ytok[:, i, :], ident)
                    last.then_inc(m_ytt, 1)
                if what == "project":
                    mm(bank, wpT[:, :], yaT[:, :], start=True, stop=True).then_inc(m_pr, 1)

            def s_unit(n, i):
                u, k = 5 * n + i, (n // 8) % 2
                if i == 0 and n % 8 == 0:
                    pe.wait_ge(m_stk, 16 * 13 * (n // 8 + 1))
                if u >= 2:
                    pe.wait_ge(m_max, u - 1)
                for col, h, qt in s_units(n)[i]:
                    w = 128 * (qt + 1)
                    o = PS[:, 5 + u % 2, col:col + w]
                    mm(o, qstb[0:96, k, h, 128 * qt:128 * qt + 128], kstb[0:96, k, h, 0:w],
                       start=True, stop=False)
                    last = mm(o[:, w - 128:w], identb, mask_qk, start=False, stop=True)
                last.then_inc(m_s, 1)

            def st_unit(n, i):
                k = (n // 8) % 2
                if i == 0 and n % 2 == 0:
                    pe.wait_ge(max_stacked[n // 2 % 4], 16 * (n // 8 + 1))
                if n:
                    pe.wait_ge(m_exp, 3 * (n - 1) + i + 1)
                for bank, col, h, kt in st_units(n)[i]:
                    w = SEQ - 128 * kt
                    mm(PS[:, bank, col:col + w], kstb[0:96, k, h, 128 * kt:128 * kt + 128],
                       qstb[0:96, k, h, 128 * kt:SEQ], start=True, stop=False)
                    last = mm(PS[:, bank, col:col + 128], identb, mask_kq, start=False, stop=True)
                last.then_inc(m_st, 1)

            for w in PREPARE:
                slot(*w)
            for r in range(ROUNDS):
                work = slots(r)
                for i in range(5):
                    if r < PAIRS:
                        s_unit(r, i)
                    if i < 3 and LAG <= r < PAIRS + LAG:
                        st_unit(r - LAG, i)
                    if i < 3 and work[i] is not None:
                        slot(*work[i])

            norms(SECOND_NORM, 9)
            pe.wait_ge(hn_done, SECOND_NORM + 4)
            layers(1)
            for i in range(16):
                pe.wait_ge(x_ready, 12 + i // 4 + 1)
                if i >= 2:
                    pe.wait_ge(out_sb, i - 1)
                tr(PS[:, i % 2, 0:128], xT[:, i // 4, (i % 4) * 128:(i % 4) * 128 + 128], ident).then_inc(
                    out_ps, 1)

        @block.scalar
        def _(act):
            A = nc.scalar.activation
            nc.scalar.preload_act_table_set("natural_log_exp_and_others")

            def squares(t):
                n = num(t)
                act.wait_ge(qkv_done, n + 1)
                if not isinstance(t[1], int) or n:
                    act.wait_ge(ss_done, n)
                A(sq, qk_ps, ACT.Square).then_inc(sq_done, 1)

            def v_evict(t):
                n = num(t)
                if not isinstance(t[1], int) or n >= 4:
                    act.wait_ge(pv_done, n - 3)
                    act.wait_ge(vm_done, n - 2)
                A(v_s[:, t[2], :], v_ps, ACT.Copy).then_inc(v_ready, 1)

            def norms_of_heads(t):
                n = num(t)
                act.wait_ge(ssc_done, n + 1)
                A(nrm[:, 2, :], nrm[:, 1, :], ACT.Ln, scale=65536.0).then_inc(lnq_done, 1)
                act.wait_ge(lnq_done, n + 1)
                if not isinstance(t[1], int) or n:
                    act.wait_ge(qn_done, n)
                A(rn, nrm[:, 2, :], ACT.Exp, scale=-0.5).then_inc(r_done, 1)

            def k_evict(t):
                n = num(t)
                act.wait_ge(qktr_done, n + 1)
                if late(t, 1):
                    act.wait_ge(sc_done, n)
                A(kT[:, t[2] % 2, :, :], tr_ps[:, 512:1024].rearrange("p (h n) -> p h n", h=4),
                  ACT.Copy).then_inc(kt_done, 1)

            def q_upper(t):
                n = num(t)
                act.wait_ge(qktr_done, n + 1)
                if not isinstance(t[1], int) or n:
                    act.wait_ge(sc_done, n)
                A(qz[64:128, 1::2, :], tr_ps[64:128, 0:512].rearrange("p (h n) -> p h n", h=4),
                  ACT.Copy).then_inc(qzhi_done, 1)

            def softmax(t):
                (L, b, j), n = t, num(t)
                k = j % 2
                act.wait_ge(max_done, n + 1)
                if not isinstance(b, int) or n >= 2:
                    act.wait_ge(pttr_done, n - 1)
                    act.wait_ge(rden_done, n - 1)
                for h in range(HEADS):
                    last = A(p_s[:, k, h, :], sc_ps[:, h * 128:(h + 1) * 128], ACT.Exp,
                             bias=nmax[:, k, h:h + 1], accum_out=den[:, k, h:h + 1])
                last.then_inc(exp_done, 1)

            def pt_evict(t):
                n = num(t)
                act.wait_ge(pttr_done, n + 1)
                if not isinstance(t[1], int) or n:
                    act.wait_ge(pv_done, n)
                A(pT[:, 0:4, :], tr_ps[:, 0:512].rearrange("p (h n) -> p h n", h=4),
                  ACT.Copy).then_inc(pta_done, 1)

            def o_evict(t):
                n = num(t)
                act.wait_ge(pv_done, n + 1)
                if not isinstance(t[1], int) or n:
                    act.wait_ge(wo_done, n)
                A(oT, o_ps.rearrange("p (k n) -> p k n", k=4), ACT.Copy).then_inc(oev_done, 1)

            def log_deviation(q, src, k):
                act.wait_ge(var_done, q + 1)
                if not isinstance(q, int) or q:
                    act.wait_ge(hn_done, q - k)
                A(rstd[:, k, :], src, ACT.Ln, bias=cc[:, 0:1]).then_inc(lnr_done, 1)

            def inverse_deviation(q, k):
                act.wait_ge(lnr_done, q + 1)
                A(rstd[:, k, :], rstd[:, k, :], ACT.Exp, scale=-0.5).then_inc(rstd_done, 1)

            def norms(base):
                for b in range(BATCH):
                    act.wait_ge(cen_done, base + b + 1)
                    A(nsq[:, b, :], PS[:, b, :], ACT.Square).then_inc(csq_done, 1)
                for b in range(BATCH):
                    log_deviation(base + b, PS[:, 4 + b, :], b)
                for b in range(BATCH):
                    inverse_deviation(base + b, b)

            def mlp_squares(t):
                q = norm_index(t[0], t[1])
                act.wait_ge(hc_done, 4 * t[0] + t[1] + 1)
                A(nsq[:, 0, :], hc[:, :], ACT.Square).then_inc(csq_done, 1)

            def mlp(t):
                L, b, _ = t
                nq = 4 * L + b
                for m in range(3):
                    act.wait_ge(g_done, 3 * nq + m + 1)
                    if not (isinstance(nq, int) and nq == 0):
                        act.wait_ge(w2_done, nq)
                    A(u_s[0:HB[m], m, :], PS[0:HB[m], (3, 4, 7)[m], :], ACT.Gelu,
                      bias=b1_s[0:HB[m], L % 2, 1, m:m + 1]).then_inc(gl_done, 1)
                nc.scalar.preload_act_table_set("natural_log_exp_and_others")

            def step(L, b, j, live=True):
                t0, t1, t2, t3, t4 = stages(L, b, j, live)
                mlp_due = t4 is not None and j == 3
                if mlp_due:
                    mlp_squares(t4)
                if t3 is not None:
                    pt_evict(t3)
                if t2 is not None:
                    softmax(t2)
                if t0 is not None:
                    squares(t0)
                if mlp_due:
                    q = norm_index(t4[0], t4[1])
                    log_deviation(q, o_ps, 0)
                    inverse_deviation(q, 0)
                if t3 is not None:
                    o_evict(t3)
                if t1 is not None:
                    k_evict(t1)
                if t0 is not None:
                    norms_of_heads(t0)
                if t1 is not None:
                    q_upper(t1)
                if t0 is not None:
                    v_evict(t0)
                if mlp_due:
                    mlp(t4)

            def layers(block_no):
                for L in (2 * block_no, 2 * block_no + 1):
                    for j in range(4):
                        step(L, 0, j)
                    with act.Fori(1, BATCH) as b:
                        for j in range(4):
                            step(L, b, j)
                for j in range(4):
                    step(L, BATCH, j, live=False)

            act.wait_ge(zeroed, 1)
            norms(0)
            layers(0)

            def slot(what, n):
                bank = PS[:, 7, :]
                if what == "centre":
                    q = MID_NORM + n
                    act.wait_ge(cen_done, q + 1)
                    act.wait_ge(hn_done, q)
                    A(hc[:, :], bank, ACT.Copy).then_inc(m_hc, 1)
                    act.wait_ge(m_hc, n + 1)
                    A(nsq[:, 0, :], hc[:, :], ACT.Square).then_inc(csq_done, 1)
                if what == "variance":
                    log_deviation(MID_NORM + n, bank, 0)
                    inverse_deviation(MID_NORM + n, 0)
                if what == "v":
                    act.wait_ge(m_v, n + 1)
                    if n == 0:
                        act.wait_ge(zeroed, 2)
                    if n >= 2:
                        act.wait_ge(m_pv, 4 * (n - 1))
                    A(vp[:, n % 2, :, :, 0:HD], bank.rearrange("p (t h d) -> p t h d", t=TILES, h=NH),
                      ACT.Copy).then_inc(m_vp, 1)
                if what == "k":
                    act.wait_ge(m_f, 2 * n + 2)
                    if n:
                        act.wait_ge(m_sav, 48 * n)
                    A(partb[:, 0, :, :], qkf, ACT.Copy).then_inc(m_p1, 1)
                if what == "pv":
                    act.wait_ge(m_pv, n + 1)
                    A(osb, bank, ACT.Copy).then_inc(m_osb, 1)
                if what == "y":
                    act.wait_ge(m_ytt, n + 1)
                    A(yaT, bank, ACT.Copy).then_inc(m_ya, 1)

            def second_part(b):
                act.wait_ge(m_r1, b + 1)
                A(partb[:, 1, :, :], qkf, ACT.Copy).then_inc(m_p2, 1)

            def exp_unit(n, i):
                k = 2 * (n % 3)
                act.wait_ge(m_st, 3 * n + i + 1)
                if i == 0 and n >= 3:
                    act.wait_ge(m_pv, (n - 3) // 2 + 1)
                if i < 2:
                    A(pe_s[:, k + i, 0:1024], PS[:, 2 * i:2 * i + 2, :].rearrange("p a n -> p (a n)"),
                      ACT.Exp).then_inc(m_exp, 1)
                else:
                    A(pe_s[:, k:k + 2, 1024:1280], PS[:, 4, :].rearrange("p (a n) -> p a n", a=2),
                      ACT.Exp).then_inc(m_exp, 1)

            for w in PREPARE:
                slot(*w)
            second_part(0)
            for r in range(ROUNDS):
                work = slots(r)
                for i in range(3):
                    if LAG <= r < PAIRS + LAG:
                        exp_unit(r - LAG, i)
                    if work[i] is not None:
                        slot(*work[i])
                if r % 8 == 4 and r // 8 + 1 < BATCH:
                    second_part(r // 8 + 1)
            norms(SECOND_NORM)
            layers(1)

        @block.vector
        def _(dve):
            V = nc.vector

            def sum_squares(t):
                n = num(t)
                dve.wait_ge(sq_done, n + 1)
                V.reduce_sum(nrm[:, 0, :], sq.rearrange("p (g d) -> p g d", d=DH), AX).then_inc(ss_done, 1)
                dve.wait_ge(ss_done, n + 1)
                if not isinstance(t[1], int) or n:
                    dve.wait_ge(lnq_done, n)
                V.tensor_scalar(nrm[:, 1, :], nrm[:, 0, :], 1e-24, None, ALU.max).then_inc(ssc_done, 1)

            def copy_v(t):
                (L, b, j), n = t, num(t)
                dve.wait_ge(v_ready, n + 1)
                if not isinstance(b, int) or n >= 4:
                    dve.wait_ge(pv_done, n - 3)
                V.tensor_copy(vm[0:64, j, :], v_s[0:64, j, :])
                V.tensor_copy(vm[64:128, j, :], v_s[64:128, (j + 3) % 4, :]).then_inc(vm_done, 1)

            def normalise(t):
                n, k = num(t), t[2] % 2
                dve.wait_ge(r_done, n + 1)
                if not isinstance(t[1], int) or n >= 2:
                    dve.wait_ge(rots_done, n - 1)
                    dve.wait_ge(rotc_done, n - 1)
                V.tensor_tensor(qn[:, k, :].rearrange("p (g d) -> p g d", d=DH),
                                qk_ps.rearrange("p (g d) -> p g d", d=DH),
                                rn.rearrange("p (g o) -> p g o", o=1).broadcast_to((128, 16, DH)),
                                ALU.mult).then_inc(qn_done, 1)

            def rotate(t):
                (L, b, j), n = t, num(t)
                k = j % 2
                dve.wait_ge(qn_done, n + 1)
                if late(t, 2):
                    dve.wait_ge(qr_done, n - 1)
                V.tensor_tensor(rc[:, k, :].rearrange("p (c h d) -> p c h d", c=2, h=HEADS),
                                qn[:, k, :].rearrange("p (c h d) -> p c h d", c=2, h=HEADS),
                                cosT[:, L % 2, j, :, :].rearrange("p c (o d) -> p c o d", o=1)
                                .broadcast_to((128, 2, HEADS, DH)), ALU.mult).then_inc(rotc_done, 1)

            def q_lower(t):
                n = num(t)
                dve.wait_ge(qktr_done, n + 1)
                if not isinstance(t[1], int) or n:
                    dve.wait_ge(sc_done, n)
                V.tensor_copy(qz[0:64, 0::2, :],
                              tr_ps[0:64, 0:512].rearrange("p (h n) -> p h n", h=4)).then_inc(qzlo_done, 1)

            def row_max(t):
                n, k = num(t), t[2] % 2
                dve.wait_ge(sc_done, n + 1)
                if not isinstance(t[1], int) or n >= 2:
                    dve.wait_ge(exp_done, n - 1)
                V.reduce_max(nmax[:, k, :], sc_ps.rearrange("p (h n) -> p h n", h=HEADS), AX,
                             negate=True).then_inc(max_done, 1)

            def reciprocal(t):
                n, k = num(t), t[2] % 2
                dve.wait_ge(exp_done, n + 1)
                if not isinstance(t[1], int) or n >= 2:
                    dve.wait_ge(pn_done, n - 1)
                V.reciprocal(rden[:, k, :], den[:, k, :]).then_inc(rden_done, 1)

            def pt_evict(t):
                n = num(t)
                dve.wait_ge(pttr_done, n + 1)
                if not isinstance(t[1], int) or n:
                    dve.wait_ge(pv_done, n)
                V.tensor_copy(pT[:, 4:8, :],
                              tr_ps[:, 512:1024].rearrange("p (h n) -> p h n", h=4)).then_inc(ptd_done, 1)

            def residual(t):
                (L, b, j), n = t, num(t)
                dve.wait_ge(wo_done, n + 1)
                lo, up = slice(128 * j, 128 * j + 128), slice(128 * j + 1, 128 * j + 129)
                V.tensor_tensor(zT[0:64, b, lo], o_ps[0:64, 0:128], yT[0:64, b, lo], ALU.add)
                V.tensor_tensor(zT[64:128, b, up], o_ps[64:128, 0:128], yT[64:128, b, up],
                                ALU.add).then_inc(z_done, 1)

            def mlp_copy(t):
                nq = 4 * t[0] + t[1]
                q = norm_index(t[0], t[1])
                dve.wait_ge(cen_done, q + 1)
                V.tensor_copy(hc[:, :], o_ps).then_inc(hc_done, 1)

            def mlp_norm(t):
                q = norm_index(t[0], t[1])
                dve.wait_ge(rstd_done, q + 1)
                V.tensor_tensor(hn[:, :], hc[:, :], rstd[:, 0, :], ALU.mult).then_inc(hn_done, 1)

            def mlp(t):
                L, b, _ = t
                nq, l = 4 * L + b, L % 2
                for m in range(3):
                    dve.wait_ge(a_done, 3 * nq + m + 1)
                    dve.wait_ge(gl_done, 3 * nq + m + 1)
                    V.scalar_tensor_tensor(u_s[0:HB[m], m, :], PS[0:HB[m], m, :],
                                           b1_s[0:HB[m], l, 0, m:m + 1], u_s[0:HB[m], m, :],
                                           ALU.add, ALU.mult).then_inc(u_done, 1)
                dve.wait_ge(w2_done, nq + 1)
                V.scalar_tensor_tensor(yT[0:64, b, 0:SEQ], PS[0:64, 5, :], b2_s[0:64, l:l + 1],
                                       zT[0:64, b, 0:SEQ], ALU.add, ALU.add)
                V.scalar_tensor_tensor(yT[64:128, b, 1:SEQ + 1], PS[64:128, 5, :], b2_s[64:128, l:l + 1],
                                       zT[64:128, b, 1:SEQ + 1], ALU.add, ALU.add).then_inc(y_ready, 1)

            def step(L, b, j, live=True):
                t0, t1, t2, t3, t4 = stages(L, b, j, live)
                mlp_due = t4 is not None and j == 3
                if t2 is not None:
                    row_max(t2)
                if mlp_due:
                    mlp_copy(t4)
                if t3 is not None:
                    pt_evict(t3)
                if t1 is not None:
                    copy_v(t1)
                if t2 is not None:
                    reciprocal(t2)
                if t0 is not None:
                    sum_squares(t0)
                if t1 is not None:
                    q_lower(t1)
                if t0 is not None:
                    normalise(t0)
                if t3 is not None:
                    residual(t3)
                if mlp_due:
                    mlp_norm(t4)
                if t0 is not None:
                    rotate(t0)
                if mlp_due:
                    mlp(t4)

            def layers(block_no):
                for L in (2 * block_no, 2 * block_no + 1):
                    for j in range(4):
                        step(L, 0, j)
                    with dve.Fori(1, BATCH) as b:
                        for j in range(4):
                            step(L, b, j)
                for j in range(4):
                    step(L, BATCH, j, live=False)

            def block_norm(q, b):
                dve.wait_ge(rstd_done, q + 1)
                V.tensor_tensor(yT[0:64, b, 0:SEQ], PS[0:64, b, :], rstd[0:64, b, :], ALU.mult)
                V.tensor_tensor(yT[64:128, b, 1:SEQ + 1], PS[64:128, b, :], rstd[64:128, b, :],
                                ALU.mult).then_inc(hn_done, 1)
                dve.wait_ge(hn_done, q + 1)
                V.engine_nop().then_inc(y_ready, 1)

            def add_half(b, k):
                dve.wait_ge(y_ready, 12 * (k + 1))
                V.scalar_tensor_tensor(xT[0:64, b, :], yT[0:64, b, 0:SEQ], 0.5, xT[0:64, b, :],
                                       ALU.mult, ALU.add)
                V.scalar_tensor_tensor(xT[64:128, b, :], yT[64:128, b, 1:SEQ + 1], 0.5, xT[64:128, b, :],
                                       ALU.mult, ALU.add).then_inc(x_ready, 1)

            V.memset(cc[:, 0:1], 1e-5)
            for b in range(BATCH):
                V.memset(yT[64:128, b, 0:1], 0.0)
                V.memset(zT[64:128, b, 0:1], 0.0)
            dve.wait_ge(loaded, N_LOADS)
            V.tensor_copy(cb[:, 0, :], ident)
            V.tensor_copy(cb[:, 1:5, :], CS[:, 0:512].rearrange("p (i n) -> p i n", i=4))
            for b in range(BATCH):
                dve.wait_ge(xt_ps, b + 1)
                V.tensor_copy(xT[:, b, :], PS[:, b % 2, :]).then_inc(xt_done, 1)
            dve.wait_ge(w_ps, 1)
            for c in range(2):
                V.tensor_copy(wqkT[:, c, :].rearrange("p (d h) -> p h d", d=HD),
                              PS[:, 2, c * 128:(c + 1) * 128].rearrange("p (h d) -> p h d", d=HD))
            V.tensor_copy(wqkT[:, 2, :], PS[:, 2, 256:384])
            V.tensor_copy(wpT[:, :], PS[:, 2, 384:512]).then_inc(w_done, 1)
            dve.wait_ge(bias_ps, 1)
            dve.wait_ge(xt_done, 4)
            for l in range(LAYERS):
                for a in range(2):
                    for m in range(3):
                        i = (l * 2 + a) * 3 + m
                        r = slice(0, HB[m])
                        V.tensor_tensor(b1_s[r, l, a, m:m + 1], b1_s[r, l, a, m:m + 1],
                                        PS[r, 3, i:i + 1], ALU.add)
            V.tensor_tensor(bvp[:, 2:3], bvp[:, 1:2], PS[:, 3, 12:13], ALU.add)
            for l in range(LAYERS):
                V.tensor_scalar(w1_s[:, l, :], w1_s[:, l, :], g_s[:, l, 0:1], None, ALU.mult)
                for j in range(TILES):
                    V.tensor_tensor(cosT[:, l, j, :, :],
                                    CS[:, C_COS - C_KEPT + 128 * j:C_COS - C_KEPT + 128 * j + 128].rearrange("p (c d) -> p c d", c=2),
                                    qks[:, l, :, :], ALU.mult)
                    for half in range(2):
                        d, e = slice(32 * half, 32 * half + 32), slice(32 - 32 * half, 64 - 32 * half)
                        V.tensor_tensor(sinT[:, l, j, :, d],
                                        CS[:, C_SIN - C_KEPT + 128 * j:C_SIN - C_KEPT + 128 * j + 128].rearrange(
                                            "p (c d) -> p c d", c=2)[:, :, d],
                                        qks[:, l, :, e], ALU.mult)
            for i in range(4):
                V.engine_nop().then_inc(x_ready, 1)
            V.memset(qz, 0.0)
            V.memset(kT, 0.0)
            V.memset(v_s[:, 3, :], 0.0).then_inc(scaled, 1)
            V.engine_nop().then_inc(zeroed, 1)
            for b in range(BATCH):
                block_norm(b, b)
            layers(0)
            for b in range(BATCH):
                add_half(b, 0)

            def slot(what, n):
                bank, g = PS[:, 7, :], n % 4
                if what == "variance":
                    q = MID_NORM + n
                    dve.wait_ge(rstd_done, q + 1)
                    if n:
                        dve.wait_ge(m_v, n)
                    V.tensor_tensor(hn[:, :], hc[:, :], rstd[:, 0, :], ALU.mult).then_inc(hn_done, 1)
                if what in ("q", "k"):
                    c = 0 if what == "q" else 1
                    dve.wait_ge(m_qk, 2 * n + c + 1)
                    if n:
                        dve.wait_ge(m_p3, n)
                    V.scalar_tensor_tensor(qkf[:, c, :], bank, bqk[:, c:c + 1],
                                           C[:, C_F + c * SEQ:C_F + (c + 1) * SEQ], ALU.add,
                                           ALU.mult).then_inc(m_f, 1)
                if what == "max":
                    t = bank[0:16, 0:128]
                    dve.wait_ge(m_t, n + 1)
                    if n:
                        dve.wait_ge(m_msav, 16 * n)
                    V.tensor_scalar(mpartb[0:16, 0, :], t, -1.0, None, ALU.mult).then_inc(m_m1, 1)
                    dve.wait_ge(m_m1, n + 1)
                    V.scalar_tensor_tensor(mres[0:16, :], t, -1.0, mpartb[0:16, 0, :], ALU.mult,
                                           ALU.subtract).then_inc(m_m2, 1)
                    dve.wait_ge(m_m2, n + 1)
                    V.tensor_copy(mpartb[0:16, 1, :], mres[0:16, :]).then_inc(m_m3, 1)
                    dve.wait_ge(m_m3, n + 1)
                    V.tensor_tensor(mpartb[0:16, 2, :], mres[0:16, :], mpartb[0:16, 1, :],
                                    ALU.subtract).then_inc(m_m4, 1)
                if what == "o":
                    dve.wait_ge(m_ot, n + 1)
                    o = bank.rearrange("p (q j e) -> p q j e", q=TILES, j=4)
                    r4 = rec.rearrange("p q (j o) -> p q j o", o=1)
                    if n:
                        dve.wait_ge(m_yt, n)
                    V.reciprocal(r4, o[:, :, :, HD:HD + 1]).then_inc(m_rec, 1)
                    dve.wait_ge(m_rec, n + 1)
                    if g == 0 and n:
                        dve.wait_ge(m_ytt, n // 4)
                    V.tensor_tensor(ytok[:, :, 32 * g:32 * g + 32].rearrange("p q (j e) -> p q j e", j=4),
                                    o[:, :, :, 0:HD], r4.broadcast_to((128, TILES, 4, HD)),
                                    ALU.mult).then_inc(m_yt, 1)
                if what == "project":
                    dve.wait_ge(m_pr, n + 1)
                    V.scalar_tensor_tensor(xT[:, n, :], bank, bvp[:, 2:3], xT[:, n, :],
                                           ALU.add, ALU.add).then_inc(x_ready, 1)

            def max_unit(n, i):
                u, g, c = 5 * n + i, n // 2 % 4, 8 * (n % 2)
                bank, m = PS[:, 5 + u % 2, :], mx[:, g, :]
                dve.wait_ge(m_s, u + 1)
                if i == 0 and n >= 8:
                    dve.wait_ge(m_t, n // 2 - 3)
                if i in (0, 2):
                    o = c + 4 * (i // 2) + 3
                    last = V.reduce_max(m[:, o:o + 1], bank, AX)
                elif i in (1, 3):
                    o = c + 4 * (i // 2)
                    V.reduce_max(m[:, o + 2:o + 3], bank[:, 0:384], AX)
                    last = V.reduce_max(m[:, o:o + 1], bank[:, 384:512], AX)
                else:
                    last = V.reduce_max(m[:, c + 1:c + 6:4], bank.rearrange("p (a n) -> p a n", a=2), AX)
                last.then_inc(m_max, 1)

            for k in range(2):
                V.memset(qst[64:96, k, :], 0.0)
                V.memset(kstb[64:96, k, :, :], 1.0)
                V.memset(vp[:, k, :, :, HD + 1:32], 0.0)
                last = V.memset(vp[:, k, :, :, HD:HD + 1], 1.0)
            last.then_inc(zeroed, 1)
            for w in PREPARE:
                slot(*w)
            for r in range(ROUNDS):
                work = slots(r)
                for i in range(5):
                    if r < PAIRS:
                        max_unit(r, i)
                    if i < 3 and work[i] is not None and work[i][0] != "o":
                        slot(*work[i])
                if work[2] is not None and work[2][0] == "o":
                    slot(*work[2])

            V.memset(qz, 0.0)
            V.memset(kT, 0.0)
            V.memset(v_s[:, 3, :], 0.0).then_inc(zeroed, 1)
            for b in range(BATCH):
                block_norm(SECOND_NORM + b, b)
            layers(1)
            for b in range(BATCH):
                add_half(b, 1)
            for i in range(16):
                dve.wait_ge(out_ps, i + 1)
                V.tensor_copy(arena[:, i * 128:(i + 1) * 128], PS[:, i % 2, 0:128]).then_inc(out_sb, 1)

        @block.gpsimd
        def _(pool):
            P = nc.gpsimd

            def shifted_input(t):
                (L, b, j), n = t, num(t)
                pool.wait_ge(y_ready, y_count(L, b))
                if not isinstance(b, int) or n >= 2:
                    pool.wait_ge(qkv_done, n - 1)
                P.tensor_copy(h_in[:, j % 2, :], yT[:, b, 128 * j:128 * j + 128]).then_inc(h_ready, 1)

            def sine_part(t):
                (L, b, j), n = t, num(t)
                k = j % 2
                pool.wait_ge(qn_done, n + 1)
                if late(t, 2):
                    pool.wait_ge(qr_done, n - 1)
                for c in range(2):
                    src = qn[:, k, 512 * c:512 * c + 512]
                    base = src.offset
                    swapped = bass.AP(src.tensor, base + 32, [list(src.ap[0]), [64, HEADS], [-32, 2], [1, 32]])
                    last = P.tensor_tensor(
                        rs[:, k, 512 * c:512 * c + 512].rearrange("p (h a d) -> p h a d", h=HEADS, a=2),
                        swapped,
                        sinT[:, L % 2, j, c, :].rearrange("p (o a d) -> p o a d", o=1, a=2)
                        .broadcast_to((128, HEADS, 2, 32)), ALU.mult)
                last.then_inc(rots_done, 1)

            def rotated(t):
                n, k = num(t), t[2] % 2
                pool.wait_ge(rotc_done, n + 1)
                pool.wait_ge(rots_done, n + 1)
                if late(t, 2):
                    pool.wait_ge(qktr_done, n - 1)
                P.tensor_tensor(qr[:, k, :], rc[:, k, :], rs[:, k, :], ALU.add).then_inc(qr_done, 1)

            def normalise(t):
                n, k = num(t), t[2] % 2
                pool.wait_ge(rden_done, n + 1)
                P.tensor_tensor(p_s[:, k, :, :], p_s[:, k, :, :],
                                rden[:, k, :].rearrange("p (h o) -> p h o", o=1).broadcast_to((128, HEADS, 128)),
                                ALU.mult).then_inc(pn_done, 1)

            def step(L, b, j, live=True):
                t0, t1, t2, t3, t4 = stages(L, b, j, live)
                if t0 is not None:
                    shifted_input(t0)
                if t1 is not None:
                    sine_part(t1)
                    rotated(t1)
                if t2 is not None:
                    normalise(t2)

            def layers(block_no):
                for L in (2 * block_no, 2 * block_no + 1):
                    for j in range(4):
                        step(L, 0, j)
                    with pool.Fori(1, BATCH) as b:
                        for j in range(4):
                            step(L, b, j)
                for j in range(4):
                    step(L, BATCH, j, live=False)

            pool.wait_ge(zeroed, 1)
            layers(0)

            def parts(b):
                k = b % 2
                pool.wait_ge(m_p1, b + 1)
                P.tensor_tensor(qkf, qkf, partb[:, 0, :, :], ALU.subtract).then_inc(m_r1, 1)
                pool.wait_ge(m_p2, b + 1)
                P.tensor_tensor(partb[:, 2, :, :], qkf, partb[:, 1, :, :], ALU.subtract).then_inc(m_p3, 1)
                pool.wait_ge(m_p3, b + 1)
                for i in range(3):
                    pool.dma_start(scr[i], partb[:, i, :, :]).then_inc(m_sav, 16)
                pool.wait_ge(m_sav, 48 * (b + 1))
                pool.wait_ge(zeroed, 2)
                if b >= 2:
                    pool.wait_ge(m_st, 24 * (b - 1))
                v = scr.rearrange("i (d h) c t -> (i d) c h t", h=NH)
                for i in range(3):
                    pool.dma_start(kstb[24 * i:24 * i + 24, k, :, :], v[:, 1, :, :]).then_inc(m_stk, 16)
                    for j in range(3):
                        r = 24 * i + 8 * j
                        pool.dma_start(qstb[r:r + 8, k, :, :], v[8 * i:8 * i + 8, 0, :, :]).then_inc(m_stk, 16)
                pool.dma_start(qstb[72:75, k, :, :], qstb[76:79, k, :, :]).then_inc(m_stk, 16)

            for b in range(BATCH):
                parts(b)
            pool.wait_ge(zeroed, 3)
            layers(1)


_INS = ['L0_attn_x', 'L0_attn_W_attn', 'L0_attn_b_attn', 'L0_attn_W_proj', 'L0_attn_b_proj',
        'L0_ffn_wqkv', 'L0_ffn_q_scale', 'L0_ffn_k_scale', 'L0_ffn_wo', 'L0_ffn_ln_g', 'L0_ffn_ln_b',
        'L0_ffn_w1', 'L0_ffn_b1', 'L0_ffn_w2', 'L0_ffn_b2']


def kernel(**inputs):
    import numpy as _np
    import concourse.bacc as _bacc
    from concourse import mybir as _mybir
    from concourse.bass_utils import run_bass_kernel_spmd as _run

    nc = _bacc.Bacc("TRN2", target_bir_lowering=False, num_devices=1)
    arrays, args = {}, []
    for name in _INS:
        a = _np.ascontiguousarray(inputs[name])
        arrays[f"in_{name}_dram"] = a
        args.append(nc.dram_tensor(f"in_{name}_dram", a.shape, _mybir.dt.from_np(a.dtype), kind="ExternalInput").ap())
    c = constants()
    arrays["constants_dram"] = c
    args.append(nc.dram_tensor("constants_dram", c.shape, _mybir.dt.float32, kind="ExternalInput").ap())
    args.append(nc.dram_tensor("out_0_dram", (BATCH, SEQ, DIM), _mybir.dt.float32, kind="ExternalOutput").ap())
    macaron(nc, *args)
    r = _run(nc, [arrays], core_ids=[0])
    return r.results[0]["out_0_dram"]
```

```python
import math
import concourse.bass as bass
from concourse import mybir
from contextlib import ExitStack

import numpy as np

BATCH, SEQ, DIM = 4, 512, 128
HEADS, DH, WIN = 8, 64, 64
INNER = HEADS * DH
LAYERS = 2
HID = int(DIM * 4 * 2 / 3)
TILES = SEQ // 128
HB = [114, 114, HID - 228]
HO = [0, 114, 228]
NH, HD = 16, DIM // 16
BIG = -1e30
ARENA = 27216

C_ID, C_CEN, C_ONE, C_F = 0, 128, 256, 384
C_KEPT = C_F + 2 * SEQ
C_MF, C_MS, C_CS, C_CT = (C_KEPT + 128 * i for i in range(4))
C_COS = C_KEPT + 512
C_SIN = C_COS + 2 * SEQ // 2
C_ALL = C_SIN + 2 * SEQ // 2


V_B1, V_B2, V_G, V_B, V_Q, V_V, V_P, V_O = 0, 12, 14, 16, 18, 20, 21, 22


def b1_column(l, a, m):
    return V_B1 + 4 * m + 2 * l + a


def constants():
    c = np.zeros((128, C_ALL), np.float32)
    i = np.arange(128)
    c[:, C_ID:C_ID + 128] = np.eye(128)
    c[:, C_CEN:C_CEN + 128] = np.eye(128) - 1.0 / 128
    c[:, C_ONE:C_ONE + 128] = 1.0 / 128
    q, col = i[:64, None], i[None, :]
    first = np.where(col < 64, col <= q, col >= q + 64)
    second = (col >= q) & (col <= q + 64)
    start = first & (col < 64)
    c[:, C_MS:C_MS + 128] = np.where(np.concatenate([first, second]), 0, BIG)
    c[:, C_MF:C_MF + 128] = np.where(np.concatenate([start, second]), 0, BIG)
    c[:, C_CS:C_CS + 128] = np.where(i[None, :] <= i[:, None], 0, BIG)
    c[:, C_CT:C_CT + 128] = np.where(i[None, :] >= i[:, None], 0, BIG)
    half = np.arange(0, DH, 2, dtype=np.float32)
    inv = (np.float32(1.0) / np.float32(10000.0) ** (half / np.float32(DH))).astype(np.float32)
    t = np.arange(SEQ, dtype=np.float32)
    fr = (t[:, None] * inv[None, :]).astype(np.float32)
    fr = np.concatenate([fr, fr], -1).astype(np.float64)
    base = ((half + 0.4 * DH) / (1.4 * DH)).astype(np.float32).astype(np.float64)
    sc = base[None, :] ** ((t.astype(np.float64) - SEQ // 2) / float(WIN // 2))[:, None]
    sc = np.concatenate([sc, sc], -1)
    sign = np.where(np.arange(DH) < DH // 2, -1.0, 1.0)
    for h, (s, g) in enumerate(((sc, 8.0), (1 / sc, 1.0))):
        cos = np.cos(fr) * s * g * 256.0
        sin = np.sin(fr) * s * g * 256.0 * sign
        for j in range(TILES):
            o = j * 128 + h * DH
            c[:, C_COS + o:C_COS + o + DH] = cos[j * 128:(j + 1) * 128]
            c[:, C_SIN + o:C_SIN + o + DH] = sin[j * 128:(j + 1) * 128]
    th = (1.0 / 10000.0 ** (2.0 * np.arange(0, HD // 2, dtype=np.float32) / HD)).astype(np.float32)
    ang = (np.arange(1, SEQ + 1, dtype=np.float32)[:, None] * th[None, :]).astype(np.float32)
    ang = np.concatenate([ang, ang], -1).astype(np.float64)
    f = np.repeat((np.cos(ang) + np.sin(ang)).T, NH, axis=0)
    c[:, C_F:C_F + SEQ] = f / math.sqrt(HD)
    c[:, C_F + SEQ:C_KEPT] = f
    return c


def macaron(nc, x, W_attn, b_attn, W_proj, b_proj, wqkv, q_scale, k_scale, wo, ln_g, ln_b,
            w1, b1, w2, b2, cst, out):
    F, BF = mybir.dt.float32, mybir.dt.bfloat16
    FR = mybir.dt.float32r
    ALU, ACT, AX = mybir.AluOpType, mybir.ActivationFunctionType, mybir.AxisListType.X

    ctx = ExitStack()
    with ctx:
        def sb(name, shape, dt=F):
            return ctx.enter_context(nc.sbuf_tensor(name, shape, dt))

        def sem(name):
            return ctx.enter_context(nc.semaphore(name))

        PS = ctx.enter_context(nc.psum_tensor("PS", [128, 8, 512], F))
        qk_ps = PS[:, 0:2, :].rearrange("p a n -> p (a n)")
        v_ps = PS[:, 2, :]
        sc_ps = PS[:, 3:5, :].rearrange("p a n -> p (a n)")
        tr_ps = PS[:, 5:7, :].rearrange("p a n -> p (a n)")
        o_ps = PS[:, 7, :]

        C = sb("C", [128, C_KEPT])
        ident, centre, mean = C[:, 0:128], C[:, 128:256], C[:, 256:384]
        cb = sb("cb", [128, 5, 128], BF)
        identb, mask_start, mask_inner, mask_qk, mask_kq = (cb[:, i, :] for i in range(5))
        cc = sb("cc", [128, 2])
        xT = sb("xT", [128, BATCH, SEQ])
        yT = sb("yT", [128, BATCH, SEQ + 2])
        zT = sb("zT", [128, BATCH, SEQ + 2])
        wqkv_s = sb("wqkv_s", [128, LAYERS, 3 * INNER])
        wq_low = sb("wq_low", [128, LAYERS, 3 * INNER])
        h_in = sb("h_in", [128, 2, 2, 128])
        wo_s = sb("wo_s", [128, LAYERS, 4, DIM])
        w1_s = sb("w1_s", [128, LAYERS, 2 * HID])
        w2_s = sb("w2_s", [128, LAYERS, 3, DIM])
        vecs = sb("vecs", [128, 23])
        qks = sb("qks", [128, LAYERS, 2, DH])
        cosT = sb("cosT", [128, LAYERS, TILES, 2, DH])
        sinT = sb("sinT", [128, LAYERS, TILES, 2, DH])
        wqkT = sb("wqkT", [128, 3, DIM])
        wpT = sb("wpT", [128, DIM])
        hn = sb("hn", [128, SEQ])
        hc = sb("hc", [128, SEQ])
        nsq = sb("nsq", [128, BATCH, SEQ])
        rstd = sb("rstd", [128, BATCH, SEQ])

        arena = sb("arena", [128, ARENA])
        at = [0]

        def carve(*shape):
            n = int(np.prod(shape))
            v = arena[:, at[0]:at[0] + n]
            at[0] += n
            if len(shape) == 2:
                v = v.rearrange("p (a b) -> p a b", a=shape[0])
            if len(shape) == 3:
                v = v.rearrange("p (a b c) -> p a b c", a=shape[0], b=shape[1])
            if len(shape) == 4:
                v = v.rearrange("p (a b c d) -> p a b c d", a=shape[0], b=shape[1], c=shape[2])
            return v

        sq = carve(1024)
        nrm = carve(3, 16)
        rn = carve(16)
        qn = carve(1024)
        rs = carve(1024)
        rc = carve(1024)
        qr = carve(1024)
        qz = carve(HEADS, 128)
        kT = carve(2, 4, 128)
        v_s = carve(4, INNER)
        vm = carve(2, INNER)
        p_s = carve(2, HEADS, 128)
        nmax = carve(2, HEADS)
        den = carve(2, HEADS)
        rden = carve(2, HEADS)
        pT = carve(HEADS, 128)
        oT = carve(4, 128)
        u_s = carve(3, SEQ)
        layer_words = at[0]

        at[0] = 0
        V_SLOT = TILES * NH * (HD + 1) + 32
        stacks_1 = carve(2 * NH * SEQ // 2 + V_SLOT)
        pe_s = carve(6, 1280)
        mx = carve(4, 16)
        mres = carve(128)
        mpart = carve(3 * 64)
        osb = carve(SEQ)
        rec = carve(TILES, 4)
        ytok = carve(TILES, DIM)
        yaT = carve(SEQ)
        beyond = max(layer_words, at[0])
        at[0] = beyond
        stacks_0 = carve(2 * NH * SEQ // 2 + V_SLOT)
        assert at[0] <= ARENA

        def stack(k, i):
            n = NH * SEQ // 2
            return (stacks_0, stacks_1)[k][:, i * n:(i + 1) * n]

        def v_slot(k):
            return (stacks_0, stacks_1)[k][:, NH * SEQ:]

        def v_heads(k):
            return v_slot(k)[:, 0:TILES * NH * (HD + 1)].rearrange("p (t h d) -> p t h d", t=TILES, h=NH)

        qstb, kstb = ([stack(k, i).bitcast(BF).rearrange("p (h t) -> p h t", h=NH) for k in range(2)]
                      for i in range(2))
        qkf = rstd[:, 1:3, :]
        partb = nsq[:, 1:4, :].bitcast(BF).rearrange("p i (c t) -> p i c t", c=2)
        mpartb = mpart.bitcast(BF).rearrange("p (i t) -> p i t", i=3)

        xin = arena[:, 0:2048].rearrange("p (n f) -> p n f", f=DIM)
        otok = arena[:, beyond:beyond + BATCH * SEQ].rearrange("p (b n) -> p b n", b=BATCH)
        rows = arena[0:22, beyond + 512:beyond + 640]
        wq_in = arena[:, beyond + 3584:beyond + 6656].rearrange("p (l n) -> p l n", l=LAYERS)
        wa = arena[:, beyond:beyond + 512].rearrange("p (n f) -> p n f", f=DIM)
        CS = arena[:, beyond + 1024:beyond + 1024 + C_ALL - C_KEPT]

        scr = nc.dram_tensor("scr", (3, 2, 128, SEQ), BF, kind="Internal").ap()
        scrm = nc.dram_tensor("scrm", (3, NH, TILES, 128), BF, kind="Internal").ap()

        x_loaded = [sem(f"x_loaded{b}") for b in range(BATCH)]
        first_loaded = sem("first_loaded")
        w1_loaded = sem("w1_loaded")
        rest_loaded = sem("rest_loaded")
        rows_loaded = sem("rows_loaded")
        rows_zero = sem("rows_zero")
        vecs_ps = sem("vecs_ps")
        vecs_done = sem("vecs_done")
        masks_done = sem("masks_done")
        xt_ps = sem("xt_ps")
        scaled = sem("scaled")
        tables_done = sem("tables_done")
        folded = sem("folded")
        w_ps = sem("w_ps")
        w_done = sem("w_done")
        bias_ps = sem("bias_ps")
        eps_set = sem("eps_set")
        zeroed = sem("zeroed")
        hi_done = sem("hi_done")
        h_ready = sem("h_ready")
        w_hi = sem("w_hi")
        w_split = sem("w_split")
        w_again = sem("w_again")
        qk_done = sem("qk_done")
        qkv_done = sem("qkv_done")
        sq_done = sem("sq_done")
        v_ready = sem("v_ready")
        ss_done = sem("ss_done")
        ssc_done = sem("ssc_done")
        lnq_done = sem("lnq_done")
        r_done = sem("r_done")
        qn_done = sem("qn_done")
        rots_done = sem("rots_done")
        rotc_done = sem("rotc_done")
        qr_done = sem("qr_done")
        kr_done = sem("kr_done")
        qktr_done = sem("qktr_done")
        qzhi_done = sem("qzhi_done")
        qzlo_done = sem("qzlo_done")
        kt_done = sem("kt_done")
        sclo_done = sem("sclo_done")
        sc_done = sem("sc_done")
        maxlo_done = sem("maxlo_done")
        max_done = sem("max_done")
        exp_done = sem("exp_done")
        rden_done = sem("rden_done")
        pn_done = sem("pn_done")
        pttr_done = sem("pttr_done")
        pta_done = sem("pta_done")
        ptd_done = sem("ptd_done")
        pv_done = sem("pv_done")
        oev_done = sem("oev_done")
        wo_done = sem("wo_done")
        z_done = sem("z_done")
        vm_done = sem("vm_done")
        cen_done = sem("cen_done")
        hc_done = sem("hc_done")
        csq_done = sem("csq_done")
        var_done = sem("var_done")
        lnr_done = sem("lnr_done")
        rstd_done = sem("rstd_done")
        hn_done = sem("hn_done")
        g_done = sem("g_done")
        gl_done = sem("gl_done")
        a_done = sem("a_done")
        u_done = sem("u_done")
        w2_done = sem("w2_done")
        y_ready = sem("y_ready")
        x_ready = sem("x_ready")
        out_ps = sem("out_ps")
        out_sb = sem("out_sb")
        stored = sem("stored")
        stack_rows = sem("stack_rows")
        m_qk = sem("m_qk")
        m_v = sem("m_v")
        m_vp = sem("m_vp")
        m_f = sem("m_f")
        m_p1 = sem("m_p1")
        m_r1 = sem("m_r1")
        m_p2 = sem("m_p2")
        m_p3 = sem("m_p3")
        m_sav = sem("m_sav")
        m_stk = sem("m_stk")
        m_s = sem("m_s")
        m_max = sem("m_max")
        m_t = sem("m_t")
        m_m1 = sem("m_m1")
        m_m2 = sem("m_m2")
        m_m3 = sem("m_m3")
        m_m4 = sem("m_m4")
        m_msav = sem("m_msav")
        m_st = sem("m_st")
        m_exp = sem("m_exp")
        m_pv = sem("m_pv")
        m_osb = sem("m_osb")
        m_ot = sem("m_ot")
        m_rec = sem("m_rec")
        m_yt = sem("m_yt")
        m_ytt = sem("m_ytt")
        m_ya = sem("m_ya")
        m_pr = sem("m_pr")
        m_hc = sem("m_hc")
        max_stacked = [sem(f"max_stacked{g}") for g in range(4)]

        def y_count(L, b):
            return (L + L // 2) * 4 + b + 1

        def y_after(L, b):
            return (L + 1 + L // 2) * 4 + b + 1

        def tile(L, b, j, back):
            while j < back:
                if isinstance(b, int) and b == 0:
                    if L % 2 == 0:
                        return None
                    L, b = L - 1, BATCH
                b, back = b - 1, back - 4
            return L, b, j - back

        def stages(L, b, j, live):
            return [(L, b, j) if live else None] + [tile(L, b, j, k) if live or j < k else None
                                                   for k in range(1, 5)]

        def late(t, n):
            return not isinstance(t[1], int) or num(t) >= n

        def num(t):
            L, b, j = t
            return 16 * L + 4 * b + j

        def norm_index(L, b):
            if L == 1 and isinstance(b, int) and b == BATCH - 1:
                return 12
            return (4 + 4 * L + b) if L < 2 else (SECOND_NORM + 4 + 4 * (L - 2) + b)

        def mid_norm(n):
            return 12 + n if n else 11

        SECOND_NORM = 16
        CENTRE_BANK, VARIANCE_BANK = (3, 4, 5, 6), (0, 1, 2, 7)

        PAIRS, LAG = 8 * BATCH, 4

        def slots(r):
            work = [None, None, None]
            if r % 2 == 0:
                if 1 <= r // 2 <= 4 * BATCH:
                    work[0] = ("max", r // 2 - 1)
                if r >= LAG + 2:
                    work[1:] = [("pv", (r - LAG - 2) // 2), ("o", (r - LAG - 2) // 2)]
            else:
                b = r // 8
                if r == 1:
                    work = [("centre", 1), ("variance", 1), None]
                if r % 8 == (3 if b == 0 else 1) and b + 1 < BATCH:
                    work = [("q", b + 1), ("k", b + 1), None]
                if r % 8 == 5 and b >= 1:
                    work = [("y", b - 1), ("project", b - 1), None]
                if r % 8 == 7 and b + 1 < BATCH:
                    work = [("v", b + 1), None, None]
                    if b + 2 < BATCH:
                        work[1:] = [("centre", b + 2), ("variance", b + 2)]
            return work

        ROUNDS = PAIRS + LAG
        ROUND = [("scores", 0), ("transposed", 0), ("scores", 1), ("slot", 0), ("scores", 2),
                 ("transposed", 1), ("scores", 3), ("slot", 1), ("transposed", 2), ("scores", 4), ("slot", 2)]
        TAIL = [("pv", 4 * BATCH - 1), ("o", 4 * BATCH - 1), ("y", BATCH - 1), ("project", BATCH - 1)]
        USES = [w for r in range(ROUNDS) for w in slots(r) if w is not None] + TAIL

        def bank_of(what, n):
            early = {"centre": 0, "variance": 1, "q": 0, "k": 1, "v": 2}
            return PS[:, early[what] if n == 0 and what in early else 7, :]

        def freed(what, n):
            return {"centre": (m_hc, n + 1), "variance": (lnr_done, mid_norm(n) + 1),
                    "q": (m_f, 2 * n + 1), "k": (m_f, 2 * n + 2), "v": (m_vp, n + 1),
                    "max": (m_m2, n + 1), "pv": (m_osb, n + 1), "o": (m_yt, n + 1),
                    "y": (m_ya, n + 1), "project": (x_ready, 4 + n + 1)}[what]

        def s_units(n):
            h = 2 * (n % 8)
            return [[(0, h, 3)], [(0, h, 2), (384, h, 0)], [(0, h + 1, 3)],
                    [(0, h + 1, 2), (384, h + 1, 0)], [(0, h, 1), (256, h + 1, 1)]]

        def st_units(n):
            h = 2 * (n % 8)
            return [[(0, 0, h, 0), (1, 0, h, 1), (1, 384, h, 3)],
                    [(2, 0, h + 1, 0), (3, 0, h + 1, 1), (3, 384, h + 1, 3)],
                    [(4, 0, h, 2), (4, 256, h + 1, 2)]]

        block = ctx.enter_context(nc.Block())

        load_x, load_first, load_w1, load_rest = [], [], [], []
        load_x.append((C[:, 0:C_F], cst[:, 0:C_F], 0))
        for i in range(BATCH * TILES):
            load_x.append((xin[:, i, :], x[i // TILES, 128 * (i % TILES):128 * (i % TILES) + 128, :],
                           i // TILES))
        load_first.append((wq_in[:, 0, :], wqkv[0]))
        load_first.append((CS, cst[:, C_KEPT:]))
        load_first.append((qks[:, :, 0, :], q_scale.rearrange("(o l) d -> o l d", o=1)
                           .broadcast_to((128, LAYERS, DH))))
        load_first.append((qks[:, :, 1, :], k_scale.rearrange("(o l) d -> o l d", o=1)
                           .broadcast_to((128, LAYERS, DH))))
        load_rest.append((wo_s[:, :, :, :], wo.rearrange("l (k p) n -> p l k n", p=128)))
        load_w1.append((w1_s[:, :, :], w1.rearrange("l p n -> p l n")))
        for m in range(3):
            load_rest.append((w2_s[0:HB[m], :, m, :],
                              w2[:, HO[m]:HO[m] + HB[m], :].rearrange("l p n -> p l n")))
        load_rest.append((wq_in[:, 1, :], wqkv[1]))
        load_w1.append((wa[:, 0:3, :], W_attn.rearrange("(c p) n -> p c n", p=128)))
        load_w1.append((wa[:, 3, :], W_proj))
        load_rest.append((C[:, C_F:], cst[:, C_F:C_KEPT]))
        load_rows = [(rows[4 * m:4 * m + 4, 0:HB[m]],
                      b1.rearrange("l (a h) -> (l a) h", a=2)[:, HO[m]:HO[m] + HB[m]]) for m in range(3)]
        load_rows.append((rows[V_B2:V_B2 + 2, :], b2))
        load_rows.append((rows[V_G:V_G + 2, :], ln_g))
        load_rows.append((rows[V_B:V_B + 2, :], ln_b))
        for c in range(2):
            load_rows.append((rows[V_Q + c:V_Q + c + 1, :].rearrange("o (d h) -> o d h", d=HD),
                              b_attn[c * DIM:(c + 1) * DIM].rearrange("(o h d) -> o d h", o=1, h=NH)))
        load_rows.append((rows[V_V:V_V + 1, :], b_attn[2 * DIM:3 * DIM].rearrange("(o n) -> o n", o=1)))
        load_rows.append((rows[V_P:V_P + 1, :], b_proj.rearrange("(o n) -> o n", o=1)))

        @block.sync
        def _(sp):
            for dst, src, b in load_x[0::2]:
                sp.dma_start(dst, src).then_inc(x_loaded[b], 16)
            for dst, src in load_first:
                sp.dma_start(dst, src).then_inc(first_loaded, 16)
            for dst, src in load_w1:
                sp.dma_start(dst, src).then_inc(w1_loaded, 16)
            for dst, src in load_rest:
                sp.dma_start(dst, src).then_inc(rest_loaded, 16)

            def stack_max(n):
                b, g = n // 4, n % 4
                sp.wait_ge(m_m4, n + 1)
                sp.dma_start(scrm[:, 4 * g:4 * g + 4, :, :].rearrange("i h q t -> (h q) i t"),
                             mpartb[0:16, :, :]).then_inc(m_msav, 16)
                sp.wait_ge(m_msav, 16 * (n + 1))
                sp.dma_start(qstb[b % 2][72:75, 4 * g:4 * g + 4, :],
                             scrm[:, 4 * g:4 * g + 4, :, :].rearrange("i h q t -> i h (q t)")
                             ).then_inc(max_stacked[g], 16)

            def save_parts(b):
                sp.wait_ge(m_p3, b + 1)
                sp.dma_start(scr.rearrange("i c p t -> p i c t"), partb).then_inc(m_sav, 16)

            def stack_parts(b):
                k = b % 2
                sp.wait_ge(m_sav, 16 * (b + 1))
                sp.wait_ge(zeroed, 2 + min(b, 1))
                if b >= 2:
                    sp.wait_ge(m_st, 24 * (b - 1))
                q, kk = (scr[:, c].rearrange("i (d h) t -> i d (h t)", h=NH) for c in range(2))
                for i in range(3):
                    r = slice(24 * i, 24 * i + 24)
                    sp.dma_start(stack(k, 1)[r, :].bitcast(BF), kk).then_inc(m_stk, 16)
                    sp.dma_start(stack(k, 0)[r, :].bitcast(BF),
                                 q[i:i + 1].broadcast_to((3, HD, NH * SEQ))).then_inc(m_stk, 16)
                sp.dma_start(stack(k, 0)[72:75, :], stack(k, 0)[76:79, :]).then_inc(m_stk, 16)

            save_parts(0)
            stack_parts(0)
            for n in range(4 * BATCH):
                b = n // 4 + 1
                if b < BATCH and n in (2, 5, 9):
                    save_parts(b)
                if b < BATCH and n in (2, 6, 10):
                    stack_parts(b)
                stack_max(n)
            sp.wait_ge(m_pv, 4 * BATCH - 4)
            for l in range(LAYERS):
                sp.dma_start(wq_in[:, l, :], wqkv[l]).then_inc(w_again, 16)
            for b in range(BATCH):
                sp.wait_ge(out_sb, b + 1)
                sp.dma_start(out[b].rearrange("(n p) f -> p n f", p=128),
                             otok[:, b, :].rearrange("p (n f) -> p n f", f=DIM)
                             ).then_inc(stored, 16)
            sp.wait_ge(stored, 16 * BATCH)

        @block.tensor
        def _(pe):
            mm, tr = nc.tensor.matmul, nc.tensor.transpose

            def q_product(t):
                (L, b, j), n = t, num(t)
                pe.wait_ge(h_ready, n + 1)
                if isinstance(b, int) and n in (0, 16, 32):
                    pe.wait_ge(w_split, n // 16 + 1)
                if isinstance(b, int) and n == 0:
                    pe.wait_ge(vecs_done, 1)
                if not (isinstance(b, int) and n == 0):
                    pe.wait_ge(qn_done, n)
                    pe.wait_ge(v_ready, n)
                split_product(qk_ps[:, 0:512], L, j, 0)

            def split_product(out, L, j, c):
                hi, lo = (h_in[:, j % 2, i, :].bitcast(FR) for i in range(2))
                w_hi, w_lo = (w[:, L % 2, 512 * c:512 * c + 512].bitcast(FR) for w in (wqkv_s, wq_low))
                mm(out, hi, w_hi, start=True, stop=False)
                mm(out, hi, w_lo, start=False, stop=False)
                return mm(out, lo, w_hi, start=False, stop=True)

            def kv_products(t):
                L, b, j = t
                split_product(qk_ps[:, 512:1024], L, j, 1).then_inc(qk_done, 1)
                split_product(v_ps, L, j, 2).then_inc(qkv_done, 1)

            def qk_transposes(t):
                (L, b, j), n = t, num(t)
                pe.wait_ge(qr_done, n + 1)
                pe.wait_ge(kr_done, n + 1)
                if isinstance(b, int) and n in (0, 32):
                    pe.wait_ge(hn_done, L // 2 * SECOND_NORM + 4)
                if not (isinstance(b, int) and n < 2):
                    pe.wait_ge(pta_done, n - 1)
                    pe.wait_ge(ptd_done, n - 1)
                for i in range(8):
                    last = tr(tr_ps[:, i * 128:(i + 1) * 128], qr[:, i * 128:(i + 1) * 128], ident)
                last.then_inc(qktr_done, 1)

            def scores(t):
                (L, b, j), n = t, num(t)
                k = j % 2
                if not (isinstance(b, int) and n == 0):
                    pe.wait_ge(exp_done, n)
                m = (mask_inner if j else mask_start).rearrange("p (o n) -> p o n", o=1)
                for c in range(2):
                    mm(sc_ps[:, c * 512:(c + 1) * 512].rearrange("p (h n) -> p h n", h=4), identb,
                       m.broadcast_to((128, 4, 128)), start=True, stop=False)
                pe.wait_ge(qzhi_done, n + 1)
                pe.wait_ge(qzlo_done, n + 1)
                pe.wait_ge(kt_done, n + 1)
                for c in range(2):
                    for h in range(4 * c, 4 * c + 4):
                        o = sc_ps[:, h * 128:(h + 1) * 128]
                        keys = kT[:, k, h // 2, :]
                        base = keys.offset
                        step = (1 - 2 * k) * 512 + 64
                        split = bass.AP(keys.tensor, base, [list(keys.ap[0]), [step, 2], [1, 64]])
                        mm(o[0:64].rearrange("p (a c) -> p a c", a=2), qz[:, h, 0:64], split,
                           start=False, stop=h % 4 == 3)
                        last = mm(o[64:128], qz[:, h, 64:128], keys, start=False, stop=h % 4 == 3)
                    last.then_inc(sc_done if c else sclo_done, 1)

            def p_transposes(t, newer, behind):
                n = num(t)
                pe.wait_ge(pn_done, n + 1)
                if newer is not None:
                    m = num(newer)
                    pe.wait_ge(qzhi_done, m + 1)
                    pe.wait_ge(qzlo_done, m + 1)
                    pe.wait_ge(kt_done, m + 1)
                if t[2] == 1 and behind is not None:
                    pe.wait_ge(y_ready, y_after(behind[0], behind[1]))
                for h in range(HEADS):
                    last = tr(tr_ps[:, h * 128:(h + 1) * 128], p_s[:, t[2] % 2, h, :], ident)
                last.then_inc(pttr_done, 1)

            def pv(t):
                (L, b, j), n = t, num(t)
                pe.wait_ge(pta_done, n + 1)
                pe.wait_ge(ptd_done, n + 1)
                pe.wait_ge(v_ready, n + 1)
                pe.wait_ge(vm_done, n + 1)
                if not (isinstance(b, int) and n == 0):
                    pe.wait_ge(z_done, n)
                for w in range(2):
                    for h in range(HEADS):
                        r, c = 64 * (h % 2), (h // 2) * 128 + 64 * w
                        val = v_s[:, j, :] if w else vm[:, j % 2, :]
                        last = mm(o_ps[r:r + 64, c:c + 64], val[:, h * 64:(h + 1) * 64],
                                  pT[:, h, 64 * w:64 * w + 64], start=True, stop=True)
                last.then_inc(pv_done, 1)

            def project(t):
                L, n = t[0], num(t)
                pe.wait_ge(oev_done, n + 1)
                for k in range(4):
                    last = mm(o_ps[:, 0:128], wo_s[:, L % 2, k, :], oT[:, k, :], start=k == 0, stop=k == 3)
                last.then_inc(wo_done, 1)

            def mlp_centre(t):
                L, b, _ = t
                pe.wait_ge(z_done, num(t) + 1)
                mm(o_ps, centre, zT[:, b, 0:SEQ], start=True, stop=True).then_inc(cen_done, 1)

            def mlp_variance(t):
                q = norm_index(t[0], t[1])
                pe.wait_ge(csq_done, q + 1)
                mm(o_ps, mean, nsq[:, 0, :], start=True, stop=True).then_inc(var_done, 1)

            def mlp(t, newest, live):
                L, b, _ = t
                q, nq, l = norm_index(L, b), 4 * L + b, L % 2
                g_ps, a_ps = (PS[:, 3, :], PS[:, 4, :], PS[:, 7, :]), (PS[:, 2, :], PS[:, 0, :], PS[:, 1, :])
                pe.wait_ge(hn_done, q + 1)
                for m in range(3):
                    if m == 0:
                        pe.wait_ge(exp_done, newest - 1 if live else newest + 1)
                    if m == 2 and live:
                        pe.wait_ge(oev_done, newest - 2)
                    o = HID + HO[m]
                    mm(g_ps[m][0:HB[m]], w1_s[:, l, o:o + HB[m]], hn[:, :], start=True,
                       stop=True).then_inc(g_done, 1)
                for m in range(3):
                    if m == 0:
                        pe.wait_ge(v_ready, newest + 1)
                    if m == 1:
                        pe.wait_ge(qn_done, newest + 1)
                    mm(a_ps[m][0:HB[m]], w1_s[:, l, HO[m]:HO[m] + HB[m]], hn[:, :], start=True,
                       stop=True).then_inc(a_done, 1)
                for evicted in (qzhi_done, qzlo_done, kt_done):
                    pe.wait_ge(evicted, newest if live else newest + 1)
                for m in range(3):
                    pe.wait_ge(u_done, 3 * nq + m + 1)
                    last = mm(PS[:, 5, :], w2_s[0:HB[m], l, m, :], u_s[0:HB[m], m, :],
                              start=m == 0, stop=m == 2)
                last.then_inc(w2_done, 1)

            def step(L, b, j, live=True):
                t0, t1, t2, t3, t4 = stages(L, b, j, live)
                mlp_due = t4 is not None and j == 3
                if t2 is not None:
                    scores(t2)
                if t4 is not None:
                    project(t4)
                if t3 is not None:
                    p_transposes(t3, t2, tile(L, b, j, 5) if j == 0 else None)
                if t0 is not None:
                    q_product(t0)
                if mlp_due:
                    mlp_centre(t4)
                if t0 is not None:
                    kv_products(t0)
                if mlp_due:
                    mlp_variance(t4)
                if t1 is not None:
                    qk_transposes(t1)
                if mlp_due:
                    pe.wait_ge(lnr_done, norm_index(t4[0], t4[1]) + 1)
                if t3 is not None:
                    pv(t3)
                if mlp_due:
                    mlp(t4, num(t0 if live else t4), live)

            def output(b):
                pe.wait_ge(x_ready, 12 + b + 1)
                for i in range(TILES):
                    last = tr(PS[:, b, i * 128:(i + 1) * 128], xT[:, b, i * 128:(i + 1) * 128], ident)
                last.then_inc(out_ps, 1)

            def bank7(what, n):
                i = USES.index((what, n))
                if i:
                    pe.wait_ge(*freed(*USES[i - 1]))

            def slot(what, n):
                bank, b, g = bank_of(what, n), n // 4, n % 4
                if (what, n) in USES:
                    bank7(what, n)
                if what == "centre":
                    pe.wait_ge(x_ready, 5 + n)
                    mm(bank, centre, xT[:, n, :], start=True, stop=True).then_inc(cen_done, 1)
                if what == "variance":
                    pe.wait_ge(csq_done, mid_norm(n) + 1)
                    mm(bank, mean, nsq[:, 0, :], start=True, stop=True).then_inc(var_done, 1)
                if what == "q":
                    pe.wait_ge(hn_done, mid_norm(n) + 1)
                    mm(bank, wqkT[:, 0, :], hn[:, :], start=True, stop=True).then_inc(m_qk, 1)
                if what == "k":
                    mm(bank, wqkT[:, 1, :], hn[:, :], start=True, stop=True).then_inc(m_qk, 1)
                if what == "v":
                    for i in range(TILES):
                        last = mm(bank[:, i * 128:(i + 1) * 128], hn[:, i * 128:(i + 1) * 128],
                                  wqkT[:, 2, :], start=True, stop=True)
                    last.then_inc(m_v, 1)
                if what == "max":
                    pe.wait_ge(m_max, 10 * (n + 1))
                    tr(bank[0:16, 0:128], mx[:, g, :], ident).then_inc(m_t, 1)
                if what == "pv":
                    pe.wait_ge(m_exp, 6 * (n + 1))
                    pe.wait_ge(m_vp, b + 1)
                    for kt in range(TILES):
                        for j in range(4):
                            col = {0: 0, 1: 512, 3: 896, 2: 1024}[kt]
                            row = 2 * ((2 * n + j // 2) % 3) + j % 2
                            first = (kt * NH + 4 * g + j) * (HD + 1)
                            last = mm(bank[32 * j:32 * j + 32, 128 * kt:SEQ], v_slot(b % 2)[:, first:first + 32],
                                      pe_s[:, row, col:col + SEQ - 128 * kt],
                                      start=kt == 0, stop=kt == TILES - 1, tile_position=(0, 32 * j))
                    last.then_inc(m_pv, 1)
                if what == "o":
                    for i in range(TILES):
                        last = tr(bank[:, i * 128:(i + 1) * 128], osb[:, i * 128:(i + 1) * 128], ident)
                    last.then_inc(m_ot, 1)
                if what == "y":
                    pe.wait_ge(m_yt, 4 * (n + 1))
                    for i in range(TILES):
                        last = tr(bank[:, i * 128:(i + 1) * 128], ytok[:, i, :], ident)
                    last.then_inc(m_ytt, 1)
                if what == "project":
                    mm(bank, wpT[:, :], yaT[:, :], start=True, stop=True).then_inc(m_pr, 1)

            def s_unit(n, i):
                u, k = 5 * n + i, (n // 8) % 2
                if i == 0 and n % 8 == 0:
                    pe.wait_ge(m_stk, 16 * 7 * (n // 8 + 1))
                if u >= 2:
                    pe.wait_ge(m_max, u - 1)
                for col, h, qt in s_units(n)[i]:
                    w = 128 * (qt + 1)
                    o = PS[:, 5 + u % 2, col:col + w]
                    mm(o, qstb[k][0:96, h, 128 * qt:128 * qt + 128], kstb[k][0:96, h, 0:w],
                       start=True, stop=False)
                    last = mm(o[:, w - 128:w], identb, mask_qk, start=False, stop=True)
                last.then_inc(m_s, 1)

            def st_unit(n, i):
                k = (n // 8) % 2
                if i == 0 and n % 2 == 0:
                    pe.wait_ge(max_stacked[n // 2 % 4], 16 * (n // 8 + 1))
                if n:
                    pe.wait_ge(m_exp, 3 * (n - 1) + i + 1)
                for bank, col, h, kt in st_units(n)[i]:
                    w = SEQ - 128 * kt
                    mm(PS[:, bank, col:col + w], kstb[k][0:96, h, 128 * kt:128 * kt + 128],
                       qstb[k][0:96, h, 128 * kt:SEQ], start=True, stop=False)
                    last = mm(PS[:, bank, col:col + 128], identb, mask_kq, start=False, stop=True)
                last.then_inc(m_st, 1)

            def drain(block_no, j):
                if j == 0:
                    pe.wait_ge(qn_done, 32 * (block_no + 1))
                    pe.wait_ge(v_ready, 32 * (block_no + 1))
                if block_no == 0:
                    for what in {0: ["centre"], 1: [], 2: ["variance"], 3: ["q", "k", "v"]}[j]:
                        slot(what, 0)
                    if j == 3:
                        pe.wait_ge(m_f, 2)
                        pe.wait_ge(m_vp, 1)
                else:
                    if j < 3:
                        output(j)
                    else:
                        pe.wait_ge(out_sb, 3)

            def layers(block_no):
                for L in (2 * block_no, 2 * block_no + 1):
                    for j in range(4):
                        base = block_no * SECOND_NORM
                        if L % 2 == 0 and j == 0:
                            pe.wait_ge(lnr_done, base + 3)
                        step(L, 0, j)
                        if L == 0 and j == 0:
                            weights()
                        if L == 0 and j == 1:
                            pe.wait_ge(folded, 1)
                            pe.wait_ge(masks_done, 1)
                            pe.wait_ge(rest_loaded, 16 * len(load_rest))
                    if L == 0:
                        pe.wait_ge(scaled, 2)
                    with pe.Fori(1, BATCH) as b:
                        for j in range(4):
                            step(L, b, j)
                for j in range(4):
                    drain(block_no, j)
                    step(L, BATCH, j, live=False)

            def norm_centre(b, wait_x):
                pe.wait_ge(x_ready, wait_x + b)
                mm(PS[:, CENTRE_BANK[b], :], centre, xT[:, b, :], start=True, stop=True).then_inc(cen_done, 1)

            def norm_mean(b, base):
                pe.wait_ge(csq_done, base + b + 1)
                mm(PS[:, VARIANCE_BANK[b], :], mean, nsq[:, b, :], start=True, stop=True).then_inc(var_done, 1)

            def small_vectors():
                pe.wait_ge(rows_loaded, 16 * len(load_rows))
                pe.wait_ge(lnr_done, 4)
                tr(PS[:, 2, 0:22], rows[:, :], ident[0:22, 0:22]).then_inc(vecs_ps, 1)

            def weights():
                pe.wait_ge(w1_loaded, 16 * len(load_w1))
                for i in range(4):
                    last = tr(PS[:, 7, i * 128:(i + 1) * 128], wa[:, i, :], ident)
                last.then_inc(w_ps, 1)
                pe.wait_ge(vecs_done, 1)
                pe.wait_ge(hn_done, 1)
                for l in range(LAYERS):
                    for a in range(2):
                        for m in range(3):
                            i, o = b1_column(l, a, m), a * HID + HO[m]
                            mm(PS[0:HB[m], 3, i:i + 1], w1_s[:, l, o:o + HB[m]],
                               vecs[:, V_B + l:V_B + l + 1], start=True, stop=True)
                pe.wait_ge(w_done, 1)
                mm(PS[:, 3, 12:13], wpT[:, :], vecs[:, V_V:V_V + 1], start=True, stop=True).then_inc(
                    bias_ps, 1)

            for step_no in range(BATCH + 2):
                if step_no < BATCH:
                    pe.wait_ge(x_loaded[step_no], 16 * (TILES + (step_no == 0)))
                    for i in range(TILES):
                        last = tr(PS[:, VARIANCE_BANK[step_no], i * 128:(i + 1) * 128],
                                  xin[:, TILES * step_no + i, :], ident)
                    last.then_inc(xt_ps, 1)
                if 1 <= step_no <= BATCH:
                    norm_centre(step_no - 1, 1)
                if step_no >= 2:
                    norm_mean(step_no - 2, 0)
            small_vectors()
            layers(0)

            pe.wait_ge(x_ready, 8)
            for r in range(ROUNDS):
                work = slots(r)
                for kind, i in ROUND:
                    if kind == "scores" and r < PAIRS:
                        s_unit(r, i)
                    if kind == "transposed" and r >= LAG:
                        st_unit(r - LAG, i)
                    if kind == "slot" and work[i] is not None:
                        slot(*work[i])

            slot(*TAIL[0])
            for b in range(3):
                norm_centre(b, 9)
            slot(*TAIL[1])
            for b in range(3):
                norm_mean(b, SECOND_NORM)
            slot(*TAIL[2])
            slot(*TAIL[3])
            norm_centre(3, 9)
            norm_mean(3, SECOND_NORM)
            layers(1)
            output(3)

        @block.scalar
        def _(act):
            A = nc.scalar.activation
            nc.scalar.preload_act_table_set("natural_log_exp_and_others")
            for dst, src, b in load_x[1::2]:
                act.dma_start(dst, src).then_inc(x_loaded[b], 16)

            def scale_w1():
                act.wait_ge(bias_ps, 1)
                for l in range(LAYERS):
                    A(w1_s[:, l, :], w1_s[:, l, :], ACT.Copy, scale=vecs[:, V_G + l:V_G + l + 1]).then_inc(
                        scaled, 1)

            def squares(t):
                n = num(t)
                act.wait_ge(qk_done, n + 1)
                if not isinstance(t[1], int) or n:
                    act.wait_ge(ss_done, n)
                A(sq, qk_ps, ACT.Square).then_inc(sq_done, 1)

            def v_evict(t):
                n = num(t)
                act.wait_ge(qkv_done, n + 1)
                if not isinstance(t[1], int) or n >= 4:
                    act.wait_ge(pv_done, n - 3)
                    act.wait_ge(vm_done, n - 2)
                A(v_s[:, t[2], :], v_ps, ACT.Copy).then_inc(v_ready, 1)

            def norms_of_heads(t):
                n = num(t)
                act.wait_ge(ssc_done, n + 1)
                A(nrm[:, 2, :], nrm[:, 1, :], ACT.Ln, scale=65536.0).then_inc(lnq_done, 1)
                act.wait_ge(lnq_done, n + 1)
                if not isinstance(t[1], int) or n:
                    act.wait_ge(qn_done, n)
                A(rn, nrm[:, 2, :], ACT.Exp, scale=-0.5).then_inc(r_done, 1)

            def q_upper(t):
                n = num(t)
                act.wait_ge(qktr_done, n + 1)
                if isinstance(t[1], int) and n == 0:
                    act.wait_ge(zeroed, 1)
                else:
                    act.wait_ge(sc_done, n)
                A(qz[64:128, 1::2, :], tr_ps[64:128, 0:512].rearrange("p (h n) -> p h n", h=4),
                  ACT.Copy).then_inc(qzhi_done, 1)

            def k_evict(t):
                n = num(t)
                act.wait_ge(qktr_done, n + 1)
                if late(t, 1):
                    act.wait_ge(sc_done, n)
                A(kT[:, t[2] % 2, :, :], tr_ps[:, 512:1024].rearrange("p (h n) -> p h n", h=4),
                  ACT.Copy).then_inc(kt_done, 1)

            def softmax(t, heads):
                (L, b, j), n = t, num(t)
                k = j % 2
                act.wait_ge(max_done if heads[0] else maxlo_done, n + 1)
                if heads[0] == 0 and (not isinstance(b, int) or n >= 2):
                    act.wait_ge(pttr_done, n - 1)
                    act.wait_ge(rden_done, n - 1)
                for h in heads:
                    last = A(p_s[:, k, h, :], sc_ps[:, h * 128:(h + 1) * 128], ACT.Exp,
                             bias=nmax[:, k, h:h + 1], accum_out=den[:, k, h:h + 1])
                if heads[-1] == HEADS - 1:
                    last.then_inc(exp_done, 1)

            def pt_evict(t):
                n = num(t)
                act.wait_ge(pttr_done, n + 1)
                if not isinstance(t[1], int) or n:
                    act.wait_ge(pv_done, n)
                A(pT[:, 0:4, :], tr_ps[:, 0:512].rearrange("p (h n) -> p h n", h=4),
                  ACT.Copy).then_inc(pta_done, 1)

            def o_evict(t):
                n = num(t)
                act.wait_ge(pv_done, n + 1)
                if not isinstance(t[1], int) or n:
                    act.wait_ge(wo_done, n)
                A(oT, o_ps.rearrange("p (k n) -> p k n", k=4), ACT.Copy).then_inc(oev_done, 1)

            def log_deviation(q, src, k):
                act.wait_ge(var_done, q + 1)
                if not isinstance(q, int) or q:
                    act.wait_ge(hn_done, q - k)
                A(rstd[:, k, :], src, ACT.Ln, bias=cc[:, 0:1]).then_inc(lnr_done, 1)

            def inverse_deviation(q, k):
                act.wait_ge(lnr_done, q + 1)
                A(rstd[:, k, :], rstd[:, k, :], ACT.Exp, scale=-0.5).then_inc(rstd_done, 1)

            def block_deviations(base, batches):
                for b in batches:
                    log_deviation(base + b, PS[:, VARIANCE_BANK[b], :], b)
                    inverse_deviation(base + b, b)

            def norm_square(b, base):
                act.wait_ge(cen_done, base + b + 1)
                A(nsq[:, b, :], PS[:, CENTRE_BANK[b], :], ACT.Square).then_inc(csq_done, 1)

            def mlp_squares(t):
                q = norm_index(t[0], t[1])
                act.wait_ge(hc_done, 4 * t[0] + t[1] + 1)
                A(nsq[:, 0, :], hc[:, :], ACT.Square).then_inc(csq_done, 1)

            def mlp(t):
                L, b, _ = t
                nq = 4 * L + b
                for m in range(3):
                    act.wait_ge(g_done, 3 * nq + m + 1)
                    if not (isinstance(nq, int) and nq == 0):
                        act.wait_ge(w2_done, nq)
                    A(u_s[0:HB[m], m, :], PS[0:HB[m], (3, 4, 7)[m], :], ACT.Gelu,
                      bias=vecs[0:HB[m], b1_column(L % 2, 1, m):b1_column(L % 2, 1, m) + 1]).then_inc(gl_done, 1)
                nc.scalar.preload_act_table_set("natural_log_exp_and_others")

            def step(L, b, j, live=True):
                t0, t1, t2, t3, t4 = stages(L, b, j, live)
                mlp_due = t4 is not None and j == 3
                if t2 is not None:
                    softmax(t2, range(0, 4))
                    softmax(t2, range(4, 8))
                if t3 is not None:
                    pt_evict(t3)
                if mlp_due:
                    mlp_squares(t4)
                if t0 is not None:
                    squares(t0)
                if mlp_due:
                    q = norm_index(t4[0], t4[1])
                    log_deviation(q, o_ps, 0)
                    inverse_deviation(q, 0)
                if t1 is not None:
                    q_upper(t1)
                    k_evict(t1)
                if t3 is not None:
                    o_evict(t3)
                if t0 is not None:
                    norms_of_heads(t0)
                    v_evict(t0)
                if mlp_due:
                    mlp(t4)

            def slot(what, n):
                bank = bank_of(what, n)
                if what == "centre":
                    q = mid_norm(n)
                    act.wait_ge(cen_done, q + 1)
                    act.wait_ge(hn_done, q)
                    A(hc[:, :], bank, ACT.Copy).then_inc(m_hc, 1)
                    act.wait_ge(m_hc, n + 1)
                    A(nsq[:, 0, :], hc[:, :], ACT.Square).then_inc(csq_done, 1)
                if what == "variance":
                    log_deviation(mid_norm(n), bank, 0)
                    inverse_deviation(mid_norm(n), 0)
                if what == "v":
                    act.wait_ge(m_v, n + 1)
                    if n < 2:
                        act.wait_ge(zeroed, 2 + n)
                    if n >= 2:
                        act.wait_ge(m_pv, 4 * (n - 1))
                    A(v_heads(n % 2)[:, :, :, 0:HD], bank.rearrange("p (t h d) -> p t h d", t=TILES, h=NH),
                      ACT.Copy).then_inc(m_vp, 1)
                if what == "k":
                    act.wait_ge(m_f, 2 * n + 2)
                    if n:
                        act.wait_ge(m_sav, 16 * n)
                    A(partb[:, 0, :, :], qkf, ACT.Copy).then_inc(m_p1, 1)
                if what == "pv":
                    act.wait_ge(m_pv, n + 1)
                    A(osb, bank, ACT.Copy).then_inc(m_osb, 1)
                if what == "y":
                    act.wait_ge(m_ytt, n + 1)
                    A(yaT, bank, ACT.Copy).then_inc(m_ya, 1)

            def second_part(b):
                act.wait_ge(m_r1, b + 1)
                A(partb[:, 1, :, :], qkf, ACT.Copy).then_inc(m_p2, 1)

            def exp_unit(n, i):
                k = 2 * (n % 3)
                act.wait_ge(m_st, 3 * n + i + 1)
                if i == 0 and n >= 3:
                    act.wait_ge(m_pv, (n - 3) // 2 + 1)
                if i < 2:
                    A(pe_s[:, k + i, 0:1024], PS[:, 2 * i:2 * i + 2, :].rearrange("p a n -> p (a n)"),
                      ACT.Exp).then_inc(m_exp, 1)
                else:
                    A(pe_s[:, k:k + 2, 1024:1280], PS[:, 4, :].rearrange("p (a n) -> p a n", a=2),
                      ACT.Exp).then_inc(m_exp, 1)

            def drain(block_no, j):
                if block_no == 0:
                    for what in {0: [], 1: ["centre"], 2: [], 3: ["variance", "v", "k"]}[j]:
                        slot(what, 0)
                    if j == 3:
                        second_part(0)
                elif j:
                    output(j - 1)

            def output(b):
                act.wait_ge(out_ps, b + 1)
                A(otok[:, b, :], PS[:, b, :], ACT.Copy).then_inc(out_sb, 1)

            def layers(block_no):
                for L in (2 * block_no, 2 * block_no + 1):
                    for j in range(4):
                        step(L, 0, j)
                        if L == 0 and j == 1:
                            scale_w1()
                    with act.Fori(1, BATCH) as b:
                        for j in range(4):
                            step(L, b, j)
                for j in range(4):
                    drain(block_no, j)
                    step(L, BATCH, j, live=False)

            act.wait_ge(eps_set, 1)
            for b in range(BATCH + 1):
                if b < BATCH:
                    norm_square(b, 0)
                if b:
                    block_deviations(0, [b - 1])
            layers(0)

            for r in range(ROUNDS):
                work = slots(r)
                for i in range(3):
                    if LAG <= r < PAIRS + LAG:
                        exp_unit(r - LAG, i)
                    if work[i] is not None:
                        slot(*work[i])
                if r in (4, 10, 18):
                    second_part(r // 8 + 1)
            slot(*TAIL[0])
            for b in range(3):
                norm_square(b, SECOND_NORM)
            slot(*TAIL[2])
            block_deviations(SECOND_NORM, range(3))
            norm_square(3, SECOND_NORM)
            block_deviations(SECOND_NORM, [3])
            layers(1)
            output(3)

        @block.vector
        def _(dve):
            V = nc.vector

            def low_part(t):
                (L, b, j), n = t, num(t)
                dve.wait_ge(hi_done, n + 1)
                V.tensor_tensor(h_in[:, j % 2, 1, :].bitcast(FR), yT[:, b, 128 * j:128 * j + 128],
                                h_in[:, j % 2, 0, :], ALU.subtract).then_inc(h_ready, 1)

            def sum_squares(t):
                n = num(t)
                dve.wait_ge(sq_done, n + 1)
                V.reduce_sum(nrm[:, 0, :], sq.rearrange("p (g d) -> p g d", d=DH), AX).then_inc(ss_done, 1)
                dve.wait_ge(ss_done, n + 1)
                if not isinstance(t[1], int) or n:
                    dve.wait_ge(lnq_done, n)
                V.tensor_scalar(nrm[:, 1, :], nrm[:, 0, :], 1e-24, None, ALU.max).then_inc(ssc_done, 1)

            def copy_v(t):
                (L, b, j), n = t, num(t)
                dve.wait_ge(v_ready, n + 1)
                if not isinstance(b, int) or n >= 2:
                    dve.wait_ge(pv_done, n - 1)
                V.tensor_copy(vm[0:64, j % 2, :], v_s[0:64, j, :])
                V.tensor_copy(vm[64:128, j % 2, :], v_s[64:128, (j + 3) % 4, :]).then_inc(vm_done, 1)

            def normalise(t):
                n, k = num(t), t[2] % 2
                dve.wait_ge(r_done, n + 1)
                if late(t, 1):
                    dve.wait_ge(rots_done, n)
                    dve.wait_ge(rotc_done, n)
                V.tensor_tensor(qn.rearrange("p (g d) -> p g d", d=DH),
                                qk_ps.rearrange("p (g d) -> p g d", d=DH),
                                rn.rearrange("p (g o) -> p g o", o=1).broadcast_to((128, 16, DH)),
                                ALU.mult).then_inc(qn_done, 1)

            def rotate(t):
                (L, b, j), n = t, num(t)
                k = j % 2
                dve.wait_ge(qn_done, n + 1)
                if isinstance(b, int) and n in (0, 16):
                    dve.wait_ge(tables_done, L + 1)
                if late(t, 1):
                    dve.wait_ge(qr_done, n)
                    dve.wait_ge(kr_done, n)
                V.tensor_tensor(rc.rearrange("p (c h d) -> p c h d", c=2, h=HEADS),
                                qn.rearrange("p (c h d) -> p c h d", c=2, h=HEADS),
                                cosT[:, L % 2, j, :, :].rearrange("p c (o d) -> p c o d", o=1)
                                .broadcast_to((128, 2, HEADS, DH)), ALU.mult).then_inc(rotc_done, 1)

            def rotated_rest(t):
                n, k = num(t), t[2] % 2
                dve.wait_ge(rotc_done, n + 1)
                dve.wait_ge(rots_done, n + 1)
                if late(t, 1):
                    dve.wait_ge(qktr_done, n)
                V.tensor_tensor(qr[:, 256:1024], rc[:, 256:1024], rs[:, 256:1024],
                                ALU.add).then_inc(kr_done, 1)

            def q_lower(t):
                n = num(t)
                dve.wait_ge(qktr_done, n + 1)
                if isinstance(t[1], int) and n == 0:
                    dve.wait_ge(zeroed, 1)
                else:
                    dve.wait_ge(sc_done, n)
                V.tensor_copy(qz[0:64, 0::2, :],
                              tr_ps[0:64, 0:512].rearrange("p (h n) -> p h n", h=4)).then_inc(qzlo_done, 1)

            def row_max(t, half):
                n, k, h = num(t), t[2] % 2, slice(4 * half, 4 * half + 4)
                dve.wait_ge(sc_done if half else sclo_done, n + 1)
                if not half and (not isinstance(t[1], int) or n >= 2):
                    dve.wait_ge(exp_done, n - 1)
                V.reduce_max(nmax[:, k, h], PS[:, 3 + half, :].rearrange("p (h n) -> p h n", h=4), AX,
                             negate=True).then_inc(max_done if half else maxlo_done, 1)

            def reciprocal(t):
                n, k = num(t), t[2] % 2
                dve.wait_ge(exp_done, n + 1)
                if not isinstance(t[1], int) or n >= 2:
                    dve.wait_ge(pn_done, n - 1)
                V.reciprocal(rden[:, k, :], den[:, k, :]).then_inc(rden_done, 1)

            def pt_evict(t):
                n = num(t)
                dve.wait_ge(pttr_done, n + 1)
                if not isinstance(t[1], int) or n:
                    dve.wait_ge(pv_done, n)
                V.tensor_copy(pT[:, 4:8, :],
                              tr_ps[:, 512:1024].rearrange("p (h n) -> p h n", h=4)).then_inc(ptd_done, 1)

            def residual(t):
                (L, b, j), n = t, num(t)
                dve.wait_ge(wo_done, n + 1)
                lo, up = slice(128 * j, 128 * j + 128), slice(128 * j + 1, 128 * j + 129)
                V.tensor_tensor(zT[0:64, b, lo], o_ps[0:64, 0:128], yT[0:64, b, lo], ALU.add)
                V.tensor_tensor(zT[64:128, b, up], o_ps[64:128, 0:128], yT[64:128, b, up],
                                ALU.add).then_inc(z_done, 1)

            def mlp_copy(t):
                nq = 4 * t[0] + t[1]
                q = norm_index(t[0], t[1])
                dve.wait_ge(cen_done, q + 1)
                V.tensor_copy(hc[:, :], o_ps).then_inc(hc_done, 1)

            def mlp_norm(t):
                q = norm_index(t[0], t[1])
                dve.wait_ge(rstd_done, q + 1)
                V.tensor_tensor(hn[:, :], hc[:, :], rstd[:, 0, :], ALU.mult).then_inc(hn_done, 1)

            def mlp(t):
                L, b, _ = t
                nq, l = 4 * L + b, L % 2
                for m in range(3):
                    dve.wait_ge(a_done, 3 * nq + m + 1)
                    dve.wait_ge(gl_done, 3 * nq + m + 1)
                    V.scalar_tensor_tensor(u_s[0:HB[m], m, :], PS[0:HB[m], (2, 0, 1)[m], :],
                                           vecs[0:HB[m], b1_column(l, 0, m):b1_column(l, 0, m) + 1], u_s[0:HB[m], m, :],
                                           ALU.add, ALU.mult).then_inc(u_done, 1)
                dve.wait_ge(w2_done, nq + 1)
                V.scalar_tensor_tensor(yT[0:64, b, 0:SEQ], PS[0:64, 5, :], vecs[0:64, V_B2 + l:V_B2 + l + 1],
                                       zT[0:64, b, 0:SEQ], ALU.add, ALU.add)
                V.scalar_tensor_tensor(yT[64:128, b, 1:SEQ + 1], PS[64:128, 5, :], vecs[64:128, V_B2 + l:V_B2 + l + 1],
                                       zT[64:128, b, 1:SEQ + 1], ALU.add, ALU.add).then_inc(y_ready, 1)

            def block_norm(q, b):
                dve.wait_ge(rstd_done, q + 1)
                bank = CENTRE_BANK[b]
                V.tensor_tensor(yT[0:64, b, 0:SEQ], PS[0:64, bank, :], rstd[0:64, b, :], ALU.mult)
                V.tensor_tensor(yT[64:128, b, 1:SEQ + 1], PS[64:128, bank, :], rstd[64:128, b, :],
                                ALU.mult).then_inc(hn_done, 1)
                dve.wait_ge(hn_done, q + 1)
                V.engine_nop().then_inc(y_ready, 1)

            def tables(l):
                for j in range(TILES):
                    cos, sin = (CS[:, o - C_KEPT + 128 * j:o - C_KEPT + 128 * j + 128]
                                .rearrange("p (c d) -> p c d", c=2) for o in (C_COS, C_SIN))
                    V.tensor_tensor(cosT[:, l, j, :, :], cos, qks[:, l, :, :], ALU.mult)
                    for half in range(2):
                        d, e = slice(32 * half, 32 * half + 32), slice(32 - 32 * half, 64 - 32 * half)
                        last = V.tensor_tensor(sinT[:, l, j, :, d], sin[:, :, d], qks[:, l, :, e], ALU.mult)
                last.then_inc(tables_done, 1)

            def split_w(l):
                V.tensor_copy(wqkv_s[:, l, :].bitcast(FR), wq_in[:, l, :]).then_inc(w_hi, 1)
                dve.wait_ge(w_hi, l + 1)
                V.tensor_tensor(wq_low[:, l, :].bitcast(FR), wq_in[:, l, :], wqkv_s[:, l, :],
                                ALU.subtract).then_inc(w_split, 1)

            def masks():
                V.tensor_copy(cb[:, 0, :], ident)
                V.tensor_copy(cb[:, 1:5, :], CS[:, 0:512].rearrange("p (i n) -> p i n", i=4)).then_inc(
                    masks_done, 1)

            def weights():
                dve.wait_ge(w_ps, 1)
                for c in range(2):
                    V.tensor_copy(wqkT[:, c, :].rearrange("p (d h) -> p h d", d=HD),
                                  PS[:, 7, c * 128:(c + 1) * 128].rearrange("p (h d) -> p h d", d=HD))
                V.tensor_copy(wqkT[:, 2, :], PS[:, 7, 256:384])
                V.tensor_copy(wpT[:, :], PS[:, 7, 384:512]).then_inc(w_done, 1)

            def fold():
                dve.wait_ge(bias_ps, 1)
                dve.wait_ge(vecs_done, 1)
                for m in range(3):
                    r, c = slice(0, HB[m]), slice(4 * m, 4 * m + 4)
                    V.tensor_tensor(vecs[r, c], vecs[r, c], PS[r, 3, c], ALU.add)
                V.tensor_tensor(vecs[:, V_O:V_O + 1], vecs[:, V_P:V_P + 1], PS[:, 3, 12:13],
                                ALU.add).then_inc(folded, 1)

            def step(L, b, j, live=True):
                t0, t1, t2, t3, t4 = stages(L, b, j, live)
                mlp_due = t4 is not None and j == 3
                if t0 is not None and j == 0:
                    low_part(t0)
                first_step = live and j == 0 and L % 2 == 0 and isinstance(b, int) and b == 0
                if first_step:
                    block_norm(L // 2 * SECOND_NORM + 1, 1)
                    if L == 0:
                        masks()
                        tables(0)
                    else:
                        block_norm(L // 2 * SECOND_NORM + 2, 2)
                if t2 is not None:
                    row_max(t2, 0)
                    row_max(t2, 1)
                if mlp_due:
                    residual(t4)
                if t1 is not None:
                    rotate(t1)
                if t3 is not None:
                    pt_evict(t3)
                if mlp_due:
                    mlp_copy(t4)
                if t1 is not None:
                    rotated_rest(t1)
                if t4 is not None and not mlp_due:
                    residual(t4)
                if t2 is not None:
                    reciprocal(t2)
                if t0 is not None and not mlp_due:
                    sum_squares(t0)
                if t1 is not None:
                    q_lower(t1)
                if mlp_due:
                    mlp_norm(t4)
                    if t0 is not None:
                        sum_squares(t0)
                if t0 is not None and j < 3:
                    low_part((L, b, j + 1))
                if t2 is not None:
                    copy_v(t2)
                if t0 is not None:
                    normalise(t0)
                if first_step:
                    if L == 0:
                        block_norm(L // 2 * SECOND_NORM + 2, 2)
                    block_norm(L // 2 * SECOND_NORM + 3, 3)
                if mlp_due:
                    mlp(t4)

            def add_half(b, k):
                dve.wait_ge(y_ready, y_after(2 * k + 1, b))
                V.scalar_tensor_tensor(xT[0:64, b, :], yT[0:64, b, 0:SEQ], 0.5, xT[0:64, b, :],
                                       ALU.mult, ALU.add)
                V.scalar_tensor_tensor(xT[64:128, b, :], yT[64:128, b, 1:SEQ + 1], 0.5, xT[64:128, b, :],
                                       ALU.mult, ALU.add).then_inc(x_ready, 1)

            def slot(what, n):
                bank, g = bank_of(what, n), n % 4
                if what == "variance":
                    q = mid_norm(n)
                    dve.wait_ge(rstd_done, q + 1)
                    if n:
                        dve.wait_ge(m_v, n)
                    V.tensor_tensor(hn[:, :], hc[:, :], rstd[:, 0, :], ALU.mult).then_inc(hn_done, 1)
                if what in ("q", "k"):
                    c = 0 if what == "q" else 1
                    dve.wait_ge(m_qk, 2 * n + c + 1)
                    if n:
                        dve.wait_ge(m_p3, n)
                    V.scalar_tensor_tensor(qkf[:, c, :], bank, vecs[:, V_Q + c:V_Q + c + 1],
                                           C[:, C_F + c * SEQ:C_F + (c + 1) * SEQ], ALU.add,
                                           ALU.mult).then_inc(m_f, 1)
                if what == "max":
                    t = bank[0:16, 0:128]
                    dve.wait_ge(m_t, n + 1)
                    if n:
                        dve.wait_ge(m_msav, 16 * n)
                    V.tensor_scalar(mpartb[0:16, 0, :], t, -1.0, None, ALU.mult).then_inc(m_m1, 1)
                    dve.wait_ge(m_m1, n + 1)
                    V.scalar_tensor_tensor(mres[0:16, :], t, -1.0, mpartb[0:16, 0, :], ALU.mult,
                                           ALU.subtract).then_inc(m_m2, 1)
                    dve.wait_ge(m_m2, n + 1)
                    V.tensor_copy(mpartb[0:16, 1, :], mres[0:16, :]).then_inc(m_m3, 1)
                    dve.wait_ge(m_m3, n + 1)
                    V.tensor_tensor(mpartb[0:16, 2, :], mres[0:16, :], mpartb[0:16, 1, :],
                                    ALU.subtract).then_inc(m_m4, 1)
                if what == "o":
                    dve.wait_ge(m_ot, n + 1)
                    o = bank.rearrange("p (q j e) -> p q j e", q=TILES, j=4)
                    r4 = rec.rearrange("p q (j o) -> p q j o", o=1)
                    if n:
                        dve.wait_ge(m_yt, n)
                    V.reciprocal(r4, o[:, :, :, HD:HD + 1]).then_inc(m_rec, 1)
                    dve.wait_ge(m_rec, n + 1)
                    if g == 0 and n:
                        dve.wait_ge(m_ytt, n // 4)
                    V.tensor_tensor(ytok[:, :, 32 * g:32 * g + 32].rearrange("p q (j e) -> p q j e", j=4),
                                    o[:, :, :, 0:HD], r4.broadcast_to((128, TILES, 4, HD)),
                                    ALU.mult).then_inc(m_yt, 1)
                if what == "project":
                    dve.wait_ge(m_pr, n + 1)
                    V.scalar_tensor_tensor(xT[:, n, :], bank, vecs[:, V_O:V_O + 1], xT[:, n, :],
                                           ALU.add, ALU.add).then_inc(x_ready, 1)

            def max_unit(n, i):
                u, g, c = 5 * n + i, n // 2 % 4, 8 * (n % 2)
                bank, m = PS[:, 5 + u % 2, :], mx[:, g, :]
                dve.wait_ge(m_s, u + 1)
                if i == 0 and n >= 8:
                    dve.wait_ge(m_t, n // 2 - 3)
                if i in (0, 2):
                    o = c + 4 * (i // 2) + 3
                    last = V.reduce_max(m[:, o:o + 1], bank, AX)
                elif i in (1, 3):
                    o = c + 4 * (i // 2)
                    V.reduce_max(m[:, o + 2:o + 3], bank[:, 0:384], AX)
                    last = V.reduce_max(m[:, o:o + 1], bank[:, 384:512], AX)
                else:
                    last = V.reduce_max(m[:, c + 1:c + 6:4], bank.rearrange("p (a n) -> p a n", a=2), AX)
                last.then_inc(m_max, 1)

            def drain(block_no, j):
                if j == 0:
                    for b in range(3):
                        add_half(b, block_no)
                if block_no == 0 and j == 3:
                    for what in ("variance", "q", "k"):
                        slot(what, 0)
                    dve.wait_ge(m_v, 1)

            def layers(block_no):
                for L in (2 * block_no, 2 * block_no + 1):
                    for j in range(4):
                        step(L, 0, j)
                        if L == 0 and j == 0:
                            weights()
                        if L == 0 and j == 1:
                            fold()
                    if L == 0:
                        tables(1)
                        dve.wait_ge(rest_loaded, 16 * len(load_rest))
                        split_w(1)
                    with dve.Fori(1, BATCH) as b:
                        for j in range(4):
                            step(L, b, j)
                for j in range(4):
                    drain(block_no, j)
                    step(L, BATCH, j, live=False)

            V.memset(rows[:, :], 0.0).then_inc(rows_zero, 1)
            V.memset(cc[:, 0:1], 1e-5)
            for b in range(BATCH):
                V.memset(yT[64:128, b, 0:1], 0.0)
                last = V.memset(zT[64:128, b, 0:1], 0.0)
            last.then_inc(eps_set, 1)
            for b in range(BATCH):
                dve.wait_ge(xt_ps, b + 1)
                V.tensor_copy(xT[:, b, :], PS[:, VARIANCE_BANK[b], :]).then_inc(x_ready, 1)
            block_norm(0, 0)
            dve.wait_ge(vecs_ps, 1)
            V.tensor_copy(vecs[:, 0:22], PS[:, 2, 0:22]).then_inc(vecs_done, 1)
            dve.wait_ge(first_loaded, 16 * len(load_first))
            split_w(0)
            layers(0)
            add_half(3, 0)

            for r in range(ROUNDS):
                work = slots(r)
                for kind, i in ROUND:
                    if kind == "scores" and r < PAIRS:
                        max_unit(r, i)
                    if kind == "slot" and work[i] is not None:
                        slot(*work[i])

            slot(*TAIL[1])
            slot(*TAIL[3])
            block_norm(SECOND_NORM, 0)
            layers(1)
            add_half(3, 1)

        @block.gpsimd
        def _(pool):
            P = nc.gpsimd

            def high_part(t):
                (L, b, j), n = t, num(t)
                hi, y = h_in[:, j % 2, 0, :], yT[:, b, 128 * j:128 * j + 128]
                pool.wait_ge(y_ready, y_count(L, b))
                if late(t, 2):
                    pool.wait_ge(qkv_done, n - 1)
                P.tensor_copy(hi.bitcast(FR), y).then_inc(hi_done, 1)

            def sine_part(t):
                (L, b, j), n = t, num(t)
                pool.wait_ge(qn_done, n + 1)
                if isinstance(b, int) and n in (0, 16):
                    pool.wait_ge(tables_done, L + 1)
                if late(t, 1):
                    pool.wait_ge(qr_done, n)
                    pool.wait_ge(kr_done, n)
                for c in (1, 0):
                    src = qn[:, 512 * c:512 * c + 512]
                    base = src.offset
                    swapped = bass.AP(src.tensor, base + 32, [list(src.ap[0]), [64, HEADS], [-32, 2], [1, 32]])
                    last = P.tensor_tensor(
                        rs[:, 512 * c:512 * c + 512].rearrange("p (h a d) -> p h a d", h=HEADS, a=2),
                        swapped,
                        sinT[:, L % 2, j, c, :].rearrange("p (o a d) -> p o a d", o=1, a=2)
                        .broadcast_to((128, HEADS, 2, 32)), ALU.mult)
                last.then_inc(rots_done, 1)

            def rotated_q(t):
                n = num(t)
                pool.wait_ge(rotc_done, n + 1)
                pool.wait_ge(rots_done, n + 1)
                if late(t, 1):
                    pool.wait_ge(qktr_done, n)
                P.tensor_tensor(qr[:, 0:256], rc[:, 0:256], rs[:, 0:256],
                                ALU.add).then_inc(qr_done, 1)

            def normalise(t):
                n, k = num(t), t[2] % 2
                pool.wait_ge(rden_done, n + 1)
                P.tensor_tensor(p_s[:, k, :, :], p_s[:, k, :, :],
                                rden[:, k, :].rearrange("p (h o) -> p h o", o=1).broadcast_to((128, HEADS, 128)),
                                ALU.mult).then_inc(pn_done, 1)

            def step(L, b, j, live=True):
                t0, t1, t2, t3, t4 = stages(L, b, j, live)
                if t0 is not None and j == 0:
                    high_part(t0)
                if t1 is not None:
                    sine_part(t1)
                    rotated_q(t1)
                if t2 is not None:
                    normalise(t2)
                if t0 is not None and j < 3:
                    high_part((L, b, j + 1))

            def set_slot(k):
                P.memset(stack(k, 0)[64:96, :], 0.0)
                P.memset(kstb[k][64:96, :, :], 1.0).then_inc(stack_rows, 1)
                pool.wait_ge(stack_rows, k + 1)
                P.memset(v_slot(k)[:, TILES * NH * (HD + 1):], 0.0)
                P.memset(v_heads(k)[:, :, :, HD:HD + 1], 1.0).then_inc(zeroed, 1)

            def zero_layers():
                P.memset(qz, 0.0)
                P.memset(kT, 0.0)
                P.memset(v_s[:, 3, :], 0.0).then_inc(zeroed, 1)

            def drain(block_no, j):
                if block_no == 0 and j == 0:
                    pool.wait_ge(pn_done, 16 * 2 - 2)
                    pool.wait_ge(qkv_done, 16 * 2)
                    set_slot(0)

            def layers(block_no):
                for L in (2 * block_no, 2 * block_no + 1):
                    for j in range(4):
                        step(L, 0, j)
                    with pool.Fori(1, BATCH) as b:
                        for j in range(4):
                            step(L, b, j)
                for j in range(4):
                    drain(block_no, j)
                    step(L, BATCH, j, live=False)

            pool.wait_ge(rows_zero, 1)
            with nc.allow_non_contiguous_dma("256 biases, reordered"):
                for dst, src in load_rows:
                    pool.dma_start(dst, src).then_inc(rows_loaded, 16)
            zero_layers()
            layers(0)

            def parts(b):
                pool.wait_ge(m_p1, b + 1)
                P.tensor_tensor(qkf, qkf, partb[:, 0, :, :], ALU.subtract).then_inc(m_r1, 1)
                pool.wait_ge(m_p2, b + 1)
                P.tensor_tensor(partb[:, 2, :, :], qkf, partb[:, 1, :, :], ALU.subtract).then_inc(m_p3, 1)

            parts(0)
            pool.wait_ge(x_ready, 8)
            pool.wait_ge(m_p3, 1)
            set_slot(1)
            for b in range(1, BATCH):
                parts(b)
            pool.wait_ge(w_again, 16 * LAYERS)
            P.tensor_tensor(wq_low[:, :, :].bitcast(FR), wq_in, wqkv_s[:, :, :], ALU.subtract).then_inc(w_split, 1)
            pool.wait_ge(m_pv, 4 * BATCH)
            zero_layers()
            layers(1)


_INS = ['L0_attn_x', 'L0_attn_W_attn', 'L0_attn_b_attn', 'L0_attn_W_proj', 'L0_attn_b_proj',
        'L0_ffn_wqkv', 'L0_ffn_q_scale', 'L0_ffn_k_scale', 'L0_ffn_wo', 'L0_ffn_ln_g', 'L0_ffn_ln_b',
        'L0_ffn_w1', 'L0_ffn_b1', 'L0_ffn_w2', 'L0_ffn_b2']


def kernel(**inputs):
    import numpy as _np
    import concourse.bacc as _bacc
    from concourse import mybir as _mybir
    from concourse.bass_utils import run_bass_kernel_spmd as _run

    nc = _bacc.Bacc("TRN2", target_bir_lowering=False, num_devices=1)
    arrays, args = {}, []
    for name in _INS:
        a = _np.ascontiguousarray(inputs[name])
        arrays[f"in_{name}_dram"] = a
        args.append(nc.dram_tensor(f"in_{name}_dram", a.shape, _mybir.dt.from_np(a.dtype), kind="ExternalInput").ap())
    c = constants()
    arrays["constants_dram"] = c
    args.append(nc.dram_tensor("constants_dram", c.shape, _mybir.dt.float32, kind="ExternalInput").ap())
    args.append(nc.dram_tensor("out_0_dram", (BATCH, SEQ, DIM), _mybir.dt.float32, kind="ExternalOutput").ap())
    macaron(nc, *args)
    r = _run(nc, [arrays], core_ids=[0])
    return r.results[0]["out_0_dram"]
```
